# Optimizing a Trainium2 kernel written in Bass

```python
import numpy as np
import jax
import jax.numpy as jnp

def _softmax(x, axis=-1):
    return jax.nn.softmax(x, axis=axis)

def _gelu(x):
    return jax.nn.gelu(x, approximate=True)

def _silu(x):
    return jax.nn.silu(x)

def _sigmoid(x):
    return jax.nn.sigmoid(x)

def _layernorm(x, axis=-1, eps=1e-05):
    m = jnp.mean(x, axis=axis, keepdims=True)
    v = jnp.var(x, axis=axis, keepdims=True)
    return (x - m) / jnp.sqrt(v + eps)

def _scatter_add(tgt, idx, src, axis=0):
    return tgt.at[idx].add(src)

def _segment_sum(src, seg, n):
    return jax.ops.segment_sum(src, seg, n)
kernel_name = 'mk_audio_tower_d1_tok_audfeat768_r4_405c2b'

def setup_inputs(seed: int=0):
    np.random.seed(seed)
    _w = jnp.asarray

    def _rec_inputs():
        import jax
        import jax.numpy as jnp
        _rk = jax.random.key(seed)
        x = -0.000222058 + 0.999998 * jax.random.normal(jax.random.fold_in(_rk, 1), (4, 1024, 192), jnp.float32)
        return x
    x = _rec_inputs()

    def _L0_tok_setup():
        import jax, jax.numpy as jnp
        import numpy as np
        B, S, D, K = (8, 1024, 192, 7)
        EPS = 1e-05
        key = jax.random.key(seed)
        k0, k1, k2, k3, k4 = jax.random.split(key, 5)
        return {'x': jax.random.normal(k0, (B, S, D), jnp.float32), 'w_dw': jax.random.normal(k1, (D, 1, K), jnp.float32) * 0.2, 'b_dw': jax.random.normal(k2, (D,), jnp.float32) * 0.02, 'w_pw': jax.random.normal(k3, (D, D, 1), jnp.float32) * 0.03, 'b_pw': jax.random.normal(k4, (D,), jnp.float32) * 0.02, 'gamma': jnp.ones((D,), jnp.float32), 'beta': jnp.zeros((D,), jnp.float32)}
    _L0_tok_all = _L0_tok_setup()
    _L0_tok_in = {k: v for k, v in _L0_tok_all.items() if k in ('w_dw', 'b_dw', 'w_pw', 'b_pw', 'gamma', 'beta')}
    del _L0_tok_all

    def _L0_attn_setup():
        import math
        import jax, jax.numpy as jnp
        import numpy as np
        D_MODEL = 192
        NUM_HEADS = 12
        NUM_KV_HEADS = 12
        FEATURE_DIM = 16
        HEAD_DIM = D_MODEL // NUM_KV_HEADS
        EPS = 1e-12
        R2 = math.sqrt(2.0)
        RD = math.sqrt(FEATURE_DIM)
        RRD = math.sqrt(RD)

        def taylor_exp(x):
            b, h, l, f = x.shape
            x2 = (x[..., :, None] * x[..., None, :]).reshape(b, h, l, f * f) / R2
            ones = jnp.ones((b, h, l, 1), dtype=x.dtype)
            return jnp.concatenate([ones, x / RRD, x2 / RD], axis=-1)
        key = jax.random.key(seed)
        k0, k1, k2, k3, k4 = jax.random.split(key, 5)
        B, L = (1, 128)
        hidden_states = jax.random.normal(k0, (B, L, D_MODEL), dtype=jnp.float32)
        s = 0.02
        Wq = jax.random.normal(k1, (FEATURE_DIM * NUM_HEADS, D_MODEL), dtype=jnp.float32) * s
        Wk = jax.random.normal(k2, (FEATURE_DIM * NUM_KV_HEADS, D_MODEL), dtype=jnp.float32) * s
        Wv = jax.random.normal(k3, (NUM_KV_HEADS * HEAD_DIM, D_MODEL), dtype=jnp.float32) * s
        Wo = jax.random.normal(k4, (D_MODEL, NUM_HEADS * HEAD_DIM), dtype=jnp.float32) * s
        return {'hidden_states': hidden_states, 'Wq': Wq, 'Wk': Wk, 'Wv': Wv, 'Wo': Wo}
    _L0_attn_all = _L0_attn_setup()
    _L0_attn_in = {k: v for k, v in _L0_attn_all.items() if k in ('Wq', 'Wk', 'Wv', 'Wo')}
    del _L0_attn_all

    def _L0_ffn_setup():
        import jax, jax.numpy as jnp
        import numpy as np
        B, N, D, E = (2, 512, 192, 8)
        H = 4 * D
        TARGET_SPARSITY = 0.6
        K_KEEP = int(N * (1.0 - TARGET_SPARSITY))
        V_MAX, FEAT_CLAMP, ETA = (3.0, 10.0, 1.0)

        def _bk_gii(v):
            dr, di = (v, jnp.full_like(v, -ETA))

            def cf(reverse):
                init = (jnp.full((v.shape[0],), 1e+18, v.dtype), jnp.zeros((v.shape[0],), v.dtype))

                def step(c, d):
                    ar, ai = c
                    drr, dii = d
                    den = ar * ar + ai * ai
                    out = (drr - ar / den, dii + ai / den)
                    return (out, out)
                _, (r, i) = jax.lax.scan(step, init, (dr.T, di.T), reverse=reverse)
                return (r.T, i.T)
            ar, ai = cf(False)
            br, bi = cf(True)
            cr, ci = (ar + br - dr, ai + bi - di)
            den = cr * cr + ci * ci
            return (cr / den, -ci / den)
        key = jax.random.key(seed)
        ks = jax.random.split(key, 8)
        s = 0.02
        return {'x': jax.random.normal(ks[0], (B, N, D), jnp.float32), 'Wg': jax.random.normal(ks[1], (D, E), jnp.float32) * s, 'bg': jnp.zeros((E,), jnp.float32), 'W1': jax.random.normal(ks[2], (E, D, H), jnp.float32) * s, 'b1': jnp.zeros((E, H), jnp.float32), 'W2': jax.random.normal(ks[3], (E, H, D), jnp.float32) * s, 'b2': jnp.zeros((E, D), jnp.float32), 'Wv': jax.random.normal(ks[4], (D,), jnp.float32) * s, 'bv': jnp.zeros((), jnp.float32), 'Wm': jax.random.normal(ks[5], (D,), jnp.float32) * s, 'bm': jnp.zeros((), jnp.float32), 'Wo': jax.random.normal(ks[6], (2, D), jnp.float32) * s, 'bo': jnp.zeros((D,), jnp.float32), 'bk_scale': jnp.ones((), jnp.float32)}
    _L0_ffn_all = _L0_ffn_setup()
    _L0_ffn_in = {k: v for k, v in _L0_ffn_all.items() if k in ('Wg', 'bg', 'W1', 'b1', 'W2', 'b2', 'Wv', 'bv', 'Wm', 'bm', 'Wo', 'bo', 'bk_scale')}
    del _L0_ffn_all
    return {'x': x, 'L0_tok_w_dw': _L0_tok_in['w_dw'], 'L0_tok_b_dw': _L0_tok_in['b_dw'], 'L0_tok_w_pw': _L0_tok_in['w_pw'], 'L0_tok_b_pw': _L0_tok_in['b_pw'], 'L0_tok_gamma': _L0_tok_in['gamma'], 'L0_tok_beta': _L0_tok_in['beta'], 'L0_attn_Wq': _L0_attn_in['Wq'], 'L0_attn_Wk': _L0_attn_in['Wk'], 'L0_attn_Wv': _L0_attn_in['Wv'], 'L0_attn_Wo': _L0_attn_in['Wo'], 'L0_ffn_Wg': _L0_ffn_in['Wg'], 'L0_ffn_bg': _L0_ffn_in['bg'], 'L0_ffn_W1': _L0_ffn_in['W1'], 'L0_ffn_b1': _L0_ffn_in['b1'], 'L0_ffn_W2': _L0_ffn_in['W2'], 'L0_ffn_b2': _L0_ffn_in['b2'], 'L0_ffn_Wv': _L0_ffn_in['Wv'], 'L0_ffn_bv': _L0_ffn_in['bv'], 'L0_ffn_Wm': _L0_ffn_in['Wm'], 'L0_ffn_bm': _L0_ffn_in['bm'], 'L0_ffn_Wo': _L0_ffn_in['Wo'], 'L0_ffn_bo': _L0_ffn_in['bo'], 'L0_ffn_bk_scale': _L0_ffn_in['bk_scale']}

def reference(x, L0_tok_w_dw, L0_tok_b_dw, L0_tok_w_pw, L0_tok_b_pw, L0_tok_gamma, L0_tok_beta, L0_attn_Wq, L0_attn_Wk, L0_attn_Wv, L0_attn_Wo, L0_ffn_Wg, L0_ffn_bg, L0_ffn_W1, L0_ffn_b1, L0_ffn_W2, L0_ffn_b2, L0_ffn_Wv, L0_ffn_bv, L0_ffn_Wm, L0_ffn_bm, L0_ffn_Wo, L0_ffn_bo, L0_ffn_bk_scale):
    import jax
    import jax.numpy as jnp

    def _L0_tok_ref(x, w_dw, b_dw, w_pw, b_pw, gamma, beta):
        import jax, jax.numpy as jnp
        import numpy as np
        B, S, D, K = (8, 1024, 192, 7)
        EPS = 1e-05
        d = w_dw.shape[0]
        h = jnp.transpose(x, (0, 2, 1))
        h = jax.lax.conv_general_dilated(h, w_dw, window_strides=(1,), padding='SAME', dimension_numbers=('NCH', 'OIH', 'NCH'), feature_group_count=d) + b_dw[None, :, None]
        h = jnp.einsum('od,bds->bos', w_pw[:, :, 0], h) + b_pw[None, :, None]
        h = jax.nn.relu(h)
        h = jax.lax.reduce_window(h, -jnp.inf, jax.lax.max, (1, 1, 2), (1, 1, 2), 'VALID')
        h = jnp.transpose(h, (0, 2, 1))
        y = jnp.real(jnp.fft.fft2(h))
        mu = jnp.mean(y, axis=-1, keepdims=True)
        var = jnp.var(y, axis=-1, keepdims=True)
        return (y - mu) * jax.lax.rsqrt(var + EPS) * gamma + beta

    def _L0_attn_ref(hidden_states, Wq, Wk, Wv, Wo):
        import math
        import jax, jax.numpy as jnp
        import numpy as np
        D_MODEL = 192
        NUM_HEADS = 12
        NUM_KV_HEADS = 12
        FEATURE_DIM = 16
        HEAD_DIM = D_MODEL // NUM_KV_HEADS
        EPS = 1e-12
        R2 = math.sqrt(2.0)
        RD = math.sqrt(FEATURE_DIM)
        RRD = math.sqrt(RD)

        def taylor_exp(x):
            b, h, l, f = x.shape
            x2 = (x[..., :, None] * x[..., None, :]).reshape(b, h, l, f * f) / R2
            ones = jnp.ones((b, h, l, 1), dtype=x.dtype)
            return jnp.concatenate([ones, x / RRD, x2 / RD], axis=-1)
        b, l, _ = hidden_states.shape
        q = (hidden_states @ Wq.T).reshape(b, l, NUM_HEADS, FEATURE_DIM).transpose(0, 2, 1, 3)
        k = (hidden_states @ Wk.T).reshape(b, l, NUM_KV_HEADS, FEATURE_DIM).transpose(0, 2, 1, 3)
        v = (hidden_states @ Wv.T).reshape(b, l, NUM_KV_HEADS, HEAD_DIM).transpose(0, 2, 1, 3)
        q = taylor_exp(q)
        k = taylor_exp(k)
        kv = k[..., None, :] * v[..., :, None]
        kv = jnp.cumsum(kv, axis=2)
        num = jnp.einsum('bhlD,bhldD->bhld', q, kv)
        den = jnp.einsum('bhlD,bhlD->bhl', q, jnp.cumsum(k, axis=2)) + EPS
        y = num / den[..., None]
        y = y.transpose(0, 2, 1, 3).reshape(b, l, NUM_HEADS * HEAD_DIM)
        return y @ Wo.T

    def _L0_ffn_ref(x, Wg, bg, W1, b1, W2, b2, Wv, bv, Wm, bm, Wo, bo, bk_scale):
        import jax, jax.numpy as jnp
        import numpy as np
        B, N, D, E = (2, 512, 192, 8)
        H = 4 * D
        TARGET_SPARSITY = 0.6
        K_KEEP = int(N * (1.0 - TARGET_SPARSITY))
        V_MAX, FEAT_CLAMP, ETA = (3.0, 10.0, 1.0)

        def _bk_gii(v):
            dr, di = (v, jnp.full_like(v, -ETA))

            def cf(reverse):
                init = (jnp.full((v.shape[0],), 1e+18, v.dtype), jnp.zeros((v.shape[0],), v.dtype))

                def step(c, d):
                    ar, ai = c
                    drr, dii = d
                    den = ar * ar + ai * ai
                    out = (drr - ar / den, dii + ai / den)
                    return (out, out)
                _, (r, i) = jax.lax.scan(step, init, (dr.T, di.T), reverse=reverse)
                return (r.T, i.T)
            ar, ai = cf(False)
            br, bi = cf(True)
            cr, ci = (ar + br - dr, ai + bi - di)
            den = cr * cr + ci * ci
            return (cr / den, -ci / den)
        probs = jax.nn.softmax(x @ Wg + bg, axis=-1)
        top_p = jnp.max(probs, axis=-1)
        comb = jax.nn.one_hot(jnp.argmax(probs, -1), E, dtype=x.dtype) * top_p[..., None]
        h = jax.nn.gelu(jnp.einsum('bnd,edh->ebnh', x, W1) + b1[:, None, None, :])
        y = jnp.einsum('ebnh,ehd->ebnd', h, W2) + b2[:, None, None, :]
        ffn_out = jnp.einsum('ebnd,bne->bnd', y, comb)
        v = jnp.clip(ffn_out @ Wv + bv, -V_MAX, V_MAX)
        scores = jax.nn.sigmoid(x @ Wm + bm)
        thr = jax.lax.top_k(scores, K_KEEP)[0][:, -1]
        mask = (scores >= thr[:, None]).astype(x.dtype)
        gr, gi = _bk_gii(v)
        feats = jnp.clip(jnp.stack([gr, gi], -1) * mask[..., None], -FEAT_CLAMP, FEAT_CLAMP)
        return ffn_out + bk_scale * (feats @ Wo + bo)
    h = _L0_tok_ref(x, L0_tok_w_dw, L0_tok_b_dw, L0_tok_w_pw, L0_tok_b_pw, L0_tok_gamma, L0_tok_beta)
    h = h + _L0_attn_ref(_layernorm(h, axis=-1), L0_attn_Wq, L0_attn_Wk, L0_attn_Wv, L0_attn_Wo)
    h = h + _L0_ffn_ref(_layernorm(h, axis=-1), L0_ffn_Wg, L0_ffn_bg, L0_ffn_W1, L0_ffn_b1, L0_ffn_W2, L0_ffn_b2, L0_ffn_Wv, L0_ffn_bv, L0_ffn_Wm, L0_ffn_bm, L0_ffn_Wo, L0_ffn_bo, L0_ffn_bk_scale)
    return h

_drawn_inputs = setup_inputs


def setup_inputs(seed=0):
    import zlib

    import numpy as np

    out = dict(_drawn_inputs(seed))
    spreads = {'L0_tok_gamma': (1.0, 0.2),
     'L0_tok_beta': (0.0, 0.1),
     'L0_ffn_bg': (0.0, 0.601),
     'L0_ffn_b1': (0.0, 0.8),
     'L0_ffn_b2': (0.0, 0.445),
     'L0_ffn_bo': (0.0, 0.1)}
    factors = {'L0_attn_Wq': 8.0,
     'L0_attn_Wk': 8.0,
     'L0_attn_Wv': 5.44,
     'L0_attn_Wo': 5.75,
     'L0_ffn_W1': 3.888,
     'L0_ffn_W2': 3.597,
     'L0_ffn_Wv': 28.667,
     'L0_ffn_Wm': 8.0,
     'L0_ffn_Wo': 8.0}
    for name, (base, spread) in spreads.items():
        noise = np.random.default_rng([zlib.crc32(name.encode()), seed]).standard_normal(out[name].shape)
        drawn = base * np.exp(spread * noise) if base else spread * noise
        out[name] = jnp.asarray(drawn.astype(out[name].dtype))
    for name, factor in factors.items():
        out[name] = (out[name] * factor).astype(out[name].dtype)
    return out
```

```python
from contextlib import ExitStack

import concourse.bass as bass
from concourse import mybir

P = 128
F32 = mybir.dt.float32
I32 = mybir.dt.int32
ALU = mybir.AluOpType
ACT = mybir.ActivationFunctionType
AX = mybir.AxisListType.X

B, S, D = 4, 1024, 192
DC = D // 2
TAPS = 7
HALO = TAPS // 2
N = S // 2
NT = N // P
TT = B * NT
NC = D // 2 + 1
NS = D // 2 - 1
HEADS, HD = 12, 16
QUAD = 32
HG = HEADS // 4
PAIRS = HEADS // 2
E, HID = 8, 768
HC = HID // P
SLOT_TILES = TT + E - 1
KEEP = int(N * (1.0 - 0.6))
LCH = 32
CH = N // LCH
EPS_LN = 1e-5
EPS_ATTN = 2e-12
V_MAX, CLAMP = 3.0, 10.0
MAGIC = float(0x5F3759DF)
RSQRT_ROUNDS = 4


class Steps:

    def __init__(self, eng, sem):
        self.eng, self.sem, self.count = eng, sem, 0

    def mark(self, ins):
        ins.then_inc(self.sem, 1)
        self.count += 1
        return ins

    def settle(self):
        self.eng.wait_ge(self.sem, self.count)

    def then(self, ins):
        self.mark(ins)
        self.settle()


def ahead(eng, sem, value):
    if not (isinstance(value, int) and value <= 0):
        eng.wait_ge(sem, value)


def build(nc, t):
    with ExitStack() as ctx:
        def sb(name, shape, dt=F32):
            return ctx.enter_context(nc.sbuf_tensor(name, shape, dt))

        def sem(name):
            return ctx.enter_context(nc.semaphore(name))

        ring = [ctx.enter_context(nc.psum_tensor(f"ring{i}", [P, 2, 512], F32)) for i in range(2)]
        att = [ctx.enter_context(nc.psum_tensor(f"att{i}", [P, 512], F32)) for i in range(HG)]
        misc = ctx.enter_context(nc.psum_tensor("misc", [P, 512], F32))
        ring4 = [r[:, :, :].rearrange("p a (b n) -> p (a b) n", b=2) for r in ring]

        wdw = sb("wdw", [DC, 2, TAPS])
        vec2 = sb("vec2", [DC, 2, 2])
        wpw = sb("wpw", [DC, 2, D])
        dft_c = sb("dft_c", [DC, 2, D])
        gamma = sb("gamma", [P, D])
        beta = sb("beta", [P, D])
        wq = sb("wq", [DC, 2, D])
        wk = sb("wk", [DC, 2, D])
        wv = sb("wv", [DC, 2, D])
        wo = sb("wo", [P, HG, D])
        ident = sb("ident", [P, P])
        tri = sb("tri", [P, P])
        tri_strict = sb("tri_strict", [P, P])
        spread = sb("spread", [P, P])
        steps = sb("steps", [P, NT - 1, NT])
        ones = sb("ones", [P, P])
        epscol = sb("epscol", [P, 1])
        rev = sb("rev", [P, E])
        thr = sb("thr", [P, TT])
        tidx = sb("tidx", [1, SLOT_TILES])
        wgm = sb("wgm", [DC + 1, 2, E + 1])
        w1a = sb("w1a", [DC, E * HID])
        w2 = sb("w2", [P, E * HC * D])
        cos_n = w2[:, 0:NT * N].rearrange("p (i n) -> p i n", n=N)
        sin_n = w2[:, NT * N:2 * NT * N].rearrange("p (i n) -> p i n", n=N)
        at = 2 * NT * N
        xin = w2[0:DC, at:at + 2 * (S + 2 * HALO)].rearrange("p (c n) -> p c n", c=2)
        at += 2 * (S + 2 * HALO)
        assert at <= E * HC * D
        w1b = sb("w1b", [DC + 1, E * HID])
        qm = w1b[0:DC, :].rearrange("p (h n) -> p h n", n=N)
        wvrow = sb("wvrow", [P, D])
        bvcol = sb("bvcol", [P, 1])
        wof = sb("wof", [3, D])
        scale3 = sb("scale3", [3, 1])

        wide = sb("wide", [P, 2 * S])
        conv = wide[0:DC, :].rearrange("p (c n) -> p c n", c=2)
        pooled = sb("pooled", [DC, 2, N])
        gh = sb("gh", [P, NT, D])
        y = sb("y", [P, NT, D])
        xn = sb("xn", [P, NT, D])
        xnT = sb("xnT", [DC + 1, 2, N])
        x2T = sb("x2T", [DC + 1, 2, N])
        qT = sb("qT", [DC, 2, N])
        kT = sb("kT", [DC, 2, N])
        va = sb("va", [P, NT, HEADS, QUAD])
        probs = sb("probs", [P, 4 * 2 * N])
        prob = probs[:].rearrange("p (a h n) -> p a h n", a=4, h=2)
        pbias = sb("pbias", [P, HG * NT])
        oT = sb("oT", [P, HG, N])
        rden = sb("rden", [P, N])
        h_all = sb("h_all", [P, TT, D])
        x2_all = sb("x2_all", [P, TT, D])
        stats = sb("stats", [P, NT, 6])
        mv = sb("mv", [P, NT, 2])
        nx = sb("nx", [P, NT])
        ny = sb("ny", [P, NT])
        nz = sb("nz", [P, NT])

        lg = sb("lg", [P, TT, E + 1])
        score = sb("score", [P, TT])
        mx = sb("mx", [P, TT])
        ex = sb("ex", [P, TT, E])
        top_p = sb("top_p", [P, TT])
        oh = sb("oh", [P, TT, E])
        key = sb("key", [P, TT, E])
        cnt = sb("cnt", [P, E, TT])
        incl = sb("incl", [P, E, TT])
        excl = sb("excl", [P, E, TT])
        et = sb("et", [P, 6, E])
        pos = sb("pos", [P, TT])
        pos_i = sb("pos_i", [P, TT], I32)
        te = sb("te", [1, SLOT_TILES])
        te_i = sb("te_i", [1, SLOT_TILES], I32)
        vm = sb("vm", [P, 2 * TT])
        score_t = sb("score_t", [TT, P])
        zero = sb("zero", [P, D])
        xs = [probs[:, D * i:D * i + D] for i in range(2)]
        ys = [probs[:, D * (2 + i):D * (3 + i)] for i in range(2)]
        hg = [probs[:, 4 * D + HID * i:4 * D + HID * (i + 1)] for i in range(2)]
        hT = [probs[:, 4 * D + HID * (2 + i):4 * D + HID * (3 + i)].rearrange("p (c n) -> p c n", n=P)
              for i in range(2)]
        b2 = oT[0:1, :, :].rearrange("p g n -> p (g n)")
        junk = y[:].rearrange("p a b -> p (a b)")[:, 0:N]
        xsT = [sb(f"xsT{i}", [DC + 1, 2, P]) for i in range(2)]
        v2 = sb("v2", [P, LCH])
        nv2 = sb("nv2", [P, LCH])
        svd = sb("svd", [P, LCH, 2])
        sgn = sb("sgn", [P, LCH])
        qq = sb("qq", [P, LCH + 2, 2, 2])
        lanes = sb("lanes", [P, LCH + 1, 2])
        bnd = sb("bnd", [2 * B, CH, 2, 2, 2])
        bux = sb("bux", [2 * B, CH, 2, 2])
        ain = sb("ain", [2 * B, CH, 2])
        bt = sb("bt", [2 * B, 2, 2])
        br = sb("br", [2 * B, 2, 2])
        bs = sb("bs", [2 * B, 8])
        den = sb("den", [P, 2])
        sq2 = sb("sq2", [P, 2])
        back = sb("back", [B * CH, LCH, 2])
        cc = sb("cc", [B * CH, 2, LCH])
        gg = sb("gg", [B * CH, 3, LCH])
        mask_l = sb("mask_l", [B * CH, LCH])
        vmT = sb("vmT", [2 * TT, P])
        f3 = wide[0:3, 0:B * N]
        def dram(name, shape):
            return nc.dram_tensor(name, shape, F32, kind="Internal").ap()

        xs_dram = dram("tokens_by_expert", (SLOT_TILES * P, D))
        ys_dram = dram("outputs_by_expert", (SLOT_TILES * P, D))
        sc_dram = dram("scores_linear", (B * N,))
        v_dram = dram("v_linear", (B, CH, LCH))
        e_dram = dram("lane_ends", (P, 8))
        a_dram = dram("lane_starts", (P, 2))
        b_dram = dram("backward_fraction", (B, CH, 2 * LCH))

        s_x = sem("x_loaded")
        s_wf = sem("front_weights_loaded")
        s_wa = sem("attention_weights_loaded")
        s_wo = sem("output_projection_loaded")
        s_wm = sem("moe_weights_loaded")
        s_out = sem("output_stored")
        zeroed = sem("buffers_zeroed")
        conv_done = sem("conv_done")
        pw_done = sem("pointwise_done")
        pool_done = sem("pooled_done")
        col_done = sem("channel_dft_done")
        gh_copied = sem("gh_copied")
        row_done = sem("token_dft_done")
        a_copied = sem("cosine_part_copied")
        y_done = sem("y_done")
        xn_ready = sem("xn_ready")
        xt_done = sem("xn_transposed")
        xt_copied = sem("xnT_copied")
        q_done, k_done, v_done = sem("q_done"), sem("k_done"), sem("v_done")
        q_copied, k_copied, v_copied = sem("q_copied"), sem("k_copied"), sem("v_copied")
        qm_ready = sem("q_spread")
        pre_done = sem("prefix_done")
        pre_copied = sem("prefix_copied")
        s_done = sem("scores_done")
        sq_done = sem("squared")
        p_ready = sem("weights_ready")
        av_done = sem("weights_used")
        ot_done = sem("attention_sums_done")
        ot_copied = sem("attention_sums_copied")
        den_done = sem("denominators_spread")
        o_ready = sem("attention_normalised")
        wo_done = sem("attention_projected")
        attn_added = sem("attention_added")
        x2_ready = sem("x2_ready")
        dve_step, act_step, pool_step = sem("dve_step"), sem("act_step"), sem("pool_step")
        ones_rows = sem("bias_rows_ready")
        t2_done, t2_copied = sem("x2_transposed"), sem("x2T_copied")
        lg_done, lg_copied = sem("logits_done"), sem("logits_copied")
        nd_ready, ex_ready, sc_ready = sem("logits_shifted"), sem("exp_ready"), sem("score_ready")
        oh_ready, cnt_done = sem("one_hot_ready"), sem("counts_done")
        pos_ready, te_ready = sem("positions_ready"), sem("tile_experts_ready")
        zero_ready, s_fill, s_scatter = sem("zero_ready"), sem("slots_filled"), sem("tokens_scattered")
        st_done, st_copied = sem("scores_transposed"), sem("score_t_copied")
        s_sc_out, s_sc_in = sem("scores_stored"), sem("scores_spread")
        s_w1a, s_w1b, s_w2 = sem("w1a_loaded"), sem("w1b_loaded"), sem("w2_loaded")
        s_xs = [sem(f"slots_loaded{i}") for i in range(2)]
        xst_done, xst_copied = sem("slots_transposed"), sem("slots_t_copied")
        up_done, gelu_done = sem("up_done"), sem("gelu_done")
        ht_done, ht_copied = sem("hidden_transposed"), sem("hidden_t_copied")
        dn_done, ys_copied = sem("down_done"), sem("expert_out_copied")
        s_ys = [sem(f"expert_out_stored{i}") for i in range(2)]
        s_gath = [sem(f"gathered{b}") for b in range(B)]
        vm_ready, vmt_done, vmt_copied = sem("v_mask_ready"), sem("v_mask_transposed"), sem("vmT_copied")
        s_v_out, s_lane = sem("v_stored"), sem("lanes_loaded")
        ends_ready, s_e_out, s_bnd = sem("lane_ends_ready"), sem("lane_ends_stored"), sem("lane_ends_gathered")
        ain_ready, s_a_out, s_a_in = sem("starts_ready"), sem("starts_stored"), sem("starts_loaded")
        frac_ready, s_b_out, s_back = sem("fraction_ready"), sem("backward_stored"), sem("backward_loaded")
        feat_ready, s_f3, f3_ones = sem("features_ready"), sem("features_spread"), sem("f3_ones")
        ft_done, out_ready = sem("feature_rows_done"), sem("output_ready")

        block = ctx.enter_context(nc.Block())
        FRONT = [(wdw, "w_dw"), (vec2, "vec2"), (wpw, "w_pw"), (dft_c, "dft_c"), (cos_n, "cos_n"),
                 (sin_n, "sin_n")]
        ATTN = [(gamma, "gamma"), (beta, "beta"), (ident, "ident"), (wq, "wq"), (wk, "wk"), (wv, "wv"),
                (tri, "tri"), (spread, "spread"), (steps, "steps"), (ones, "ones"), (epscol, "epscol")]
        MOE = [(tri_strict, "tri_strict"), (rev, "rev"), (thr, "thr"), (tidx, "tidx"), (wgm, "wgm"),
               (wvrow, "wvrow"), (bvcol, "bvcol"), (wof, "wof"), (scale3, "scale3"), (sgn, "sgn")]
        TILE_PAIRS = (SLOT_TILES - 1) // 2
        assert SLOT_TILES % 2 == 1

        def order(front, attend):
            front(0)
            for b in range(B - 1):
                front(b + 1)
                attend(b)
            attend(B - 1)

        @block.sync
        def _(sp):
            def load(dst, name, s):
                sp.dma_start(dst if isinstance(dst, bass.AP) else dst[:], t[name]).then_inc(s, 16)

            def load_x(b):
                if b > 0:
                    sp.wait_ge(conv_done, b)
                sp.dma_start(xin[:, :, HALO:HALO + S], t["x"][b]).then_inc(s_x, 16)

            load_x(0)
            for dst, name in FRONT:
                load(dst, name, s_wf)
            load_x(1)
            for dst, name in ATTN:
                load(dst, name, s_wa)
            sp.wait_ge(zeroed, 3)
            for q in range(4):
                sp.dma_start(wo[QUAD * q:QUAD * q + HD, :, :], t["wo"][q]).then_inc(s_wo, 16)

            def front(b):
                pass

            def attend(b):
                if b + 2 < B:
                    load_x(b + 2)
                sp.wait_ge(q_copied, b + 1)
                if b > 0:
                    sp.wait_ge(s_done, 24 * b)
                for h in range(HEADS):
                    r = HD * (h % 6)
                    sp.dma_start(qm[r:r + HD, h, :], qT[r:r + HD, h // 6, :]).then_inc(qm_ready, 16)

            sp.wait_ge(zero_ready, 1)
            for i in range(SLOT_TILES):
                sp.dma_start(xs_dram[P * i:P * i + P, :], zero[:]).then_inc(s_fill, 16)
            for dst, name in MOE:
                load(dst, name, s_wm)
            sp.dma_start(w1a[:], t["w1a"]).then_inc(s_w1a, 16)
            order(front, attend)
            sp.wait_ge(row_done, B)
            sp.wait_ge(conv_done, B)
            sp.dma_start(w2[:], t["w2"]).then_inc(s_w2, 16)
            sp.wait_ge(s_done, 24 * B)
            sp.dma_start(w1b[:], t["w1b"]).then_inc(s_w1b, 16)
            sp.wait_ge(wo_done, B)
            sp.dma_start(b2, t["b2"]).then_inc(s_w2, 16)
            sp.wait_ge(st_copied, 1)
            sp.dma_start(sc_dram.rearrange("(t n) -> t n", n=P), score_t[:]).then_inc(s_sc_out, 16)
            sp.wait_ge(s_sc_out, 16)
            sp.wait_ge(conv_done, B)
            sp.wait_ge(pw_done, 2 * B)
            sp.dma_start(wide[:], sc_dram[None, :].to_broadcast([P, B * N])).then_inc(s_sc_in, 16)
            sp.wait_ge(s_scatter, 16 * TT)

            def load_slots(i, slot):
                sp.dma_start(xs[slot], xs_dram[bass.ds(i * P, P), :]).then_inc(s_xs[slot], 16)

            def load_pair(i):
                ahead(sp, xst_done, 2 * i)
                load_slots(2 * i + 1, 1)
                sp.wait_ge(xst_done, 2 * i + 1)
                load_slots(2 * i + 2, 0)

            load_slots(0, 0)
            load_pair(0)
            with sp.Fori(1, TILE_PAIRS) as i:
                load_pair(i)

            sp.wait_ge(vmt_copied, 1)
            sp.dma_start(v_dram.rearrange("b c l -> (b c l)").rearrange("(t n) -> t n", n=P),
                         vmT[0:TT, :]).then_inc(s_v_out, 16)
            sp.dma_start(mask_l[:], vmT[TT:2 * TT, :]).then_inc(s_lane, 16)
            sp.wait_ge(s_v_out, 16)
            sp.dma_start(v2[0:B * CH, :], v_dram.rearrange("b c l -> (b c) l")).then_inc(s_lane, 16)
            sp.dma_start(nv2[B * CH:P, :], v_dram[:, ::-1, :]).then_inc(s_lane, 16)
            sp.wait_ge(ends_ready, 1)
            sp.dma_start(e_dram, qq[:, LCH:LCH + 2, :, :].rearrange("p k c s -> p (k c s)")).then_inc(s_e_out, 16)
            sp.wait_ge(s_e_out, 16)
            sp.dma_start(bnd[:], e_dram.rearrange("(s c) k -> s (c k)", c=CH)).then_inc(s_bnd, 16)
            sp.wait_ge(ain_ready, 1)
            sp.dma_start(a_dram.rearrange("(s c) k -> s (c k)", c=CH), ain[:]).then_inc(s_a_out, 16)
            sp.wait_ge(s_a_out, 16)
            sp.dma_start(lanes[:, 0, :], a_dram).then_inc(s_a_in, 16)
            sp.wait_ge(frac_ready, 1)
            sp.dma_start(b_dram.rearrange("b c l -> (b c) l"),
                         lanes[B * CH:P, 1:LCH + 1, :].rearrange("p l k -> p (l k)")).then_inc(s_b_out, 16)
            sp.wait_ge(s_b_out, 16)
            sp.dma_start(back[:].rearrange("p l k -> p (l k)"), b_dram[:, ::-1, :]).then_inc(s_back, 16)
            sp.wait_ge(feat_ready, 1)
            sp.wait_ge(f3_ones, 1)
            for k in range(2):
                sp.dma_start(f3[k:k + 1, :], gg[:, k, :]).then_inc(s_f3, 16)
            for b in range(B):
                sp.wait_ge(out_ready, b + 1)
                sp.dma_start(t["out"][N * b:N * b + N, :].rearrange("(n p) d -> p n d", p=P),
                             h_all[:, NT * b:NT * b + NT, :]).then_inc(s_out, 16)
            sp.wait_ge(s_out, 16 * B)

        @block.gpsimd
        def _(pool):
            nc.gpsimd.memset(xin[:, :, 0:HALO], 0.0).then_inc(pool_step, 1)
            nc.gpsimd.memset(xin[:, :, HALO + S:], 0.0).then_inc(zeroed, 1)
            nc.gpsimd.memset(wo[:], 0.0).then_inc(pool_step, 1)
            nc.gpsimd.memset(qm, 0.0).then_inc(zeroed, 1)
            nc.gpsimd.memset(va[:], 0.0).then_inc(pool_step, 1)
            pool.wait_ge(pool_step, 3)
            nc.gpsimd.memset(va[:, :, :, HD:HD + 1], 1.0).then_inc(zeroed, 1)
            nc.gpsimd.memset(zero[:], 0.0).then_inc(zero_ready, 1)

            def front(b):
                pass

            def attend(b):
                if b == 0:
                    pool.wait_ge(s_wa, 16 * len(ATTN))
                for n in range(24):
                    pool.wait_ge(sq_done, 24 * b + n + 1)
                    diag = prob[:, n % 4, :, 0:P]
                    nc.gpsimd.tensor_tensor(diag, diag, tri[:, None, :].to_broadcast([P, 2, P]),
                                            ALU.mult).then_inc(p_ready, 1)

            order(front, attend)
            pool.wait_ge(s_fill, 16 * SLOT_TILES)
            pool.wait_ge(x2_ready, B)
            pool.wait_ge(pos_ready, 1)
            for i in range(TT):
                nc.gpsimd.indirect_dma_start(xs_dram, bass.IndirectOffsetOnAxis(pos_i[:, i:i + 1], 0),
                                             x2_all[:, i, :], None).then_inc(s_scatter, 16)

            def store_slots(i, slot):
                pool.wait_ge(ys_copied, i + 1)
                pool.dma_start(ys_dram[bass.ds(i * P, P), :], ys[slot]).then_inc(s_ys[slot], 16)

            with pool.Fori(0, TILE_PAIRS) as i:
                store_slots(2 * i, 0)
                store_slots(2 * i + 1, 1)
            store_slots(SLOT_TILES - 1, 0)
            pool.wait_ge(s_ys[0], 16 * (TILE_PAIRS + 1))
            pool.wait_ge(s_ys[1], 16 * TILE_PAIRS)
            pool.wait_ge(s_scatter, 16 * TT)
            pool.wait_ge(t2_done, B)
            for i in range(TT):
                nc.gpsimd.indirect_dma_start(x2_all[:, i, :], None, ys_dram,
                                             bass.IndirectOffsetOnAxis(pos_i[:, i:i + 1], 0)
                                             ).then_inc(s_gath[i // NT], 16)

        @block.scalar
        def _(act):
            def front(b):
                act.wait_ge(col_done, b + 1)
                if b > 0:
                    act.wait_ge(row_done, b)
                nc.scalar.activation(gh[:], ring4[0][:, :, 0:D], ACT.Copy).then_inc(gh_copied, 1)
                act.wait_ge(row_done, b + 1)
                if b > 0:
                    act.wait_ge(xn_ready, b)
                nc.scalar.activation(y[:, :, 0:NC], ring4[1][:, :, 0:NC], ACT.Copy).then_inc(a_copied, 1)

            def attend(b):
                act.wait_ge(xt_done, b + 1)
                if b > 0:
                    act.wait_ge(v_done, b)
                nc.scalar.activation(xnT[0:DC, :, :], ring[0][0:DC, :, :], ACT.Copy).then_inc(xt_copied, 1)
                act.wait_ge(q_done, b + 1)
                if b > 0:
                    act.wait_ge(qm_ready, 16 * HEADS * b)
                nc.scalar.activation(qT[:], ring[1][0:DC, :, :], ACT.Copy).then_inc(q_copied, 1)
                act.wait_ge(k_done, b + 1)
                nc.scalar.activation(kT[:], ring[0][0:DC, :, :], ACT.Copy).then_inc(k_copied, 1)
                act.wait_ge(v_done, b + 1)
                if b == 0:
                    act.wait_ge(zeroed, 3)
                else:
                    act.wait_ge(ot_done, 3 * b)
                nc.scalar.activation(va[:, :, :, 0:HD],
                                     ring4[1][:, :, 0:D].rearrange("p t (h d) -> p t h d", d=HD),
                                     ACT.Copy).then_inc(v_copied, 1)
                act.wait_ge(pre_done, b + 1)
                if b > 0:
                    act.wait_ge(ot_copied, 12 * b)
                nc.scalar.activation(pbias[:], misc[:, 0:HG * NT], ACT.Identity,
                                     bias=epscol[:, 0:1]).then_inc(pre_copied, 1)
                for n in range(24):
                    j = n // PAIRS
                    act.wait_ge(s_done, 24 * b + n + 1)
                    if n >= 4 or b > 0:
                        act.wait_ge(av_done, 24 * b + n - 3)
                    w = N - P * j
                    nc.scalar.activation(prob[:, n % 4, :, 0:w], ring[n % 2][:, :, 0:w], ACT.Square,
                                         bias=ones[:, 0:1], scale=0.25).then_inc(sq_done, 1)
                for g in range(HG):
                    act.wait_ge(ot_done, 3 * b + g + 1)
                    if g == 0:
                        act.wait_ge(pre_copied, b + 1)
                        if b > 0:
                            act.wait_ge(wo_done, b)
                    for i in range(NT):
                        nc.scalar.activation(oT[:, g, P * i:P * i + P], att[g][:, P * i:P * i + P],
                                             ACT.Identity,
                                             bias=pbias[:, g * NT + i:g * NT + i + 1]).then_inc(ot_copied, 1)

            act.wait_ge(s_wf, 16 * len(FRONT))
            act.wait_ge(s_wa, 16 * len(ATTN))
            order(front, attend)
            for b in range(B):
                act.wait_ge(t2_done, b + 1)
                if b >= 2:
                    act.wait_ge(lg_done, b - 1)
                nc.scalar.activation((xnT, x2T)[b % 2][0:DC, :, :], ring[b % 2][0:DC, :, :],
                                     ACT.Copy).then_inc(t2_copied, 1)
            act.wait_ge(nd_ready, 1)
            nc.scalar.activation(ex[:], ex[:], ACT.Exp).then_inc(ex_ready, 1)
            nc.scalar.activation(score[:], lg[:, :, E], ACT.Sigmoid).then_inc(sc_ready, 1)

            def copy_slots(i, slot):
                act.wait_ge(xst_done, i + 1)
                ahead(act, up_done, i - 1)
                nc.scalar.activation(xsT[slot][0:DC, :, :],
                                     misc[0:DC, 0:2 * P].rearrange("p (c n) -> p c n", c=2),
                                     ACT.Copy).then_inc(xst_copied, 1)

            def gelu(i, slot):
                act.wait_ge(up_done, i + 1)
                ahead(act, ht_done, i - 1)
                nc.scalar.activation(hg[slot].rearrange("p (a n) -> p a n", a=2),
                                     ring[slot][:, :, 0:HID // 2], ACT.Gelu_apprx_tanh).then_inc(gelu_done, 1)

            def pair(i):
                for k in (1, 2):
                    copy_slots(2 * i + k, k % 2)
                    gelu(2 * i + k, k % 2)

            copy_slots(0, 0)
            gelu(0, 0)
            pair(0)
            with act.Fori(1, TILE_PAIRS) as i:
                pair(i)

        @block.vector
        def _(dve):
            st = Steps(dve, dve_step)

            def convolve(b):
                dve.wait_ge(s_x, 16 * (b + 1))
                if b > 0:
                    dve.wait_ge(pw_done, 2 * b)
                for tap in range(TAPS):
                    for c in range(2):
                        src = xin[:, c, tap:tap + S]
                        w = wdw[:, c, tap:tap + 1]
                        if tap == 0:
                            ins = nc.vector.tensor_scalar(conv[:, c, :], src, w, vec2[:, 0, c:c + 1],
                                                          ALU.mult, ALU.add)
                        else:
                            ins = nc.vector.scalar_tensor_tensor(conv[:, c, :], src, w, conv[:, c, :],
                                                                 ALU.mult, ALU.add)
                        st.mark(ins)
                    st.settle()
                nc.vector.tensor_scalar(nz[:, 0:1], nz[:, 0:1], 1.0, None, ALU.mult).then_inc(conv_done, 1)

            def layernorm(src, dst):
                for i in range(NT):
                    st.mark(nc.vector.bn_stats(stats[:, i, :], src(i)))
                st.settle()
                for i in range(NT):
                    st.mark(nc.vector.bn_aggr(mv[:, i, :], stats[:, i, :]))
                st.settle()
                st.then(nc.vector.tensor_scalar(nx[:], mv[:, :, 1], EPS_LN, None, ALU.add))
                st.then(nc.vector.tensor_scalar(ny[:].bitcast(I32), nx[:].bitcast(I32), -0.5, MAGIC,
                                                ALU.mult, ALU.add))
                for _ in range(RSQRT_ROUNDS):
                    st.then(nc.vector.tensor_tensor(nz[:], ny[:], ny[:], ALU.mult))
                    st.then(nc.vector.scalar_tensor_tensor(nz[:], nz[:], -0.5, nx[:], ALU.mult, ALU.mult))
                    st.then(nc.vector.scalar_tensor_tensor(ny[:], nz[:], 1.5, ny[:], ALU.add, ALU.mult))
                for i in range(NT):
                    st.mark(nc.vector.tensor_scalar(dst(i), src(i), mv[:, i, 0:1], ny[:, i:i + 1],
                                                    ALU.subtract, ALU.mult))
                st.settle()

            def front(b):
                for o in range(2):
                    dve.wait_ge(pw_done, 2 * b + o + 1)
                    if b > 0:
                        dve.wait_ge(col_done, b)
                    pairs = ring[o][0:DC, :, :].rearrange("p a (n two) -> p a n two", two=2)
                    dst = pooled[:, o, :].rearrange("p (a n) -> p a n", a=2)
                    st.then(nc.vector.tensor_reduce(dst, pairs, AX, ALU.max))
                    nc.vector.tensor_scalar(pooled[:, o, :], pooled[:, o, :], vec2[:, 1, o:o + 1], 0.0,
                                            ALU.add, ALU.max).then_inc(pool_done, 1)
                dve.wait_ge(a_copied, b + 1)
                sine = ring4[1][:, :, P:P + NS]
                st.then(nc.vector.tensor_tensor(y[:, :, D - 1:NC - 1:-1], y[:, :, 1:NC - 1], sine, ALU.add))
                st.then(nc.vector.tensor_tensor(y[:, :, 1:NC - 1], y[:, :, 1:NC - 1], sine, ALU.subtract))
                nc.vector.tensor_copy(nz[:, 0:1], y[:, 0, 0:1]).then_inc(y_done, 1)
                layernorm(lambda i: y[:, i, :], lambda i: y[:, i, :])
                if b == 0:
                    dve.wait_ge(s_wa, 16 * len(ATTN))
                else:
                    dve.wait_ge(xt_done, b)
                hb = h_all[:, NT * b:NT * b + NT, :]
                g3 = gamma[:, None, :].to_broadcast([P, NT, D])
                b3 = beta[:, None, :].to_broadcast([P, NT, D])
                st.then(nc.vector.tensor_tensor(hb, y[:], g3, ALU.mult))
                st.then(nc.vector.tensor_tensor(hb, hb, b3, ALU.add))
                layernorm(lambda i: h_all[:, NT * b + i, :], lambda i: xn[:, i, :])
                nc.vector.tensor_copy(nz[:, 0:1], xn[:, 0, 0:1]).then_inc(xn_ready, 1)

            def attend(b):
                if b + 2 < B:
                    convolve(b + 2)
                for g in range(HG):
                    dve.wait_ge(den_done, 3 * b + g + 1)
                    st.then(nc.vector.reciprocal(rden[:], ring[g // 2][:, g % 2, :]))
                    st.then(nc.vector.tensor_tensor(oT[:, g, :], oT[:, g, :], rden[:], ALU.mult))
                    nc.vector.tensor_copy(nz[:, 0:1], oT[:, g, 0:1]).then_inc(o_ready, 1)
                dve.wait_ge(wo_done, b + 1)
                hb = h_all[:, NT * b:NT * b + NT, :]
                st.then(nc.vector.tensor_tensor(hb, hb, ring4[0][:, :, 0:D], ALU.add))
                nc.vector.tensor_copy(nz[:, 0:1], hb[:, 0, 0:1]).then_inc(attn_added, 1)
                layernorm(lambda i: h_all[:, NT * b + i, :], lambda i: x2_all[:, NT * b + i, :])
                nc.vector.tensor_copy(nz[:, 0:1], x2_all[:, NT * b, 0:1]).then_inc(x2_ready, 1)

            st.then(nc.vector.memset(nz[:], 0.0))
            for m in (xnT, x2T, xsT[0], xsT[1]):
                nc.vector.memset(m[DC:DC + 1, :, :], 1.0).then_inc(ones_rows, 1)
            dve.wait_ge(zeroed, 1)
            dve.wait_ge(pool_step, 1)
            dve.wait_ge(s_wf, 16 * len(FRONT))
            convolve(0)
            convolve(1)
            order(front, attend)

            V = nc.vector
            dve.wait_ge(s_wm, 16 * len(MOE))
            dve.wait_ge(lg_done, B)
            st.then(V.tensor_copy(lg[:], misc[:, 0:16 * TT].rearrange("p (t e) -> p t e", e=16)[:, :, 0:E + 1]))
            le = lg[:, :, 0:E]

            def over(ap):
                return ap[:, :, None].to_broadcast([P, TT, E])

            st.then(V.tensor_reduce(mx[:], le, AX, ALU.max))
            V.tensor_tensor(ex[:], le, over(mx), ALU.subtract).then_inc(nd_ready, 1)
            revb = rev[:, None, :].to_broadcast([P, TT, E])
            st.then(V.tensor_tensor(key[:], le, over(mx), ALU.is_ge))
            st.then(V.tensor_tensor(key[:], key[:], revb, ALU.mult))
            st.then(V.tensor_reduce(pos[:], key[:], AX, ALU.max))
            V.tensor_tensor(oh[:], revb, over(pos), ALU.is_equal).then_inc(oh_ready, 1)
            dve.wait_ge(cnt_done, 1)
            dve.wait_ge(oh_ready, 1)
            st.then(V.tensor_copy(cnt[:], att[1][:, 0:P].rearrange("p (t e) -> p e t", e=E)))
            flat = lambda ap: ap[:].rearrange("p e t -> p (e t)")
            st.then(V.tensor_tensor_scan(flat(incl), ones[:], flat(cnt), 0.0, ALU.mult, ALU.add))
            st.then(V.tensor_tensor(excl[:], incl[:], cnt[:], ALU.subtract))
            tot, ntl, ti, tb, base = (et[:, k, :] for k in range(5))
            st.then(V.tensor_tensor(tot, incl[:, :, TT - 1], excl[:, :, 0], ALU.subtract))
            st.then(V.tensor_tensor(cnt[:], tot[:, :, None].to_broadcast([P, E, TT]),
                                    thr[:, None, :].to_broadcast([P, E, TT]), ALU.is_gt))
            st.then(V.tensor_reduce(ntl, cnt[:], AX, ALU.add))
            st.then(V.tensor_tensor_scan(ti, ones[:, 0:E], ntl, 0.0, ALU.mult, ALU.add))
            st.then(V.tensor_tensor(tb, ti, ntl, ALU.subtract))
            st.then(V.scalar_tensor_tensor(base, tb, float(P), excl[:, :, 0], ALU.mult, ALU.subtract))
            st.then(V.tensor_tensor(excl[:], excl[:], base[:, :, None].to_broadcast([P, E, TT]), ALU.add))
            pre = att[0][:, 0:P].rearrange("p (t e) -> p t e", e=E)
            st.then(V.tensor_tensor(key[:], excl[:].rearrange("p e t -> p t e"), pre, ALU.add))
            st.then(V.tensor_tensor(key[:], key[:], oh[:], ALU.mult))
            st.then(V.tensor_reduce(pos[:], key[:], AX, ALU.add))
            V.tensor_copy(pos_i[:], pos[:]).then_inc(pos_ready, 1)
            tcmp = key[0:1, :, :].rearrange("p t e -> p (t e)")
            tiles = wide[0:1, 0:SLOT_TILES * E].rearrange("p (t e) -> p t e", e=E)
            st.then(V.tensor_tensor(tiles, tidx[:, :, None].to_broadcast([1, SLOT_TILES, E]),
                                    ti[0:1, None, :].to_broadcast([1, SLOT_TILES, E]), ALU.is_ge))
            st.then(V.tensor_reduce(te[:], tiles, AX, ALU.add))
            V.tensor_scalar(te_i[:], te[:], float(E - 1), None, ALU.min).then_inc(te_ready, 1)
            dve.wait_ge(ex_ready, 1)
            st.then(V.tensor_reduce(pos[:], ex[:], AX, ALU.add))
            st.then(V.reciprocal(top_p[:], pos[:]))
            dve.wait_ge(st_done, 1)
            V.tensor_copy(score_t[:], misc[0:TT, 256:256 + P]).then_inc(st_copied, 1)

            def copy_hidden(i, slot):
                dve.wait_ge(ht_done, i + 1)
                V.tensor_copy(hT[slot][:, 0:4, :], att[0][:].rearrange("p (c n) -> p c n", n=P)).then_inc(ht_copied, 1)
                V.tensor_copy(hT[slot][:, 4:6, :],
                              att[1][:, 0:2 * P].rearrange("p (c n) -> p c n", n=P)).then_inc(ht_copied, 1)

            def copy_out(i, slot, pair):
                dve.wait_ge(dn_done, i + 1)
                ahead(dve, s_ys[slot], 16 * pair)
                V.tensor_copy(ys[slot], att[2][:, 0:D]).then_inc(ys_copied, 1)

            def copy_pair(i):
                for k in range(2):
                    copy_hidden(2 * i + k, k)
                    copy_out(2 * i + k, k, i)

            copy_pair(0)
            with dve.Fori(1, TILE_PAIRS) as i:
                copy_pair(i)
            copy_hidden(SLOT_TILES - 1, 0)
            copy_out(SLOT_TILES - 1, 0, TILE_PAIRS)

            dve.wait_ge(s_sc_in, 16)
            for i in range(TT):
                b = i // NT
                st.then(V.tensor_scalar(junk, wide[:, N * b:N * b + N], score[:, i:i + 1], None,
                                        ALU.is_gt, ALU.add, accum_out=pos[:, i:i + 1]))
            st.then(V.tensor_scalar(vm[:, TT:2 * TT], pos[:], float(KEEP), None, ALU.is_lt))
            V.memset(f3, 1.0).then_inc(f3_ones, 1)
            for b in range(B):
                dve.wait_ge(s_gath[b], 16 * NT)
                for i in range(NT * b, NT * b + NT):
                    row = x2_all[:, i, :]
                    st.then(V.tensor_scalar(row, row, top_p[:, i:i + 1], None, ALU.mult))
                    st.then(V.tensor_tensor_reduce(junk[:, 0:D], row, wvrow[:], 1.0, 0.0, ALU.mult, ALU.add,
                                                   vm[:, i:i + 1]))
            st.then(V.tensor_scalar(vm[:, 0:TT], vm[:, 0:TT], bvcol[:, 0:1], -V_MAX, ALU.add, ALU.max))
            V.tensor_scalar(vm[:, 0:TT], vm[:, 0:TT], V_MAX, None, ALU.min).then_inc(vm_ready, 1)
            dve.wait_ge(vmt_done, 1)
            V.tensor_copy(vmT[:], misc[0:2 * TT, 0:P]).then_inc(vmt_copied, 1)
            st.then(V.tensor_tensor(h_all[:], h_all[:], x2_all[:], ALU.add))
            st.then(V.tensor_scalar(wof[:], wof[:], scale3[:, 0:1], None, ALU.mult))

            st.then(V.memset(qq[:, 0:2, :, :], 0.0))
            st.mark(V.memset(qq[:, 1, 0, 0:1], 1.0))
            st.then(V.memset(qq[:, 0, 1, 1:2], -1.0))
            dve.wait_ge(s_lane, 16 * 3)
            half = B * CH
            st.then(V.tensor_copy(v2[half:P, :], nv2[half:P, ::-1]))
            st.then(V.tensor_scalar(nv2[:], v2[:], -1.0, None, ALU.mult))
            st.mark(V.tensor_tensor(svd[:, :, 0], v2[:], sgn[:], ALU.mult))
            st.then(V.memset(svd[:, :, 1], -1.0))
            for l in range(LCH):
                new, one, two = qq[:, l + 2, :, :], qq[:, l + 1, :, :], qq[:, l, :, :]
                st.then(V.tensor_tensor(new, one, two, ALU.add))
                st.mark(V.scalar_tensor_tensor(new[:, 0, :], one[:, 1, :], nv2[:, l:l + 1], new[:, 0, :],
                                               ALU.mult, ALU.add))
                st.then(V.scalar_tensor_tensor(new[:, 1, :], one[:, 0, :], v2[:, l:l + 1], new[:, 1, :],
                                               ALU.mult, ALU.add))
            V.tensor_copy(den[:, 0:1], qq[:, LCH + 1, 0, 0:1]).then_inc(ends_ready, 1)
            dve.wait_ge(s_bnd, 16)
            st.mark(V.tensor_scalar(bux[:, :, :, 0], bnd[:, :, :, 1, 0], -1.0, None, ALU.mult))
            st.mark(V.tensor_copy(bux[:, :, :, 1], bnd[:, :, :, 0, 0]))
            st.mark(V.memset(ain[:, 0, 0:1], 1e18))
            st.then(V.memset(ain[:, 0, 1:2], 0.0))
            for c in range(CH - 1):
                sol0, sol1 = bnd[:, c, :, :, 0], bnd[:, c, :, :, 1]
                if c == 0:
                    st.then(V.scalar_tensor_tensor(br[:], sol1, 1e-18, sol0, ALU.mult, ALU.add))
                else:
                    st.then(V.scalar_tensor_tensor(bt[:], sol0, ain[:, c, 0:1], sol1, ALU.mult, ALU.add))
                    st.then(V.scalar_tensor_tensor(br[:], bux[:, c, :, :], ain[:, c, 1:2], bt[:],
                                                   ALU.mult, ALU.add))
                lo, hi = br[:, 0, :], br[:, 1, :]
                st.mark(V.tensor_tensor_reduce(bt[:, 0, :], lo, lo, 1.0, 0.0, ALU.mult, ALU.add, bs[:, 0:1]))
                st.mark(V.tensor_tensor(bs[:, 2:3], hi[:, 0:1], lo[:, 1:2], ALU.mult))
                st.then(V.tensor_tensor_reduce(bt[:, 1, :], lo, hi, -1.0, 0.0, ALU.mult, ALU.add, bs[:, 1:2]))
                st.mark(V.reciprocal(bs[:, 3:4], bs[:, 0:1]))
                st.then(V.scalar_tensor_tensor(bs[:, 4:5], hi[:, 1:2], lo[:, 0:1], bs[:, 2:3],
                                               ALU.mult, ALU.subtract))
                st.mark(V.tensor_tensor(ain[:, c + 1, 0:1], bs[:, 4:5], bs[:, 3:4], ALU.mult))
                st.then(V.tensor_tensor(ain[:, c + 1, 1:2], bs[:, 1:2], bs[:, 3:4], ALU.mult))
            V.tensor_copy(bs[:, 5:6], ain[:, CH - 1, 1:2]).then_inc(ain_ready, 1)
            dve.wait_ge(s_a_in, 16)
            for l in range(LCH):
                cur = lanes[:, l, :]
                st.then(V.tensor_tensor_reduce(sq2[:], cur, cur, 1.0, 0.0, ALU.mult, ALU.add, den[:, 0:1]))
                st.then(V.reciprocal(den[:, 1:2], den[:, 0:1]))
                st.then(V.scalar_tensor_tensor(lanes[:, l + 1, :], cur, den[:, 1:2], svd[:, l, :],
                                               ALU.mult, ALU.add))
            V.tensor_copy(den[:, 0:1], lanes[:, LCH, 0:1]).then_inc(frac_ready, 1)
            dve.wait_ge(s_back, 16)
            fwd = lanes[0:half, 1:LCH + 1, :]
            cr, ci = cc[:, 0, :], cc[:, 1, :]
            st.mark(V.tensor_tensor(cr, fwd[:, :, 0], sgn[0:half, :], ALU.mult))
            st.then(V.tensor_tensor(back[:, :, 0], back[:, :, 0], sgn[0:half, :], ALU.mult))
            st.mark(V.tensor_tensor(cr, cr, back[:, ::-1, 0], ALU.add))
            st.then(V.tensor_tensor(ci, fwd[:, :, 1], back[:, ::-1, 1], ALU.add))
            st.mark(V.tensor_tensor(cr, cr, v2[0:half, :], ALU.subtract))
            st.then(V.tensor_scalar(ci, ci, 1.0, None, ALU.add))
            st.mark(V.tensor_tensor(gg[:, 0, :], cr, cr, ALU.mult))
            st.then(V.tensor_tensor(gg[:, 1, :], ci, ci, ALU.mult))
            st.then(V.tensor_tensor(gg[:, 2, :], gg[:, 0, :], gg[:, 1, :], ALU.add))
            st.then(V.reciprocal(gg[:, 2, :], gg[:, 2, :]))
            st.mark(V.tensor_tensor(gg[:, 0, :], cr, gg[:, 2, :], ALU.mult))
            st.then(V.scalar_tensor_tensor(gg[:, 1, :], ci, -1.0, gg[:, 2, :], ALU.mult, ALU.mult))
            st.then(V.tensor_tensor(gg[:, 0:2, :], gg[:, 0:2, :], mask_l[:, None, :].to_broadcast([half, 2, LCH]),
                                    ALU.mult))
            V.tensor_scalar(gg[:, 0:2, :], gg[:, 0:2, :], CLAMP, -CLAMP, ALU.min, ALU.max).then_inc(feat_ready, 1)
            for b in range(B):
                dve.wait_ge(ft_done, b + 1)
                hb = h_all[:, NT * b:NT * b + NT, :]
                V.tensor_tensor(hb, hb, ring4[b % 2][:, :, 0:D], ALU.add).then_inc(out_ready, 1)

        @block.tensor
        def _(pe):
            def front(b):
                pe.wait_ge(conv_done, b + 1)
                if b > 0:
                    pe.wait_ge(gh_copied, b)
                    pe.wait_ge(y_done, b)
                if b > 1:
                    pe.wait_ge(attn_added, b - 1)
                for o in range(2):
                    for half in range(2):
                        for c in range(2):
                            last = nc.tensor.matmul(ring[o][0:DC, half, :], wpw[:, c, DC * o:DC * o + DC],
                                                    conv[:, c, 512 * half:512 * half + 512],
                                                    start=(c == 0), stop=(c == 1))
                    last.then_inc(pw_done, 1)
                pe.wait_ge(pool_done, 2 * b + 2)
                for i in range(NT):
                    for c in range(2):
                        last = nc.tensor.matmul(ring4[0][:, i, 0:D], pooled[:, c, P * i:P * i + P],
                                                dft_c[:, c, :], start=(c == 0), stop=(c == 1))
                last.then_inc(col_done, 1)
                pe.wait_ge(gh_copied, b + 1)
                for k in range(NT):
                    for table, dst, src in ((cos_n, slice(0, NC), slice(0, NC)),
                                            (sin_n, slice(P, P + NS), slice(NC, D))):
                        for i in range(NT):
                            last = nc.tensor.matmul(ring4[1][:, k, dst], table[:, i, P * k:P * k + P],
                                                    gh[:, i, src], start=(i == 0), stop=(i == NT - 1))
                last.then_inc(row_done, 1)

            def attend(b):
                pe.wait_ge(xn_ready, b + 1)
                if b > 0:
                    pe.wait_ge(attn_added, b)
                for c in range(2):
                    for i in range(NT):
                        last = nc.tensor.transpose(ring[0][0:DC, c, P * i:P * i + P],
                                                   xn[:, i, DC * c:DC * c + DC], ident[:])
                last.then_inc(xt_done, 1)
                pe.wait_ge(xt_copied, b + 1)
                if b + 1 < B:
                    pe.wait_ge(y_done, b + 2)
                for r, w, s in ((1, wq, q_done), (0, wk, k_done)):
                    for o in range(2):
                        for c in range(2):
                            last = nc.tensor.matmul(ring[r][0:DC, o, :], w[:, c, DC * o:DC * o + DC],
                                                    xnT[0:DC, c, :], start=(c == 0), stop=(c == 1))
                    last.then_inc(s, 1)
                pe.wait_ge(q_copied, b + 1)
                for i in range(NT):
                    for c in range(2):
                        last = nc.tensor.matmul(ring4[1][:, i, 0:D], xnT[0:DC, c, P * i:P * i + P],
                                                wv[:, c, :], start=(c == 0), stop=(c == 1))
                last.then_inc(v_done, 1)
                pe.wait_ge(v_copied, b + 1)
                if b > 0:
                    pe.wait_ge(pre_copied, b)
                for g in range(HG):
                    for j in range(NT - 1):
                        last = nc.tensor.matmul(misc[:, NT * g:NT * g + NT],
                                                va[:, j, 4 * g:4 * g + 4, :].rearrange("p h d -> p (h d)"),
                                                steps[:, j, :], start=(j == 0), stop=(j == NT - 2))
                last.then_inc(pre_done, 1)
                pe.wait_ge(k_copied, b + 1)
                pe.wait_ge(qm_ready, 16 * HEADS * (b + 1))
                if b > 0:
                    pe.wait_ge(ot_copied, 12 * b)

                def scores(n):
                    j, pr = divmod(n, PAIRS)
                    if n >= 2:
                        pe.wait_ge(sq_done, 24 * b + n - 1)
                    for h in (2 * pr, 2 * pr + 1):
                        last = nc.tensor.matmul(ring[n % 2][:, h % 2, 0:N - P * j],
                                                kT[:, h // 6, P * j:P * j + P], qm[:, h, P * j:N],
                                                start=True, stop=True)
                    last.then_inc(s_done, 1)

                def values(n):
                    j, pr = divmod(n, PAIRS)
                    g = pr // 2
                    for m in (n, n + 1):
                        pe.wait_ge(p_ready, 24 * b + m + 1)
                        for h in range(2):
                            q = 2 * (m - n) + h
                            last = nc.tensor.matmul(att[g][QUAD * q:QUAD * q + QUAD, P * j:N],
                                                    va[:, j, 4 * g + q, :], prob[:, m % 4, h, 0:N - P * j],
                                                    start=(j == 0), stop=False)
                        last.then_inc(av_done, 1)
                    last = nc.tensor.matmul(att[g][:, P * j:P * j + P],
                                            va[:, j, 4 * g:4 * g + 4, :].rearrange("p h d -> p (h d)"),
                                            tri[:], start=False, stop=(j == NT - 1))
                    if j == NT - 1:
                        last.then_inc(ot_done, 1)

                for n in range(24):
                    scores(n)
                    if n % 2 and n >= 3:
                        values(n - 3)
                values(22)
                for g in range(HG):
                    pe.wait_ge(ot_copied, 12 * b + NT * (g + 1))
                    if g == 0:
                        pe.wait_ge(sq_done, 24 * b + 24)
                    nc.tensor.matmul(ring[g // 2][:, g % 2, :], spread[:], oT[:, g, :],
                                     start=True, stop=True).then_inc(den_done, 1)
                pe.wait_ge(o_ready, 3 * b + 3)
                for i in range(NT):
                    for g in range(HG):
                        last = nc.tensor.matmul(ring4[0][:, i, 0:D], oT[:, g, P * i:P * i + P], wo[:, g, :],
                                                start=(g == 0), stop=(g == HG - 1))
                last.then_inc(wo_done, 1)

            pe.wait_ge(s_wf, 16 * len(FRONT))
            front(0)
            pe.wait_ge(s_wa, 16 * len(ATTN))
            pe.wait_ge(s_wo, 16 * 4)
            for b in range(B - 1):
                front(b + 1)
                attend(b)
            attend(B - 1)

            pe.wait_ge(s_wm, 16 * len(MOE))
            pe.wait_ge(ones_rows, 4)

            def turn(b):
                pe.wait_ge(x2_ready, b + 1)
                if b == 0:
                    pe.wait_ge(attn_added, B)
                if b >= 2:
                    pe.wait_ge(t2_copied, b - 1)
                for c in range(2):
                    for i in range(NT):
                        last = nc.tensor.transpose(ring[b % 2][0:DC, c, P * i:P * i + P],
                                                   x2_all[:, NT * b + i, DC * c:DC * c + DC], ident[:])
                last.then_inc(t2_done, 1)

            turn(0)
            for b in range(B):
                if b + 1 < B:
                    turn(b + 1)
                pe.wait_ge(t2_copied, b + 1)
                for i in range(NT):
                    at = 16 * (NT * b + i)
                    for c in range(2):
                        last = nc.tensor.matmul(misc[:, at:at + E + 1],
                                                (xnT, x2T)[b % 2][0:DC + c, c, P * i:P * i + P],
                                                wgm[0:DC + c, c, :], start=(c == 0), stop=(c == 1))
                last.then_inc(lg_done, 1)
            pe.wait_ge(oh_ready, 1)
            ohf = oh[:].rearrange("p t e -> p (t e)")
            nc.tensor.matmul(att[0][:, 0:P], tri_strict[:], ohf, start=True, stop=True)
            nc.tensor.matmul(att[1][:, 0:P], ones[:], ohf, start=True, stop=True).then_inc(cnt_done, 1)
            pe.wait_ge(sc_ready, 1)
            nc.tensor.transpose(misc[0:TT, 256:256 + P], score[:], ident[:]).then_inc(st_done, 1)

            def turn_slots(i, slot, loads):
                pe.wait_ge(s_xs[slot], 16 * loads)
                ahead(pe, xst_copied, i)
                for c in range(2):
                    last = nc.tensor.transpose(misc[0:DC, P * c:P * c + P], xs[slot][:, DC * c:DC * c + DC],
                                               ident[:])
                last.then_inc(xst_done, 1)

            def up(i, slot):
                e = pe.value_load(te_i[0:1, bass.ds(i, 1)], min_val=0, max_val=E - 1)
                pe.wait_ge(xst_copied, i + 1)
                ahead(pe, gelu_done, i - 1)
                for half in range(2):
                    for c, w in ((0, w1a), (1, w1b)):
                        last = nc.tensor.matmul(ring[slot][:, half, 0:HID // 2], xsT[slot][0:DC + c, c, :],
                                                w[0:DC + c, bass.ds(e * HID + half * (HID // 2), HID // 2)],
                                                start=(c == 0), stop=(c == 1))
                last.then_inc(up_done, 1)

            def turn_hidden(i, slot):
                pe.wait_ge(gelu_done, i + 1)
                ahead(pe, ht_copied, 2 * i)
                for c in range(HC):
                    last = nc.tensor.transpose(att[c // 4][:, P * (c % 4):P * (c % 4) + P],
                                               hg[slot][:, P * c:P * c + P], ident[:])
                last.then_inc(ht_done, 1)

            def down(i, slot):
                e = pe.value_load(te_i[0:1, bass.ds(i, 1)], min_val=0, max_val=E - 1)
                pe.wait_ge(ht_copied, 2 * i + 2)
                ahead(pe, ys_copied, i)
                for c in range(HC):
                    nc.tensor.matmul(att[2][:, 0:D], hT[slot][:, c, :], w2[:, bass.ds((e * HC + c) * D, D)],
                                     start=(c == 0), stop=False)
                nc.tensor.matmul(att[2][:, 0:D], ones[0:1, :], b2[0:1, bass.ds(e * D, D)],
                                 start=False, stop=True).then_inc(dn_done, 1)

            pe.wait_ge(te_ready, 1)
            pe.wait_ge(st_copied, 1)
            pe.wait_ge(s_w1a, 16)
            pe.wait_ge(s_w1b, 16)
            pe.wait_ge(s_w2, 32)

            def expert_pair(i):
                turn_slots(2 * i + 1, 1, i + 1)
                turn_hidden(2 * i, 0)
                up(2 * i + 1, 1)
                down(2 * i, 0)
                turn_slots(2 * i + 2, 0, i + 2)
                turn_hidden(2 * i + 1, 1)
                up(2 * i + 2, 0)
                down(2 * i + 1, 1)

            turn_slots(0, 0, 1)
            up(0, 0)
            expert_pair(0)
            with pe.Fori(1, TILE_PAIRS) as i:
                expert_pair(i)
            turn_hidden(SLOT_TILES - 1, 0)
            down(SLOT_TILES - 1, 0)

            pe.wait_ge(vm_ready, 1)
            nc.tensor.transpose(misc[0:2 * TT, 0:P], vm[:], ident[:]).then_inc(vmt_done, 1)
            pe.wait_ge(s_f3, 32)
            for b in range(B):
                if b >= 2:
                    pe.wait_ge(out_ready, b - 1)
                for i in range(NT):
                    last = nc.tensor.matmul(ring4[b % 2][:, i, 0:D],
                                            f3[:, N * b + P * i:N * b + P * i + P], wof[:],
                                            start=True, stop=True)
                last.then_inc(ft_done, 1)


def layouts(inp, np):
    a = {k: np.asarray(v) for k, v in inp.items()}

    def chunked(w):
        return np.ascontiguousarray(w.reshape(2, DC, -1).transpose(1, 0, 2))

    o = {}
    o["x"] = np.ascontiguousarray(a["x"].reshape(B, S, 2, DC).transpose(0, 3, 2, 1))
    o["w_dw"] = chunked(a["L0_tok_w_dw"][:, 0, :])
    o["vec2"] = np.ascontiguousarray(np.stack([a["L0_tok_b_dw"].reshape(2, DC).T, a["L0_tok_b_pw"].reshape(2, DC).T], 1))
    o["w_pw"] = chunked(a["L0_tok_w_pw"][:, :, 0].T)
    o["gamma"] = np.ascontiguousarray(np.broadcast_to(a["L0_tok_gamma"], (P, D)))
    o["beta"] = np.ascontiguousarray(np.broadcast_to(a["L0_tok_beta"], (P, D)))
    o["wq"] = chunked(a["L0_attn_Wq"].T)
    o["wk"] = chunked(a["L0_attn_Wk"].T)
    o["wv"] = chunked(a["L0_attn_Wv"].T)
    o["wo"] = np.ascontiguousarray(a["L0_attn_Wo"].T.reshape(HG, 4, HD, D).transpose(1, 2, 0, 3))
    f = np.float32
    n = np.arange(N)
    ang = 2 * np.pi * ((n[:, None] * n[None, :]) % N) / N
    o["cos_n"] = np.ascontiguousarray(np.cos(ang).astype(f).reshape(NT, P, N).transpose(1, 0, 2))
    o["sin_n"] = np.ascontiguousarray(np.sin(ang).astype(f).reshape(NT, P, N).transpose(1, 0, 2))
    d = np.arange(D)
    ang = 2 * np.pi * ((d[:, None] * d[None, :]) % D) / D
    o["dft_c"] = chunked(np.concatenate([np.cos(ang[:, :NC]), np.sin(ang[:, 1:NC - 1])], 1).astype(f))
    p = np.arange(P)
    o["ident"] = np.eye(P, dtype=f)
    o["tri"] = (p[:, None] <= p[None, :]).astype(f)
    o["tri_strict"] = (p[:, None] < p[None, :]).astype(f)
    o["spread"] = (p[:, None] == (p[None, :] // QUAD) * QUAD + HD).astype(f)
    o["steps"] = np.broadcast_to((np.arange(NT)[None, :] > np.arange(NT - 1)[:, None]).astype(f), (P, NT - 1, NT)).copy()
    o["ones"] = np.ones((P, P), f)
    o["epscol"] = np.where(p % QUAD == HD, f(EPS_ATTN), f(0)).astype(f)[:, None]
    o["rev"] = np.broadcast_to(np.arange(E, 0, -1).astype(f), (P, E)).copy()
    o["thr"] = np.broadcast_to((P * np.arange(TT)).astype(f), (P, TT)).copy()
    o["tidx"] = np.arange(SLOT_TILES).astype(f)[None, :]
    o["sgn"] = np.broadcast_to(np.where(np.arange(LCH) % 2 == 0, -1.0, 1.0).astype(f), (P, LCH)).copy()
    wgm = np.zeros((DC + 1, 2, E + 1), f)
    wgm[:DC, :, :E] = chunked(a["L0_ffn_Wg"])
    wgm[:DC, :, E] = a["L0_ffn_Wm"].reshape(2, DC).T
    wgm[DC, 1, :E] = a["L0_ffn_bg"]
    wgm[DC, 1, E] = a["L0_ffn_bm"]
    o["wgm"] = wgm
    w1 = a["L0_ffn_W1"].reshape(E, 2, DC, HID).transpose(1, 2, 0, 3).reshape(2, DC, E * HID)
    o["w1a"] = np.ascontiguousarray(w1[0])
    o["w1b"] = np.concatenate([w1[1], a["L0_ffn_b1"].reshape(1, E * HID)], 0)
    o["w2"] = np.ascontiguousarray(a["L0_ffn_W2"].reshape(E, HC, P, D).transpose(2, 0, 1, 3).reshape(P, -1))
    o["b2"] = np.ascontiguousarray(a["L0_ffn_b2"].reshape(1, -1))
    o["wvrow"] = np.ascontiguousarray(np.broadcast_to(a["L0_ffn_Wv"], (P, D)))
    o["bvcol"] = np.ascontiguousarray(np.broadcast_to(a["L0_ffn_bv"], (P, 1)))
    o["wof"] = np.concatenate([a["L0_ffn_Wo"], a["L0_ffn_bo"][None, :]], 0)
    o["scale3"] = np.ascontiguousarray(np.broadcast_to(a["L0_ffn_bk_scale"], (3, 1)))
    return o


def kernel(**inputs):
    import numpy as np
    import concourse.bacc as bacc
    from concourse.bass_utils import run_bass_kernel_spmd as run

    nc = bacc.Bacc("TRN2", target_bir_lowering=False, num_devices=1)
    arrays, t = {}, {}
    for name, a in layouts(inputs, np).items():
        arrays[f"in_{name}"] = a
        t[name] = nc.dram_tensor(f"in_{name}", a.shape, mybir.dt.from_np(a.dtype), kind="ExternalInput").ap()
    t["out"] = nc.dram_tensor("out_0", (B * N, D), F32, kind="ExternalOutput").ap()
    build(nc, t)
    r = run(nc, [arrays], core_ids=[0])
    return r.results[0]["out_0"].reshape(B, N, D)
```

```python
from contextlib import ExitStack

import concourse.bass as bass
from concourse import mybir

P = 128
F32 = mybir.dt.float32
I32 = mybir.dt.int32
BF16 = mybir.dt.bfloat16
ALU = mybir.AluOpType
ACT = mybir.ActivationFunctionType
AX = mybir.AxisListType.X

B, S, D = 4, 1024, 192
DC = D // 2
TAPS = 7
HALO = TAPS // 2
N = S // 2
NT = N // P
TT = B * NT
NC = D // 2 + 1
NS = D // 2 - 1
HEADS, HD = 12, 16
QUAD = 32
HG = HEADS // 4
PARTS = 3
Q_PART = (0, 0, 0, 1, 1, 1, 2, 2)
K_PART = (0, 1, 2, 0, 1, 2, 0, 1)
PAIRS = HEADS // 2
E, HID = 8, 768
HC = HID // P
SLOT_TILES = TT + E - 1
KEEP = int(N * (1.0 - 0.6))
LCH = 32
CH = N // LCH
GR = 4
SL = LCH // GR
LEVELS = CH.bit_length() - 1
GROUP_SCALE = 2.0 ** -7
ROW = D + 2
EPS_LN = 1e-5
EPS_ATTN = 2e-12
V_MAX, CLAMP = 3.0, 10.0
MAGIC = float(0x5F3759DF)
RSQRT_ROUNDS = 4


class Steps:

    def __init__(self, eng, sem):
        self.eng, self.sem, self.count = eng, sem, 0

    def mark(self, ins):
        ins.then_inc(self.sem, 1)
        self.count += 1
        return ins

    def settle(self):
        self.eng.wait_ge(self.sem, self.count)

    def then(self, ins):
        self.mark(ins)
        self.settle()


def ahead(eng, sem, value):
    if not (isinstance(value, int) and value <= 0):
        eng.wait_ge(sem, value)


def build(nc, t):
    with ExitStack() as ctx:
        def sb(name, shape, dt=F32):
            return ctx.enter_context(nc.sbuf_tensor(name, shape, dt))

        def sem(name):
            return ctx.enter_context(nc.semaphore(name))

        ring = [ctx.enter_context(nc.psum_tensor(f"ring{i}", [P, 2, 512], F32)) for i in range(2)]
        att = [ctx.enter_context(nc.psum_tensor(f"att{i}", [P, 512], F32)) for i in range(HG)]
        misc = ctx.enter_context(nc.psum_tensor("misc", [P, 512], F32))
        ring4 = [r[:, :, :].rearrange("p a (b n) -> p (a b) n", b=2) for r in ring]

        wdw = sb("wdw", [DC, 2, TAPS])
        vec2 = sb("vec2", [DC, 2, 2])
        wpw = sb("wpw", [DC, 2, D])
        dft_c = sb("dft_c", [DC, 2, D])
        gamma = sb("gamma", [P, D])
        beta = sb("beta", [P, D])
        wq = sb("wq", [DC, 2, D])
        wk = sb("wk", [DC, 2, D])
        wv = sb("wv", [DC, 2, D])
        wo = sb("wo", [P, HG, D])
        ident = sb("ident", [P, P])
        tri = sb("tri", [P, P])
        tri_strict = sb("tri_strict", [P, P])
        pick = sb("pick", [P, 4])
        steps = sb("steps", [P, NT - 1, NT])
        ones = sb("ones", [P, P])
        epscol = sb("epscol", [P, 1])
        rev = sb("rev", [P, E])
        thr = sb("thr", [P, TT])
        tidx = sb("tidx", [1, SLOT_TILES])
        wgm = sb("wgm", [DC + 1, 2, E + 1])
        w1a = sb("w1a", [DC, E * HID])
        w2 = sb("w2", [P, E * HC * D])
        cos_n = w2[:, 0:NT * N].rearrange("p (i n) -> p i n", n=N)
        sin_n = w2[:, NT * N:2 * NT * N].rearrange("p (i n) -> p i n", n=N)
        at = 2 * NT * N
        xin = w2[0:DC, at:at + 2 * (S + 2 * HALO)].rearrange("p (c n) -> p c n", c=2)
        at += 2 * (S + 2 * HALO)
        assert at <= E * HC * D
        w1b_area = sb("w1b", [P, E * HID])
        w1b = w1b_area[0:DC + 1, :]
        stacks = w1b_area[:].bitcast(BF16).rearrange("p (s h n) -> p s h n", s=2, h=HEADS)
        q_stack, k_stack = stacks[:, 0, :, :], stacks[:, 1, :, :]
        wvrow = sb("wvrow", [P, D])
        bvcol = sb("bvcol", [P, 1])
        wof = sb("wof", [DC, D])
        scale3 = sb("scale3", [DC, 1])

        wide = sb("wide", [P, 2 * S])
        conv = wide[0:DC, :].rearrange("p (c n) -> p c n", c=2)
        pooled = sb("pooled", [DC, 2, N])
        gh = sb("gh", [P, NT, D])
        y = sb("y", [P, NT, D])
        xn = sb("xn", [P, NT, D])
        xnT = sb("xnT", [DC + 1, 2, N])
        x2T = sb("x2T", [DC + 1, 2, N])
        q_parts = [sb(f"q_part{i}", [DC, 2, N], BF16) for i in range(PARTS)]
        k_parts = [sb(f"k_part{i}", [DC, 2, N], BF16) for i in range(PARTS)]
        rest = x2T[0:DC, :, :]
        va = sb("va", [P, NT, HEADS, QUAD])
        probs = sb("probs", [P, 4 * 2 * N])
        prob = probs[:].rearrange("p (a h n) -> p a h n", a=4, h=2)
        rden_wide = probs[:, 0:HG * NT * P].rearrange("p (g h c) -> p g h c", h=4, c=QUAD)
        pbias = sb("pbias", [P, HG * NT])
        oT = sb("oT", [P, HG, N])
        rden = sb("rden", [P, HG * NT, 4])
        h_all = sb("h_all", [P, TT, D])
        x2_all = sb("x2_all", [P, TT, ROW])
        stats = sb("stats", [P, NT, 6])
        mv = sb("mv", [P, NT, 2])
        nx = sb("nx", [P, NT])
        ny = sb("ny", [P, NT])
        nz = sb("nz", [P, NT])

        lg = sb("lg", [P, TT, E + 1])
        score = sb("score", [P, TT])
        mx = sb("mx", [P, TT])
        ex = sb("ex", [P, TT, E])
        top_p = sb("top_p", [P, TT])
        oh = sb("oh", [P, TT, E])
        key = sb("key", [P, TT, E])
        cnt = sb("cnt", [P, E, TT])
        incl = sb("incl", [P, E, TT])
        excl = sb("excl", [P, E, TT])
        et = sb("et", [P, 6, E])
        pos = sb("pos", [P, TT])
        pos_i = sb("pos_i", [P, TT], I32)
        te = sb("te", [1, SLOT_TILES])
        te_i = sb("te_i", [1, SLOT_TILES], I32)
        mask = sb("mask", [P, TT])
        mask_t = sb("mask_t", [TT, P])
        score_t = sb("score_t", [TT, P])
        empty = sb("empty", [P, ROW])
        token_row = sb("token_row", [P, TT])
        xs = [probs[:, ROW * i:ROW * i + ROW] for i in range(2)]
        at = 2 * ROW
        ys = [probs[:, at + D * i:at + D * (1 + i)] for i in range(2)]
        at += 2 * D
        hg = [probs[:, at + HID * i:at + HID * (i + 1)] for i in range(2)]
        hT = [probs[:, at + HID * (2 + i):at + HID * (3 + i)].rearrange("p (c n) -> p c n", n=P)
              for i in range(2)]
        weight = [sb(f"weight{i}", [P, 1]) for i in range(2)]
        target = [sb(f"target{i}", [P, 1], I32) for i in range(2)]
        v_col = [sb(f"v_col{i}", [P, 1]) for i in range(2)]
        b2 = oT[0:1, :, :].rearrange("p g n -> p (g n)")
        junk = y[:].rearrange("p a b -> p (a b)")[:, 0:N]
        xsT = [sb(f"xsT{i}", [DC + 1, 2, P]) for i in range(2)]
        v2 = sb("v2", [P, LCH])
        v_raw = sb("v_raw", [P, LCH])
        vv = sb("vv", [P, GR, SL, 2])
        neg_pos = sb("neg_pos", [P, 2])
        qq = sb("qq", [P, SL + 2, GR, 2, 2])
        qv = sb("qv", [P, GR, 2, 2])
        gm = sb("gm", [P, GR, 4, 4])
        gp = sb("gp", [P, GR, 4, 4])
        lm = [sb(f"lm{i}", [P, 4, 4]) for i in range(2)]
        size = sb("size", [P, 4])
        start = sb("start", [P, GR, 2, 2])
        sw = sb("sw", [P, 2, GR, 2, 2])
        xp = sb("xp", [P, 2, SL + 1, GR, 4])
        xx = sb("xx", [P, 2, SL + 1, GR])
        fa = sb("fa", [P, 2, SL, GR])
        fb = sb("fb", [P, 6, SL, GR])
        gg = sb("gg", [B * CH, 2, LCH])
        mask_l = sb("mask_l", [B * CH, LCH])
        f3 = wide[0:DC, 0:B * N]
        scan_tab = xn[:].rearrange("p t d -> p (t d)")[:, 0:LEVELS * P + LEVELS * 16 + B * CH]
        shift = [scan_tab[:, P * i:P * i + P] for i in range(LEVELS)]
        unit = [scan_tab[:, LEVELS * P + 16 * i:LEVELS * P + 16 * i + 16] for i in range(LEVELS)]
        flip = scan_tab[:, LEVELS * (P + 16):LEVELS * (P + 16) + B * CH]
        def dram(name, shape, dt=F32):
            return nc.dram_tensor(name, shape, dt, kind="Internal").ap()

        part_dram = [dram(f"{n}_parts", (PARTS, HD, HEADS, N), BF16) for n in "qk"]

        xs_dram = dram("tokens_by_expert", (SLOT_TILES * P, ROW))
        ffn_dram = dram("ffn_by_token", (B * N + P, D))
        v_dram = dram("v_by_token", (B * N + P, 1))
        v_lanes = v_dram[0:B * N, :].rearrange("(b c l) one -> b c (l one)", b=B, l=LCH)
        sc_dram = dram("scores_linear", (B * N,))

        s_x = sem("x_loaded")
        s_wc = sem("conv_weights_loaded")
        s_wf = sem("front_weights_loaded")
        s_wa = sem("attention_weights_loaded")
        s_wo = sem("output_projection_loaded")
        s_wm = sem("moe_weights_loaded")
        s_out = sem("output_stored")
        zeroed = sem("buffers_zeroed")
        conv_done = sem("conv_done")
        pw_done = sem("pointwise_done")
        pool_done = sem("pooled_done")
        col_done = sem("channel_dft_done")
        gh_copied = sem("gh_copied")
        row_done = sem("token_dft_done")
        a_copied = sem("cosine_part_copied")
        y_done = sem("y_done")
        xn_ready = sem("xn_ready")
        q1_ready, q2_ready, q3_ready = sem("q_part1"), sem("q_part2"), sem("q_part3")
        k1_ready, k2_ready, k3_ready = sem("k_part1"), sem("k_part2"), sem("k_part3")
        q_rest, k_rest = sem("q_rest"), sem("k_rest")
        s_part_out = [sem("q_parts_stored"), sem("k_parts_stored")]
        s_stack = sem("stacks_loaded")
        xt_done = sem("xn_transposed")
        xt_copied = sem("xnT_copied")
        q_done, k_done, v_done = sem("q_done"), sem("k_done"), sem("v_done")
        v_copied = sem("v_copied")
        pre_done = sem("prefix_done")
        pre_copied = sem("prefix_copied")
        s_done = sem("scores_done")
        sq_done = sem("squared")
        p_ready = sem("weights_ready")
        av_done = sem("weights_used")
        ot_done = sem("attention_sums_done")
        ot_copied = sem("attention_sums_copied")
        den_done = sem("denominators_by_token")
        rden_ready = sem("reciprocals_ready")
        den_spread = sem("reciprocals_spread")
        o_ready = sem("attention_normalised")
        wo_done = sem("attention_projected")
        attn_added = sem("attention_added")
        x2_ready = sem("x2_ready")
        dve_step, act_step, pool_step = sem("dve_step"), sem("act_step"), sem("pool_step")
        ones_rows = sem("bias_rows_ready")
        t2_done, t2_copied = sem("x2_transposed"), sem("x2T_copied")
        lg_done, lg_copied = sem("logits_done"), sem("logits_copied")
        nd_ready, ex_ready, sc_ready = sem("logits_shifted"), sem("exp_ready"), sem("score_ready")
        oh_ready, cnt_done = sem("one_hot_ready"), sem("counts_done")
        pos_ready, te_ready = sem("positions_ready"), sem("tile_experts_ready")
        s_empty, s_fill, s_scatter = sem("empty_row_loaded"), sem("slots_filled"), sem("tokens_scattered")
        mask_ready, mt_done, mt_copied = sem("mask_ready"), sem("mask_transposed"), sem("mask_t_copied")
        s_mask = sem("mask_in_lanes")
        st_done, st_copied = sem("scores_transposed"), sem("score_t_copied")
        s_sc_out, s_sc_in = sem("scores_stored"), sem("scores_spread")
        s_w1a, s_w1b, s_w2 = sem("w1a_loaded"), sem("w1b_loaded"), sem("w2_loaded")
        s_xs = [sem(f"slots_loaded{i}") for i in range(2)]
        xst_done, xst_copied = sem("slots_transposed"), sem("slots_t_copied")
        up_done, gelu_done = sem("up_done"), sem("gelu_done")
        ht_done, ht_copied = sem("hidden_transposed"), sem("hidden_t_copied")
        target_copied, weight_copied = sem("slot_targets_copied"), sem("slot_weights_copied")
        dn_done, ys_copied, vc_ready = sem("down_done"), sem("expert_out_copied"), sem("v_col_ready")
        s_ys = [sem(f"expert_out_stored{i}") for i in range(2)]
        s_ffn = [sem(f"ffn_loaded{b}") for b in range(B)]
        h_added, stores_begun = sem("ffn_added"), sem("stores_begun")
        s_scan, s_lane = sem("scan_tables_loaded"), sem("lanes_loaded")
        lm_ready, lm_shifted = sem("lane_products_ready"), sem("lane_products_shifted")
        start_done = sem("lane_starts_done")
        frac_ready, flip_done = sem("fraction_ready"), sem("backward_fraction_flipped")
        feat_ready, s_f3, f3_ones = sem("features_ready"), sem("features_spread"), sem("f3_ones")
        ft_done, out_ready = sem("feature_rows_done"), sem("output_ready")

        block = ctx.enter_context(nc.Block())
        CONV = [(wdw, "w_dw"), (vec2, "vec2")]
        FRONT = [(wpw, "w_pw"), (dft_c, "dft_c"), (cos_n, "cos_n"), (sin_n, "sin_n")]
        ATTN = [(gamma, "gamma"), (beta, "beta"), (ident, "ident"), (wq, "wq"), (wk, "wk"), (wv, "wv"),
                (tri, "tri"), (pick, "pick"), (steps, "steps"), (ones, "ones"), (epscol, "epscol")]
        MOE = [(tri_strict, "tri_strict"), (rev, "rev"), (thr, "thr"), (tidx, "tidx"), (wgm, "wgm"),
               (wvrow, "wvrow"), (bvcol, "bvcol"), (wof, "wof"), (scale3, "scale3"), (token_row, "token_row")]
        TILE_PAIRS = (SLOT_TILES - 1) // 2
        assert SLOT_TILES % 2 == 1

        def order(front, project, attend):
            front(0)
            front(1)
            project(0)
            attend(0)
            project(1)
            for b in range(1, B):
                if b + 1 < B:
                    front(b + 1)
                attend(b)
                if b + 1 < B:
                    project(b + 1)

        @block.sync
        def _(sp):
            def load(dst, name, s):
                sp.dma_start(dst if isinstance(dst, bass.AP) else dst[:], t[name]).then_inc(s, 16)

            def load_x(b):
                if b > 0:
                    sp.wait_ge(conv_done, b)
                sp.dma_start(xin[:, :, HALO:HALO + S], t["x"][b]).then_inc(s_x, 16)

            for dst, name in CONV:
                load(dst, name, s_wc)
            load_x(0)
            for dst, name in FRONT:
                load(dst, name, s_wf)
            load_x(1)
            for dst, name in ATTN:
                load(dst, name, s_wa)
            sp.wait_ge(zeroed, 2)
            for q in range(4):
                sp.dma_start(wo[QUAD * q:QUAD * q + HD, :, :], t["wo"][q]).then_inc(s_wo, 16)

            def front(b):
                if 0 < b < B - 1:
                    load_x(b + 1)

            def project(b):
                for dram_, parts, ready, out, stack, which in (
                        (part_dram[0], q_parts, (q1_ready, q2_ready, q3_ready), s_part_out[0], q_stack, Q_PART),
                        (part_dram[1], k_parts, (k1_ready, k2_ready, k3_ready), s_part_out[1], k_stack, K_PART)):
                    for i in range(PARTS):
                        sp.wait_ge(ready[i], b + 1)
                        if b > 0 and i == 0:
                            sp.wait_ge(s_stack, 16 * 6 * b)
                        for o in range(2):
                            sp.dma_start(dram_[i, :, 6 * o:6 * o + 6, :].rearrange("d h n -> h d n"),
                                         parts[i][:, o, :]).then_inc(out, 16)
                    sp.wait_ge(out, 16 * 2 * PARTS * (b + 1))
                    if b > 0:
                        sp.wait_ge(s_done, 24 * b)
                    if which is Q_PART:
                        for i in range(PARTS):
                            m = which.count(i)
                            r = HD * which.index(i)
                            sp.dma_start(stack[r:r + HD * m, :, :],
                                         dram_[i][None, :, :, :].to_broadcast([m, HD, HEADS, N])
                                         ).then_inc(s_stack, 16)
                    else:
                        for first in range(0, len(which), PARTS):
                            m = min(PARTS, len(which) - first)
                            sp.dma_start(stack[HD * first:HD * (first + m), :, :],
                                         dram_[0:m].rearrange("i d h n -> (i d) h n")).then_inc(s_stack, 16)

            def attend(b):
                pass

            load(empty, "empty_row", s_empty)
            sp.wait_ge(s_empty, 16)
            for i in range(SLOT_TILES):
                sp.dma_start(xs_dram[P * i:P * i + P, :], empty[:]).then_inc(s_fill, 16)
            for dst, name in MOE:
                load(dst, name, s_wm)
            sp.dma_start(w1a[:], t["w1a"]).then_inc(s_w1a, 16)
            order(front, project, attend)
            sp.wait_ge(row_done, B)
            sp.wait_ge(conv_done, B)
            sp.dma_start(w2[:], t["w2"]).then_inc(s_w2, 16)
            sp.wait_ge(s_done, 24 * B)
            sp.dma_start(w1b[:], t["w1b"]).then_inc(s_w1b, 16)
            sp.wait_ge(wo_done, B)
            sp.dma_start(b2, t["b2"]).then_inc(s_w2, 16)
            sp.wait_ge(xt_done, B)
            load(scan_tab, "scan_tab", s_scan)
            sp.wait_ge(st_copied, 1)
            sp.dma_start(sc_dram.rearrange("(t n) -> t n", n=P), score_t[:]).then_inc(s_sc_out, 16)
            sp.wait_ge(s_sc_out, 16)
            sp.wait_ge(conv_done, B)
            sp.wait_ge(pw_done, 2 * B)
            sp.dma_start(wide[:], sc_dram[None, :].to_broadcast([P, B * N])).then_inc(s_sc_in, 16)
            sp.wait_ge(mt_copied, 1)
            sp.dma_start(mask_l[:], mask_t[:]).then_inc(s_mask, 16)
            sp.wait_ge(s_scatter, 16 * TT)

            def load_slots(i, slot):
                sp.dma_start(xs[slot], xs_dram[bass.ds(i * P, P), :]).then_inc(s_xs[slot], 16)

            def load_pair(i):
                for value, slot in ((2 * i, 1), (2 * i + 1, 0)):
                    for left in (xst_done, target_copied, weight_copied):
                        ahead(sp, left, value)
                    load_slots(value + 1, slot)

            load_slots(0, 0)
            load_pair(0)
            with sp.Fori(1, TILE_PAIRS) as i:
                load_pair(i)

            sp.wait_ge(s_ys[0], 32 * (TILE_PAIRS + 1))
            sp.wait_ge(s_ys[1], 32 * TILE_PAIRS)
            sp.dma_start(v2[0:B * CH, :], v_lanes.rearrange("b c l -> (b c) l")).then_inc(s_lane, 16)
            sp.dma_start(v_raw[B * CH:P, :], v_lanes[:, ::-1, :]).then_inc(s_lane, 16)
            sp.wait_ge(t2_done, B)
            for b in range(B):
                sp.dma_start(x2_all[:, NT * b:NT * b + NT, 0:D],
                             ffn_dram[N * b:N * b + N, :].rearrange("(n p) d -> p n d", p=P)
                             ).then_inc(s_ffn[b], 16)
            sp.wait_ge(feat_ready, 1)
            sp.wait_ge(f3_ones, 1)
            for k in range(2):
                sp.dma_start(f3[k:k + 1, :], gg[:, k, :]).then_inc(s_f3, 16)
            for b in range(B):
                sp.wait_ge(out_ready, b + 1)
                sp.dma_start(t["out"][N * b:N * b + N, :].rearrange("(n p) d -> p n d", p=P),
                             h_all[:, NT * b:NT * b + NT, :]).then_inc(s_out, 16)
            sp.wait_ge(s_out, 16 * B)

        @block.gpsimd
        def _(pool):
            nc.gpsimd.memset(xin[:, :, 0:HALO], 0.0).then_inc(pool_step, 1)
            nc.gpsimd.memset(xin[:, :, HALO + S:], 0.0).then_inc(zeroed, 1)
            nc.gpsimd.memset(wo[:], 0.0).then_inc(zeroed, 1)
            nc.gpsimd.memset(va[:], 0.0).then_inc(pool_step, 1)
            pool.wait_ge(pool_step, 2)
            nc.gpsimd.memset(va[:, :, :, HD:HD + 1], 1.0).then_inc(zeroed, 1)

            def front(b):
                pass

            def project(b):
                pass

            def attend(b):
                if b == 0:
                    pool.wait_ge(s_wa, 16 * len(ATTN))
                for n in range(24):
                    pool.wait_ge(sq_done, 24 * b + n + 1)
                    diag = prob[:, n % 4, :, 0:P]
                    nc.gpsimd.tensor_tensor(diag, diag, tri[:, None, :].to_broadcast([P, 2, P]),
                                            ALU.mult).then_inc(p_ready, 1)

            order(front, project, attend)
            pool.wait_ge(s_fill, 16 * SLOT_TILES)
            pool.wait_ge(x2_ready, B)
            pool.wait_ge(pos_ready, 1)
            for i in range(TT):
                nc.gpsimd.indirect_dma_start(xs_dram, bass.IndirectOffsetOnAxis(pos_i[:, i:i + 1], 0),
                                             x2_all[:, i, :], None).then_inc(s_scatter, 16)

            def store_slots(i, slot, others):
                pool.wait_ge(vc_ready, i + 1)
                ahead(pool, s_ys[1 - slot], 32 * others)
                pool.sem_inc(stores_begun, 1)
                for out, src in ((v_dram, v_col[slot][:]), (ffn_dram, ys[slot])):
                    nc.gpsimd.indirect_dma_start(out, bass.IndirectOffsetOnAxis(target[slot][:], 0),
                                                 src, None).then_inc(s_ys[slot], 16)

            def store_pair(i):
                store_slots(2 * i, 0, i)
                store_slots(2 * i + 1, 1, i + 1)

            store_pair(0)
            with pool.Fori(1, TILE_PAIRS) as i:
                store_pair(i)
            store_slots(SLOT_TILES - 1, 0, TILE_PAIRS)
            for b in range(B):
                pool.wait_ge(s_ffn[b], 16)
                hb = h_all[:, NT * b:NT * b + NT, :]
                nc.gpsimd.tensor_tensor(hb, hb, x2_all[:, NT * b:NT * b + NT, 0:D], ALU.add
                                        ).then_inc(h_added, 1)

        @block.scalar
        def _(act):
            def front(b):
                act.wait_ge(col_done, b + 1)
                if b > 0:
                    act.wait_ge(row_done, b)
                nc.scalar.activation(gh[:], ring4[0][:, :, 0:D], ACT.Copy).then_inc(gh_copied, 1)
                act.wait_ge(row_done, b + 1)
                if b > 0:
                    act.wait_ge(xn_ready, b)
                nc.scalar.activation(y[:, :, 0:NC], ring4[1][:, :, 0:NC], ACT.Copy).then_inc(a_copied, 1)

            def attend(b):
                for n in range(24):
                    j = n // PAIRS
                    act.wait_ge(s_done, 24 * b + n + 1)
                    if n == 0 and b > 0:
                        act.wait_ge(den_spread, 3 * b)
                    if n >= 4 or b > 0:
                        act.wait_ge(av_done, 24 * b + n - 3)
                    w = N - P * j
                    nc.scalar.activation(prob[:, n % 4, :, 0:w], ring[n % 2][:, :, 0:w], ACT.Square,
                                         bias=ones[:, 0:1], scale=0.25).then_inc(sq_done, 1)

            def sums(b):
                for g in range(HG):
                    act.wait_ge(ot_done, 3 * b + g + 1)
                    if g == 0:
                        act.wait_ge(pre_copied, b + 1)
                        if b > 0:
                            act.wait_ge(wo_done, b)
                    for i in range(NT):
                        nc.scalar.activation(oT[:, g, P * i:P * i + P], att[g][:, P * i:P * i + P],
                                             ACT.Identity,
                                             bias=pbias[:, g * NT + i:g * NT + i + 1]).then_inc(ot_copied, 1)

            def project(b):
                act.wait_ge(xt_done, b + 1)
                if b > 0:
                    act.wait_ge(v_done, b)
                nc.scalar.activation(xnT[0:DC, :, :], ring[0][0:DC, :, :], ACT.Copy).then_inc(xt_copied, 1)
                if b > 0:
                    sums(b - 1)
                for s, part, ready1, ready2, rest_ready, r, out in (
                        (q_done, q_parts, q1_ready, q2_ready, q_rest, 1, s_part_out[0]),
                        (k_done, k_parts, k1_ready, k2_ready, k_rest, 0, s_part_out[1])):
                    act.wait_ge(s, b + 1)
                    if b > 0:
                        act.wait_ge(out, 16 * 2 * PARTS * b)
                    nc.scalar.activation(part[0][:], ring[r][0:DC, :, :], ACT.Copy).then_inc(ready1, 1)
                    if r == 0:
                        act.wait_ge(v_done, b + 1)
                        if b == 0:
                            act.wait_ge(zeroed, 3)
                        else:
                            act.wait_ge(ot_done, 3 * b)
                        nc.scalar.activation(va[:, :, :, 0:HD],
                                             ring4[1][:, :, 0:D].rearrange("p t (h d) -> p t h d", d=HD),
                                             ACT.Copy).then_inc(v_copied, 1)
                    act.wait_ge(rest_ready, b + 1)
                    nc.scalar.activation(part[1][:], rest, ACT.Copy).then_inc(ready2, 1)
                act.wait_ge(pre_done, b + 1)
                if b > 0:
                    act.wait_ge(ot_copied, 12 * b)
                nc.scalar.activation(pbias[:], misc[:, 0:HG * NT], ACT.Identity,
                                     bias=epscol[:, 0:1]).then_inc(pre_copied, 1)

            act.wait_ge(s_wa, 16 * len(ATTN))
            order(front, project, attend)
            sums(B - 1)
            for b in range(B):
                act.wait_ge(t2_done, b + 1)
                if b >= 2:
                    act.wait_ge(lg_done, b - 1)
                nc.scalar.activation((xnT, x2T)[b % 2][0:DC, :, :], ring[b % 2][0:DC, :, :],
                                     ACT.Copy).then_inc(t2_copied, 1)
            act.wait_ge(nd_ready, 1)
            nc.scalar.activation(ex[:], ex[:], ACT.Exp).then_inc(ex_ready, 1)
            nc.scalar.activation(score[:], lg[:, :, E], ACT.Sigmoid).then_inc(sc_ready, 1)

            def copy_slots(i, slot):
                act.wait_ge(xst_done, i + 1)
                ahead(act, up_done, i - 1)
                nc.scalar.activation(xsT[slot][0:DC, :, :],
                                     misc[0:DC, 0:2 * P].rearrange("p (c n) -> p c n", c=2),
                                     ACT.Copy).then_inc(xst_copied, 1)

            def gelu(i, slot):
                act.wait_ge(up_done, i + 1)
                ahead(act, ht_done, i - 1)
                nc.scalar.activation(hg[slot].rearrange("p (a n) -> p a n", a=2),
                                     ring[slot][:, :, 0:HID // 2], ACT.Gelu_apprx_tanh).then_inc(gelu_done, 1)

            def pair(i):
                for k in (1, 2):
                    copy_slots(2 * i + k, k % 2)
                    gelu(2 * i + k, k % 2)

            copy_slots(0, 0)
            gelu(0, 0)
            pair(0)
            with act.Fori(1, TILE_PAIRS) as i:
                pair(i)

        @block.vector
        def _(dve):
            st = Steps(dve, dve_step)

            def convolve(b):
                dve.wait_ge(s_x, 16 * (b + 1))
                if b == 0:
                    dve.wait_ge(s_wc, 16 * len(CONV))
                if b > 0:
                    dve.wait_ge(pw_done, 2 * b)
                for tap in range(TAPS):
                    for c in range(2):
                        src = xin[:, c, tap:tap + S]
                        w = wdw[:, c, tap:tap + 1]
                        if tap == 0:
                            ins = nc.vector.tensor_scalar(conv[:, c, :], src, w, vec2[:, 0, c:c + 1],
                                                          ALU.mult, ALU.add)
                        else:
                            ins = nc.vector.scalar_tensor_tensor(conv[:, c, :], src, w, conv[:, c, :],
                                                                 ALU.mult, ALU.add)
                        st.mark(ins)
                    st.settle()
                nc.vector.tensor_scalar(nz[:, 0:1], nz[:, 0:1], 1.0, None, ALU.mult).then_inc(conv_done, 1)

            def layernorm(src, dst):
                for i in range(NT):
                    st.mark(nc.vector.bn_stats(stats[:, i, :], src(i)))
                st.settle()
                for i in range(NT):
                    st.mark(nc.vector.bn_aggr(mv[:, i, :], stats[:, i, :]))
                st.settle()
                st.then(nc.vector.tensor_scalar(nx[:], mv[:, :, 1], EPS_LN, None, ALU.add))
                st.then(nc.vector.tensor_scalar(ny[:].bitcast(I32), nx[:].bitcast(I32), -0.5, MAGIC,
                                                ALU.mult, ALU.add))
                for _ in range(RSQRT_ROUNDS):
                    st.then(nc.vector.tensor_tensor(nz[:], ny[:], ny[:], ALU.mult))
                    st.then(nc.vector.scalar_tensor_tensor(nz[:], nz[:], -0.5, nx[:], ALU.mult, ALU.mult))
                    st.then(nc.vector.scalar_tensor_tensor(ny[:], nz[:], 1.5, ny[:], ALU.add, ALU.mult))
                for i in range(NT):
                    st.mark(nc.vector.tensor_scalar(dst(i), src(i), mv[:, i, 0:1], ny[:, i:i + 1],
                                                    ALU.subtract, ALU.mult))
                st.settle()

            def pool(b):
                for o in range(2):
                    dve.wait_ge(pw_done, 2 * b + o + 1)
                    if b > 0:
                        dve.wait_ge(col_done, b)
                    pairs = ring[o][0:DC, :, :].rearrange("p a (n two) -> p a n two", two=2)
                    dst = pooled[:, o, :].rearrange("p (a n) -> p a n", a=2)
                    st.then(nc.vector.tensor_reduce(dst, pairs, AX, ALU.max))
                    nc.vector.tensor_scalar(pooled[:, o, :], pooled[:, o, :], vec2[:, 1, o:o + 1], 0.0,
                                            ALU.add, ALU.max).then_inc(pool_done, 1)

            def untangle(b):
                dve.wait_ge(a_copied, b + 1)
                sine = ring4[1][:, :, P:P + NS]
                st.then(nc.vector.tensor_tensor(y[:, :, D - 1:NC - 1:-1], y[:, :, 1:NC - 1], sine, ALU.add))
                st.then(nc.vector.tensor_tensor(y[:, :, 1:NC - 1], y[:, :, 1:NC - 1], sine, ALU.subtract))
                nc.vector.tensor_copy(nz[:, 0:1], y[:, 0, 0:1]).then_inc(y_done, 1)

            def normalise(b):
                layernorm(lambda i: y[:, i, :], lambda i: y[:, i, :])
                if b == 0:
                    dve.wait_ge(s_wa, 16 * len(ATTN))
                else:
                    dve.wait_ge(xt_done, b)
                hb = h_all[:, NT * b:NT * b + NT, :]
                g3 = gamma[:, None, :].to_broadcast([P, NT, D])
                b3 = beta[:, None, :].to_broadcast([P, NT, D])
                st.then(nc.vector.tensor_tensor(hb, y[:], g3, ALU.mult))
                st.then(nc.vector.tensor_tensor(hb, hb, b3, ALU.add))
                layernorm(lambda i: h_all[:, NT * b + i, :], lambda i: xn[:, i, :])
                nc.vector.tensor_copy(nz[:, 0:1], xn[:, 0, 0:1]).then_inc(xn_ready, 1)

            def front(b):
                pool(b)
                if b == 0:
                    convolve(1)
                untangle(b)
                if b != 1:
                    normalise(b)
                if 1 < b < B - 1:
                    convolve(b + 1)

            def project(b):
                for src, part, ready1, rest_ready, ready2, ready3 in (
                        (ring[1], q_parts, q1_ready, q_rest, q2_ready, q3_ready),
                        (ring[0], k_parts, k1_ready, k_rest, k2_ready, k3_ready)):
                    dve.wait_ge(ready1, b + 1)
                    nc.vector.tensor_tensor(rest, src[0:DC, :, :], part[0][:], ALU.subtract
                                            ).then_inc(rest_ready, 1)
                    dve.wait_ge(ready2, b + 1)
                    dve.wait_ge(rest_ready, b + 1)
                    nc.vector.tensor_tensor(part[2][:], rest, part[1][:], ALU.subtract).then_inc(ready3, 1)
                    dve.wait_ge(ready3, b + 1)
                if b == 0:
                    normalise(1)
                    convolve(2)
                else:
                    finish(b - 1)

            def attend(b):
                pass

            def finish(b):
                dve.wait_ge(den_done, b + 1)
                st.then(nc.vector.reciprocal(rden[:], misc[:, 64:64 + HG * NT * 4].rearrange("p (g h) -> p g h", h=4)))
                nc.vector.tensor_copy(rden_wide, rden[:, :, :, None].to_broadcast([P, HG * NT, 4, QUAD])
                                      ).then_inc(rden_ready, 1)
                for g in range(HG):
                    dve.wait_ge(den_spread, 3 * b + g + 1)
                    nc.vector.tensor_tensor(oT[:, g, :], oT[:, g, :], ring[g // 2][:, g % 2, :], ALU.mult
                                            ).then_inc(o_ready, 1)
                dve.wait_ge(wo_done, b + 1)
                hb = h_all[:, NT * b:NT * b + NT, :]
                st.then(nc.vector.tensor_tensor(hb, hb, ring4[0][:, :, 0:D], ALU.add))
                nc.vector.tensor_copy(nz[:, 0:1], hb[:, 0, 0:1]).then_inc(attn_added, 1)
                layernorm(lambda i: h_all[:, NT * b + i, :], lambda i: x2_all[:, NT * b + i, 0:D])
                nc.vector.tensor_copy(nz[:, 0:1], x2_all[:, NT * b, 0:1]).then_inc(x2_ready, 1)

            st.then(nc.vector.memset(nz[:], 0.0))
            for m in (xnT, x2T, xsT[0], xsT[1]):
                nc.vector.memset(m[DC:DC + 1, :, :], 1.0).then_inc(ones_rows, 1)
            dve.wait_ge(zeroed, 1)
            dve.wait_ge(pool_step, 1)
            convolve(0)
            order(front, project, attend)
            finish(B - 1)

            V = nc.vector
            dve.wait_ge(s_wm, 16 * len(MOE))
            dve.wait_ge(lg_done, B)
            st.then(V.tensor_copy(lg[:], misc[:, 0:16 * TT].rearrange("p (t e) -> p t e", e=16)[:, :, 0:E + 1]))
            le = lg[:, :, 0:E]

            def over(ap):
                return ap[:, :, None].to_broadcast([P, TT, E])

            st.then(V.tensor_reduce(mx[:], le, AX, ALU.max))
            V.tensor_tensor(ex[:], le, over(mx), ALU.subtract).then_inc(nd_ready, 1)
            revb = rev[:, None, :].to_broadcast([P, TT, E])
            st.then(V.tensor_tensor(key[:], le, over(mx), ALU.is_ge))
            st.then(V.tensor_tensor(key[:], key[:], revb, ALU.mult))
            st.then(V.tensor_reduce(pos[:], key[:], AX, ALU.max))
            V.tensor_tensor(oh[:], revb, over(pos), ALU.is_equal).then_inc(oh_ready, 1)
            dve.wait_ge(ex_ready, 1)
            st.mark(V.tensor_copy(x2_all[:, :, D + 1], token_row[:]))
            st.then(V.tensor_reduce(mx[:], ex[:], AX, ALU.add))
            st.then(V.reciprocal(x2_all[:, :, D], mx[:]))
            dve.wait_ge(cnt_done, 1)
            dve.wait_ge(oh_ready, 1)
            st.then(V.tensor_copy(cnt[:], att[1][:, 0:P].rearrange("p (t e) -> p e t", e=E)))
            flat = lambda ap: ap[:].rearrange("p e t -> p (e t)")
            st.then(V.tensor_tensor_scan(flat(incl), ones[:], flat(cnt), 0.0, ALU.mult, ALU.add))
            st.then(V.tensor_tensor(excl[:], incl[:], cnt[:], ALU.subtract))
            tot, ntl, ti, tb, base = (et[:, k, :] for k in range(5))
            st.then(V.tensor_tensor(tot, incl[:, :, TT - 1], excl[:, :, 0], ALU.subtract))
            st.then(V.tensor_tensor(cnt[:], tot[:, :, None].to_broadcast([P, E, TT]),
                                    thr[:, None, :].to_broadcast([P, E, TT]), ALU.is_gt))
            st.then(V.tensor_reduce(ntl, cnt[:], AX, ALU.add))
            st.then(V.tensor_tensor_scan(ti, ones[:, 0:E], ntl, 0.0, ALU.mult, ALU.add))
            st.then(V.tensor_tensor(tb, ti, ntl, ALU.subtract))
            st.then(V.scalar_tensor_tensor(base, tb, float(P), excl[:, :, 0], ALU.mult, ALU.subtract))
            st.then(V.tensor_tensor(excl[:], excl[:], base[:, :, None].to_broadcast([P, E, TT]), ALU.add))
            pre = att[0][:, 0:P].rearrange("p (t e) -> p t e", e=E)
            st.then(V.tensor_tensor(key[:], excl[:].rearrange("p e t -> p t e"), pre, ALU.add))
            st.then(V.tensor_tensor(key[:], key[:], oh[:], ALU.mult))
            st.then(V.tensor_reduce(pos[:], key[:], AX, ALU.add))
            V.tensor_copy(pos_i[:], pos[:]).then_inc(pos_ready, 1)
            tcmp = key[0:1, :, :].rearrange("p t e -> p (t e)")
            tiles = wide[0:1, 0:SLOT_TILES * E].rearrange("p (t e) -> p t e", e=E)
            st.then(V.tensor_tensor(tiles, tidx[:, :, None].to_broadcast([1, SLOT_TILES, E]),
                                    ti[0:1, None, :].to_broadcast([1, SLOT_TILES, E]), ALU.is_ge))
            st.then(V.tensor_reduce(te[:], tiles, AX, ALU.add))
            V.tensor_scalar(te_i[:], te[:], float(E - 1), None, ALU.min).then_inc(te_ready, 1)
            dve.wait_ge(st_done, 1)
            V.tensor_copy(score_t[:], misc[0:TT, 256:256 + P]).then_inc(st_copied, 1)
            st.then(V.memset(qq[:, 0:2, :, :, :], 0.0))
            st.mark(V.memset(qq[:, 1, :, 0, 0:1], 1.0))
            st.mark(V.memset(qq[:, 0, :, 0, 1:2], 1.0))
            st.mark(V.memset(neg_pos[:, 0:1], -GROUP_SCALE))
            st.mark(V.memset(neg_pos[:, 1:2], GROUP_SCALE))
            st.then(V.tensor_scalar(wof[:], wof[:], scale3[:, 0:1], None, ALU.mult))
            dve.wait_ge(s_sc_in, 16)
            for i in range(TT):
                b = i // NT
                st.then(V.tensor_scalar(junk, wide[:, N * b:N * b + N], score[:, i:i + 1], None,
                                        ALU.is_gt, ALU.add, accum_out=pos[:, i:i + 1]))
            V.tensor_scalar(mask[:], pos[:], float(KEEP), None, ALU.is_lt).then_inc(mask_ready, 1)
            st.then(V.memset(f3, 0.0))
            V.memset(f3[0:3, :], 1.0).then_inc(f3_ones, 1)
            dve.wait_ge(mt_done, 1)
            V.tensor_copy(mask_t[:], misc[0:TT, 384:384 + P]).then_inc(mt_copied, 1)

            def copy_hidden(i, slot):
                dve.wait_ge(ht_done, i + 1)
                V.tensor_copy(hT[slot][:, 0:4, :], att[0][:].rearrange("p (c n) -> p c n", n=P)).then_inc(ht_copied, 1)
                V.tensor_copy(hT[slot][:, 4:6, :],
                              att[1][:, 0:2 * P].rearrange("p (c n) -> p c n", n=P)).then_inc(ht_copied, 1)

            def copy_out(i, slot):
                dve.wait_ge(dn_done, i + 1)
                dve.wait_ge(weight_copied, i + 1)
                V.tensor_scalar(ys[slot], att[2][:, 0:D], weight[slot][:, 0:1], None, ALU.mult
                                ).then_inc(ys_copied, 1)
                dve.wait_ge(ys_copied, i + 1)
                V.tensor_tensor_reduce(junk[:, 0:D], ys[slot], wvrow[:], 1.0, 0.0, ALU.mult, ALU.add,
                                       v_col[slot][:]).then_inc(vc_ready, 1)

            def copy_meta(slot, loads, stored):
                dve.wait_ge(s_xs[slot], 16 * loads)
                ahead(dve, s_ys[slot], 32 * stored)
                V.tensor_copy(target[slot][:], xs[slot][:, D + 1:D + 2]).then_inc(target_copied, 1)
                V.tensor_copy(weight[slot][:], xs[slot][:, D:D + 1]).then_inc(weight_copied, 1)

            def copy_pair(i):
                copy_hidden(2 * i, 0)
                copy_out(2 * i, 0)
                copy_meta(1, i + 1, i)
                copy_hidden(2 * i + 1, 1)
                copy_out(2 * i + 1, 1)
                copy_meta(0, i + 2, i + 1)

            copy_meta(0, 1, 0)
            copy_pair(0)
            with dve.Fori(1, TILE_PAIRS) as i:
                copy_pair(i)
            copy_hidden(SLOT_TILES - 1, 0)
            copy_out(SLOT_TILES - 1, 0)

            dve.wait_ge(s_lane, 16 * 2)
            half = B * CH
            st.mark(V.tensor_scalar(v2[0:half, :], v2[0:half, :], bvcol[0:half, 0:1], -V_MAX, ALU.add, ALU.max))
            st.then(V.tensor_scalar(v2[half:P, :], v_raw[half:P, ::-1], bvcol[half:P, 0:1], -V_MAX,
                                    ALU.add, ALU.max))
            by_group = v2[:].rearrange("p (g l) -> p g l", g=GR)
            st.mark(V.tensor_scalar(vv[:, :, :, 0], by_group, V_MAX, -1.0, ALU.min, ALU.mult))
            st.then(V.tensor_scalar(vv[:, :, :, 1], by_group, V_MAX, None, ALU.min))
            for l in range(SL):
                new, one, two = qq[:, l + 2, :, :, :], qq[:, l + 1, :, :, :], qq[:, l, :, :, :]
                st.mark(V.tensor_tensor(new, one, two, ALU.add))
                st.then(V.tensor_tensor(qv[:], one[:, :, ::-1, :],
                                        vv[:, :, l, :, None].to_broadcast([P, GR, 2, 2]), ALU.mult))
                st.then(V.tensor_tensor(new, new, qv[:], ALU.add))
            gm6 = gm[:].rearrange("p g (k c) (s d) -> p g k c s d", c=2, d=2)
            signs = neg_pos[:, None, :, None].to_broadcast([P, GR, 2, 2])
            for k in range(2):
                src = qq[:, SL + 1 - k, :, :, :]
                st.mark(V.tensor_scalar(gm6[:, :, k, :, :, 0], src, GROUP_SCALE, None, ALU.mult))
                st.mark(V.tensor_tensor(gm6[:, :, k, :, :, 1], src[:, :, ::-1, :], signs, ALU.mult))
            st.settle()

            def times(dst, later, earlier):
                st.then(V.tensor_tensor(gp[:], later[:, :, None, :].to_broadcast([P, 4, 4, 4]),
                                        earlier.rearrange("p k j -> p j k")[:, None, :, :]
                                        .to_broadcast([P, 4, 4, 4]), ALU.mult))
                return V.tensor_reduce(dst, gp[:], AX, ALU.add)

            for g in range(1, GR):
                st.then(times(gm[:, g, :, :], gm[:, g, :, :], gm[:, g - 1, :, :]))
            whole = gm[:, GR - 1, :, :]
            st.then(V.tensor_tensor_reduce(size[:, 0:2], whole[:, 0, 0:2], whole[:, 0, 0:2], 1.0, 0.0,
                                           ALU.mult, ALU.add, size[:, 2:3]))
            st.then(V.tensor_scalar(size[:, 3:4].bitcast(I32), size[:, 2:3].bitcast(I32), -0.5, MAGIC,
                                    ALU.mult, ALU.add))
            V.tensor_scalar(lm[0][:], whole, size[:, 3:4], None, ALU.mult).then_inc(lm_ready, 1)
            for i in range(LEVELS):
                dve.wait_ge(lm_ready, i + 1)
                dve.wait_ge(lm_shifted, i + 1)
                shifted = misc[:, 16 * i:16 * i + 16].rearrange("p (k j) -> p k j", j=4)
                times(lm[(i + 1) % 2][:], lm[i % 2][:], shifted).then_inc(lm_ready, 1)
            dve.wait_ge(start_done, 1)
            lane_start = misc[:, 64:68]
            st.mark(V.tensor_copy(start[:, 0, :, :].rearrange("p s c -> p (s c)"), lane_start))
            st.then(V.tensor_tensor(gp[:, 0:GR - 1, :, :], gm[:, 0:GR - 1, :, :],
                                    lane_start[:, None, None, :].to_broadcast([P, GR - 1, 4, 4]), ALU.mult))
            st.then(V.tensor_reduce(start[:, 1:GR, :, :].rearrange("p g s c -> p g (s c)"),
                                    gp[:, 0:GR - 1, :, :], AX, ALU.add))
            st.mark(V.tensor_copy(sw[:, 0, :, 0, :], start[:, :, :, 0]))
            st.mark(V.tensor_scalar(sw[:, 0, :, 1, :], start[:, :, :, 1], -1.0, None, ALU.mult))
            st.mark(V.tensor_copy(sw[:, 1, :, 0, :], start[:, :, :, 1]))
            st.then(V.tensor_copy(sw[:, 1, :, 1, :], start[:, :, :, 0]))
            basis = qq[:, 1:SL + 2, :, :, :].rearrange("p l g c s -> p l (g c s)")
            for k in range(2):
                st.mark(V.tensor_tensor(xp[:, k, :, :, :].rearrange("p l g c -> p l (g c)"), basis,
                                        sw[:, k, :, :, :].rearrange("p g c s -> p (g c s)")[:, None, :]
                                        .to_broadcast([P, SL + 1, GR * 4]), ALU.mult))
            st.settle()
            st.then(V.tensor_reduce(xx[:].rearrange("p k l g -> p (k l g)"),
                                    xp[:].rearrange("p k l g c -> p (k l g) c"), AX, ALU.add))
            new, old = xx[:, :, 1:SL + 1, :], xx[:, :, 0:SL, :]
            st.mark(V.tensor_tensor(fb[:, 0:2, :, :], new[:, ::-1, :, :], old, ALU.mult))
            st.mark(V.tensor_tensor(fb[:, 2:4, :, :], new, old, ALU.mult))
            st.then(V.tensor_tensor(fb[:, 4:6, :, :], old, old, ALU.mult))
            st.mark(V.tensor_tensor(fb[:, 4, :, :], fb[:, 4, :, :], fb[:, 5, :, :], ALU.add))
            st.mark(V.tensor_tensor(fb[:, 0, :, :], fb[:, 0, :, :], fb[:, 1, :, :], ALU.subtract))
            st.then(V.tensor_tensor(fb[:, 2, :, :], fb[:, 2, :, :], fb[:, 3, :, :], ALU.add))
            st.then(V.reciprocal(fb[:, 5, :, :], fb[:, 4, :, :]))
            st.mark(V.tensor_tensor(fa[:, 0, :, :], fb[:, 0, :, :], fb[:, 5, :, :], ALU.mult))
            V.scalar_tensor_tensor(fa[:, 1, :, :], fb[:, 2, :, :], -1.0, fb[:, 5, :, :], ALU.mult, ALU.mult
                                   ).then_inc(frac_ready, 1)
            dve.wait_ge(flip_done, 1)
            dve.wait_ge(s_mask, 16)
            flipped = misc[0:half, P:P + 2 * LCH].rearrange("p (k l g) -> p k l g", k=2, g=GR)
            cc = fb[0:half, 0:2, :, :]
            st.then(V.tensor_tensor(cc, fa[0:half, :, :, :], flipped[:, :, ::-1, ::-1], ALU.add))
            by_step = lambda ap: ap.rearrange("p g l -> p l g")
            st.mark(V.tensor_tensor(cc[:, 0, :, :], cc[:, 0, :, :], by_step(vv[0:half, :, :, 1]), ALU.subtract))
            st.then(V.tensor_scalar(cc[:, 1, :, :], cc[:, 1, :, :], 1.0, None, ALU.add))
            sq = fb[0:half, 2:4, :, :]
            den, rec = fb[0:half, 4, :, :], fb[0:half, 5, :, :]
            st.then(V.tensor_tensor(sq, cc, cc, ALU.mult))
            st.then(V.tensor_tensor(den, sq[:, 0, :, :], sq[:, 1, :, :], ALU.add))
            st.then(V.reciprocal(rec, den))
            gg4 = gg[:].rearrange("p k (g l) -> p k g l", g=GR)
            st.mark(V.tensor_tensor(gg4[:, 0, :, :], cc[:, 0, :, :].rearrange("p l g -> p g l"),
                                    rec.rearrange("p l g -> p g l"), ALU.mult))
            st.then(V.scalar_tensor_tensor(gg4[:, 1, :, :], cc[:, 1, :, :].rearrange("p l g -> p g l"), -1.0,
                                           rec.rearrange("p l g -> p g l"), ALU.mult, ALU.mult))
            st.then(V.tensor_tensor(gg[:], gg[:], mask_l[:, None, :].to_broadcast([half, 2, LCH]), ALU.mult))
            V.tensor_scalar(gg[:], gg[:], CLAMP, -CLAMP, ALU.min, ALU.max).then_inc(feat_ready, 1)
            for b in range(B):
                dve.wait_ge(ft_done, b + 1)
                dve.wait_ge(h_added, b + 1)
                hb = h_all[:, NT * b:NT * b + NT, :]
                V.tensor_tensor(hb, hb, ring4[b % 2][:, :, 0:D], ALU.add).then_inc(out_ready, 1)

        @block.tensor
        def _(pe):
            def front(b):
                pe.wait_ge(conv_done, b + 1)
                if b > 0:
                    pe.wait_ge(gh_copied, b)
                    pe.wait_ge(y_done, b)
                if b > 1:
                    pe.wait_ge(attn_added, b - 1)
                for o in range(2):
                    for half in range(2):
                        for c in range(2):
                            last = nc.tensor.matmul(ring[o][0:DC, half, :], wpw[:, c, DC * o:DC * o + DC],
                                                    conv[:, c, 512 * half:512 * half + 512],
                                                    start=(c == 0), stop=(c == 1))
                    last.then_inc(pw_done, 1)
                pe.wait_ge(pool_done, 2 * b + 2)
                for i in range(NT):
                    for c in range(2):
                        last = nc.tensor.matmul(ring4[0][:, i, 0:D], pooled[:, c, P * i:P * i + P],
                                                dft_c[:, c, :], start=(c == 0), stop=(c == 1))
                last.then_inc(col_done, 1)
                pe.wait_ge(gh_copied, b + 1)
                for k in range(NT):
                    for table, dst, src in ((cos_n, slice(0, NC), slice(0, NC)),
                                            (sin_n, slice(P, P + NS), slice(NC, D))):
                        for i in range(NT):
                            last = nc.tensor.matmul(ring4[1][:, k, dst], table[:, i, P * k:P * k + P],
                                                    gh[:, i, src], start=(i == 0), stop=(i == NT - 1))
                last.then_inc(row_done, 1)

            def project(b):
                pe.wait_ge(xn_ready, b + 1)
                if b > 0:
                    pe.wait_ge(sq_done, 24 * b)
                for c in range(2):
                    for i in range(NT):
                        last = nc.tensor.transpose(ring[0][0:DC, c, P * i:P * i + P],
                                                   xn[:, i, DC * c:DC * c + DC], ident[:])
                last.then_inc(xt_done, 1)
                if b == 0:
                    pe.wait_ge(y_done, 2)
                pe.wait_ge(xt_copied, b + 1)
                for r, w, s in ((1, wq, q_done), (0, wk, k_done)):
                    for o in range(2):
                        for c in range(2):
                            last = nc.tensor.matmul(ring[r][0:DC, o, :], w[:, c, DC * o:DC * o + DC],
                                                    xnT[0:DC, c, :], start=(c == 0), stop=(c == 1))
                    last.then_inc(s, 1)
                pe.wait_ge(q_rest, b + 1)
                for i in range(NT):
                    for c in range(2):
                        last = nc.tensor.matmul(ring4[1][:, i, 0:D], xnT[0:DC, c, P * i:P * i + P],
                                                wv[:, c, :], start=(c == 0), stop=(c == 1))
                last.then_inc(v_done, 1)
                pe.wait_ge(v_copied, b + 1)
                for g in range(HG):
                    for j in range(NT - 1):
                        last = nc.tensor.matmul(misc[:, NT * g:NT * g + NT],
                                                va[:, j, 4 * g:4 * g + 4, :].rearrange("p h d -> p (h d)"),
                                                steps[:, j, :], start=(j == 0), stop=(j == NT - 2))
                last.then_inc(pre_done, 1)

            def attend(b):
                pe.wait_ge(s_stack, 16 * 6 * (b + 1))
                pe.wait_ge(pre_copied, b + 1)
                if b == 0:
                    pe.wait_ge(k_rest, 1)
                    pe.wait_ge(v_copied, 1)
                elif b < B - 1:
                    pe.wait_ge(y_done, b + 2)
                else:
                    pe.wait_ge(attn_added, B - 1)
                if b > 0:
                    pe.wait_ge(ot_copied, 12 * b)

                def scores(n):
                    j, pr = divmod(n, PAIRS)
                    if n >= 2:
                        pe.wait_ge(sq_done, 24 * b + n - 1)
                    for h in (2 * pr, 2 * pr + 1):
                        last = nc.tensor.matmul(ring[n % 2][:, h % 2, 0:N - P * j],
                                                k_stack[:, h, P * j:P * j + P], q_stack[:, h, P * j:N],
                                                start=True, stop=True)
                    last.then_inc(s_done, 1)

                def values(n):
                    j, pr = divmod(n, PAIRS)
                    g = pr // 2
                    for m in (n, n + 1):
                        pe.wait_ge(p_ready, 24 * b + m + 1)
                        for h in range(2):
                            q = 2 * (m - n) + h
                            last = nc.tensor.matmul(att[g][QUAD * q:QUAD * q + QUAD, P * j:N],
                                                    va[:, j, 4 * g + q, :], prob[:, m % 4, h, 0:N - P * j],
                                                    start=(j == 0), stop=False)
                        last.then_inc(av_done, 1)
                    last = nc.tensor.matmul(att[g][:, P * j:P * j + P],
                                            va[:, j, 4 * g:4 * g + 4, :].rearrange("p h d -> p (h d)"),
                                            tri[:], start=False, stop=(j == NT - 1))
                    if j == NT - 1:
                        last.then_inc(ot_done, 1)

                for n in range(24):
                    scores(n)
                    if n % 2 and n >= 3:
                        values(n - 3)
                values(22)

            def finish(b):
                for g in range(HG):
                    pe.wait_ge(ot_copied, 12 * b + NT * (g + 1))
                    if g == 0:
                        pe.wait_ge(pre_copied, min(b + 2, B))
                    for i in range(NT):
                        at = 64 + 4 * (NT * g + i)
                        last = nc.tensor.matmul(misc[:, at:at + 4], oT[:, g, P * i:P * i + P], pick[:],
                                                start=True, stop=True)
                last.then_inc(den_done, 1)
                pe.wait_ge(rden_ready, b + 1)
                if b + 1 < B:
                    pe.wait_ge(k_rest, b + 2)
                    pe.wait_ge(v_copied, b + 2)
                else:
                    pe.wait_ge(sq_done, 24 * B)
                for g in range(HG):
                    for i in range(NT):
                        last = nc.tensor.matmul(ring[g // 2][:, g % 2, P * i:P * i + P],
                                                rden_wide[:, NT * g + i, :, :].rearrange("p h c -> p (h c)"),
                                                ident[:], start=True, stop=True)
                    last.then_inc(den_spread, 1)
                pe.wait_ge(o_ready, 3 * b + 3)
                for i in range(NT):
                    for g in range(HG):
                        last = nc.tensor.matmul(ring4[0][:, i, 0:D], oT[:, g, P * i:P * i + P], wo[:, g, :],
                                                start=(g == 0), stop=(g == HG - 1))
                last.then_inc(wo_done, 1)

            pe.wait_ge(s_wf, 16 * len(FRONT))
            front(0)
            front(1)
            pe.wait_ge(s_wa, 16 * len(ATTN))
            pe.wait_ge(s_wo, 16 * 4)
            project(0)
            attend(0)
            project(1)
            finish(0)
            for b in range(1, B):
                if b + 1 < B:
                    front(b + 1)
                attend(b)
                if b + 1 < B:
                    project(b + 1)
                finish(b)

            pe.wait_ge(s_wm, 16 * len(MOE))
            pe.wait_ge(ones_rows, 4)

            def turn(b):
                pe.wait_ge(x2_ready, b + 1)
                if b == 0:
                    pe.wait_ge(attn_added, B)
                if b >= 2:
                    pe.wait_ge(t2_copied, b - 1)
                for c in range(2):
                    for i in range(NT):
                        last = nc.tensor.transpose(ring[b % 2][0:DC, c, P * i:P * i + P],
                                                   x2_all[:, NT * b + i, DC * c:DC * c + DC], ident[:])
                last.then_inc(t2_done, 1)

            turn(0)
            for b in range(B):
                if b + 1 < B:
                    turn(b + 1)
                pe.wait_ge(t2_copied, b + 1)
                for i in range(NT):
                    at = 16 * (NT * b + i)
                    for c in range(2):
                        last = nc.tensor.matmul(misc[:, at:at + E + 1],
                                                (xnT, x2T)[b % 2][0:DC + c, c, P * i:P * i + P],
                                                wgm[0:DC + c, c, :], start=(c == 0), stop=(c == 1))
                last.then_inc(lg_done, 1)
            pe.wait_ge(oh_ready, 1)
            ohf = oh[:].rearrange("p t e -> p (t e)")
            nc.tensor.matmul(att[0][:, 0:P], tri_strict[:], ohf, start=True, stop=True)
            nc.tensor.matmul(att[1][:, 0:P], ones[:], ohf, start=True, stop=True).then_inc(cnt_done, 1)
            pe.wait_ge(sc_ready, 1)
            nc.tensor.transpose(misc[0:TT, 256:256 + P], score[:], ident[:]).then_inc(st_done, 1)
            pe.wait_ge(mask_ready, 1)
            nc.tensor.transpose(misc[0:TT, 384:384 + P], mask[:], ident[:]).then_inc(mt_done, 1)

            def turn_slots(i, slot, loads):
                pe.wait_ge(s_xs[slot], 16 * loads)
                ahead(pe, xst_copied, i)
                for c in range(2):
                    last = nc.tensor.transpose(misc[0:DC, P * c:P * c + P], xs[slot][:, DC * c:DC * c + DC],
                                               ident[:])
                last.then_inc(xst_done, 1)

            def up(i, slot):
                e = pe.value_load(te_i[0:1, bass.ds(i, 1)], min_val=0, max_val=E - 1)
                pe.wait_ge(xst_copied, i + 1)
                ahead(pe, gelu_done, i - 1)
                for half in range(2):
                    for c, w in ((0, w1a), (1, w1b)):
                        last = nc.tensor.matmul(ring[slot][:, half, 0:HID // 2], xsT[slot][0:DC + c, c, :],
                                                w[0:DC + c, bass.ds(e * HID + half * (HID // 2), HID // 2)],
                                                start=(c == 0), stop=(c == 1))
                last.then_inc(up_done, 1)

            def turn_hidden(i, slot):
                pe.wait_ge(gelu_done, i + 1)
                ahead(pe, ht_copied, 2 * i)
                for c in range(HC):
                    last = nc.tensor.transpose(att[c // 4][:, P * (c % 4):P * (c % 4) + P],
                                               hg[slot][:, P * c:P * c + P], ident[:])
                last.then_inc(ht_done, 1)

            def down(i, slot):
                e = pe.value_load(te_i[0:1, bass.ds(i, 1)], min_val=0, max_val=E - 1)
                pe.wait_ge(ht_copied, 2 * i + 2)
                ahead(pe, ys_copied, i)
                for c in range(HC):
                    nc.tensor.matmul(att[2][:, 0:D], hT[slot][:, c, :], w2[:, bass.ds((e * HC + c) * D, D)],
                                     start=(c == 0), stop=False)
                nc.tensor.matmul(att[2][:, 0:D], ones[0:1, :], b2[0:1, bass.ds(e * D, D)],
                                 start=False, stop=True).then_inc(dn_done, 1)

            pe.wait_ge(te_ready, 1)
            pe.wait_ge(st_copied, 1)
            pe.wait_ge(s_w1a, 16)
            pe.wait_ge(s_w1b, 16)
            pe.wait_ge(s_w2, 32)

            def expert_pair(i):
                turn_slots(2 * i + 1, 1, i + 1)
                turn_hidden(2 * i, 0)
                up(2 * i + 1, 1)
                down(2 * i, 0)
                turn_slots(2 * i + 2, 0, i + 2)
                turn_hidden(2 * i + 1, 1)
                up(2 * i + 2, 0)
                down(2 * i + 1, 1)

            turn_slots(0, 0, 1)
            up(0, 0)
            expert_pair(0)
            with pe.Fori(1, TILE_PAIRS) as i:
                expert_pair(i)
            turn_hidden(SLOT_TILES - 1, 0)
            down(SLOT_TILES - 1, 0)

            pe.wait_ge(s_scan, 16)
            for i in range(LEVELS):
                pe.wait_ge(lm_ready, i + 1)
                at = misc[:, 16 * i:16 * i + 16]
                nc.tensor.matmul(at, shift[i], lm[i % 2][:].rearrange("p i j -> p (i j)"), start=True, stop=False)
                nc.tensor.matmul(at, ident[:], unit[i], start=False, stop=True).then_inc(lm_shifted, 1)
            pe.wait_ge(lm_ready, LEVELS + 1)
            nc.tensor.matmul(misc[:, 64:68], shift[0], lm[LEVELS % 2][:, :, 0], start=True, stop=False)
            nc.tensor.matmul(misc[:, 64:68], ident[:], unit[0][:, 0:16:4], start=False, stop=True
                             ).then_inc(start_done, 1)
            pe.wait_ge(frac_ready, 1)
            nc.tensor.matmul(misc[0:B * CH, P:P + 2 * LCH], flip, fa[:].rearrange("p k l g -> p (k l g)"),
                             start=True, stop=True).then_inc(flip_done, 1)
            pe.wait_ge(s_f3, 32)
            for b in range(B):
                if b >= 2:
                    pe.wait_ge(out_ready, b - 1)
                for i in range(NT):
                    last = nc.tensor.matmul(ring4[b % 2][:, i, 0:D],
                                            f3[:, N * b + P * i:N * b + P * i + P], wof[:],
                                            start=True, stop=True)
                last.then_inc(ft_done, 1)


def layouts(inp, np):
    a = {k: np.asarray(v) for k, v in inp.items()}

    def chunked(w):
        return np.ascontiguousarray(w.reshape(2, DC, -1).transpose(1, 0, 2))

    o = {}
    o["x"] = np.ascontiguousarray(a["x"].reshape(B, S, 2, DC).transpose(0, 3, 2, 1))
    o["w_dw"] = chunked(a["L0_tok_w_dw"][:, 0, :])
    o["vec2"] = np.ascontiguousarray(np.stack([a["L0_tok_b_dw"].reshape(2, DC).T, a["L0_tok_b_pw"].reshape(2, DC).T], 1))
    o["w_pw"] = chunked(a["L0_tok_w_pw"][:, :, 0].T)
    o["gamma"] = np.ascontiguousarray(np.broadcast_to(a["L0_tok_gamma"], (P, D)))
    o["beta"] = np.ascontiguousarray(np.broadcast_to(a["L0_tok_beta"], (P, D)))
    o["wq"] = chunked(a["L0_attn_Wq"].T)
    o["wk"] = chunked(a["L0_attn_Wk"].T)
    o["wv"] = chunked(a["L0_attn_Wv"].T)
    o["wo"] = np.ascontiguousarray(a["L0_attn_Wo"].T.reshape(HG, 4, HD, D).transpose(1, 2, 0, 3))
    f = np.float32
    n = np.arange(N)
    ang = 2 * np.pi * ((n[:, None] * n[None, :]) % N) / N
    o["cos_n"] = np.ascontiguousarray(np.cos(ang).astype(f).reshape(NT, P, N).transpose(1, 0, 2))
    o["sin_n"] = np.ascontiguousarray(np.sin(ang).astype(f).reshape(NT, P, N).transpose(1, 0, 2))
    d = np.arange(D)
    ang = 2 * np.pi * ((d[:, None] * d[None, :]) % D) / D
    o["dft_c"] = chunked(np.concatenate([np.cos(ang[:, :NC]), np.sin(ang[:, 1:NC - 1])], 1).astype(f))
    p = np.arange(P)
    o["ident"] = np.eye(P, dtype=f)
    o["tri"] = (p[:, None] <= p[None, :]).astype(f)
    o["tri_strict"] = (p[:, None] < p[None, :]).astype(f)
    o["pick"] = (p[:, None] == np.arange(4)[None, :] * QUAD + HD).astype(f)
    o["steps"] = np.broadcast_to((np.arange(NT)[None, :] > np.arange(NT - 1)[:, None]).astype(f), (P, NT - 1, NT)).copy()
    o["ones"] = np.ones((P, P), f)
    o["epscol"] = np.where(p % QUAD == HD, f(EPS_ATTN), f(0)).astype(f)[:, None]
    o["rev"] = np.broadcast_to(np.arange(E, 0, -1).astype(f), (P, E)).copy()
    o["thr"] = np.broadcast_to((P * np.arange(TT)).astype(f), (P, TT)).copy()
    o["tidx"] = np.arange(SLOT_TILES).astype(f)[None, :]
    o["empty_row"] = np.zeros((P, ROW), f)
    o["empty_row"][:, D + 1] = B * N + p
    o["token_row"] = (P * np.arange(TT)[None, :] + p[:, None]).astype(f)
    shifts = [((p[:, None] + 2 ** i == p[None, :]) & (p[None, :] % CH >= 2 ** i)).astype(f) for i in range(LEVELS)]
    units = [np.where(p[:, None] % CH < 2 ** i, np.eye(4).reshape(1, 16), 0).astype(f) for i in range(LEVELS)]
    m = np.arange(B * CH)
    turned = B * CH + m // CH * CH + CH - 1 - m % CH
    o["scan_tab"] = np.concatenate(shifts + units + [(p[:, None] == turned[None, :]).astype(f)], 1)
    wgm = np.zeros((DC + 1, 2, E + 1), f)
    wgm[:DC, :, :E] = chunked(a["L0_ffn_Wg"])
    wgm[:DC, :, E] = a["L0_ffn_Wm"].reshape(2, DC).T
    wgm[DC, 1, :E] = a["L0_ffn_bg"]
    wgm[DC, 1, E] = a["L0_ffn_bm"]
    o["wgm"] = wgm
    w1 = a["L0_ffn_W1"].reshape(E, 2, DC, HID).transpose(1, 2, 0, 3).reshape(2, DC, E * HID)
    o["w1a"] = np.ascontiguousarray(w1[0])
    o["w1b"] = np.concatenate([w1[1], a["L0_ffn_b1"].reshape(1, E * HID)], 0)
    o["w2"] = np.ascontiguousarray(a["L0_ffn_W2"].reshape(E, HC, P, D).transpose(2, 0, 1, 3).reshape(P, -1))
    o["b2"] = np.ascontiguousarray(a["L0_ffn_b2"].reshape(1, -1))
    o["wvrow"] = np.ascontiguousarray(np.broadcast_to(a["L0_ffn_Wv"], (P, D)))
    o["bvcol"] = np.ascontiguousarray(np.broadcast_to(a["L0_ffn_bv"], (P, 1)))
    o["wof"] = np.concatenate([a["L0_ffn_Wo"], a["L0_ffn_bo"][None, :], np.zeros((DC - 3, D), f)], 0)
    o["scale3"] = np.ascontiguousarray(np.broadcast_to(a["L0_ffn_bk_scale"], (DC, 1)))
    return o


def kernel(**inputs):
    import numpy as np
    import concourse.bacc as bacc
    from concourse.bass_utils import run_bass_kernel_spmd as run

    nc = bacc.Bacc("TRN2", target_bir_lowering=False, num_devices=1)
    arrays, t = {}, {}
    for name, a in layouts(inputs, np).items():
        arrays[f"in_{name}"] = a
        t[name] = nc.dram_tensor(f"in_{name}", a.shape, mybir.dt.from_np(a.dtype), kind="ExternalInput").ap()
    t["out"] = nc.dram_tensor("out_0", (B * N, D), F32, kind="ExternalOutput").ap()
    build(nc, t)
    r = run(nc, [arrays], core_ids=[0])
    return r.results[0]["out_0"].reshape(B, N, D)
```

```python
from contextlib import ExitStack

import concourse.bass as bass
from concourse import mybir

P = 128
F32 = mybir.dt.float32
I32 = mybir.dt.int32
BF16 = mybir.dt.bfloat16
ALU = mybir.AluOpType
ACT = mybir.ActivationFunctionType
AX = mybir.AxisListType.X

B, S, D = 4, 1024, 192
DC = D // 2
TAPS = 7
HALO = TAPS // 2
N = S // 2
NT = N // P
TT = B * NT
NC = D // 2 + 1
NS = D // 2 - 1
HEADS, HD = 12, 16
QUAD = 32
HG = HEADS // 4
PARTS = 3
Q_PART = (0, 0, 0, 1, 1, 1, 2, 2)
K_PART = (0, 1, 2, 0, 1, 2, 0, 1)
PAIRS = HEADS // 2
E, HID = 8, 768
HC = HID // P
SLOT_TILES = TT + E - 1
KEEP = int(N * (1.0 - 0.6))
LCH = 32
CH = N // LCH
GR = 4
SL = LCH // GR
LEVELS = CH.bit_length() - 1
GROUP_SCALE = 2.0 ** -7
ROW = D + 2
EPS_LN = 1e-5
EPS_ATTN = 2e-12
V_MAX, CLAMP = 3.0, 10.0
MAGIC = float(0x5F3759DF)
RSQRT_ROUNDS = 3


class Steps:

    def __init__(self, eng, sem):
        self.eng, self.sem, self.count = eng, sem, 0

    def mark(self, ins):
        ins.then_inc(self.sem, 1)
        self.count += 1
        return ins

    def settle(self, but=0):
        self.eng.wait_ge(self.sem, self.count - but)

    def then(self, ins):
        self.mark(ins)
        self.settle()


def ahead(eng, sem, value):
    if not (isinstance(value, int) and value <= 0):
        eng.wait_ge(sem, value)


def build(nc, t):
    with ExitStack() as ctx:
        def sb(name, shape, dt=F32):
            return ctx.enter_context(nc.sbuf_tensor(name, shape, dt))

        def sem(name):
            return ctx.enter_context(nc.semaphore(name))

        ring = [ctx.enter_context(nc.psum_tensor(f"ring{i}", [P, 2, 512], F32)) for i in range(2)]
        att = [ctx.enter_context(nc.psum_tensor(f"att{i}", [P, 512], F32)) for i in range(HG)]
        misc = ctx.enter_context(nc.psum_tensor("misc", [P, 512], F32))
        ring4 = [r[:, :, :].rearrange("p a (b n) -> p (a b) n", b=2) for r in ring]

        wdw = sb("wdw", [DC, 2, TAPS])
        vec2 = sb("vec2", [DC, 2, 2])
        wpw = sb("wpw", [DC, 2, D])
        dft_c = sb("dft_c", [DC, 2, D])
        gamma = sb("gamma", [P, D])
        beta = sb("beta", [P, D])
        wq = sb("wq", [DC, 2, D])
        wk = sb("wk", [DC, 2, D])
        wv = sb("wv", [DC, 2, D])
        wo = sb("wo", [P, HG, D])
        ident = sb("ident", [P, P])
        tri = sb("tri", [P, P])
        tri_strict = sb("tri_strict", [P, P])
        pick = sb("pick", [P, 4])
        steps = sb("steps", [P, NT - 1, NT])
        ones = sb("ones", [P, P])
        epscol = sb("epscol", [P, 1])
        rev = sb("rev", [P, E])
        thr = sb("thr", [P, TT])
        tidx = sb("tidx", [1, SLOT_TILES + 1])
        wgm = sb("wgm", [DC + 1, 2, E + 1])
        w1a = sb("w1a", [DC, E * HID])
        w2 = sb("w2", [P, E * HC * D])
        cos_n = w2[:, 0:NT * N].rearrange("p (i n) -> p i n", n=N)
        sin_n = w2[:, NT * N:2 * NT * N].rearrange("p (i n) -> p i n", n=N)
        at = 2 * NT * N
        xin = w2[0:DC, at:at + 2 * (S + 2 * HALO)].rearrange("p (c n) -> p c n", c=2)
        at += 2 * (S + 2 * HALO)
        assert at <= E * HC * D
        w1b_area = sb("w1b", [P, E * HID])
        w1b = w1b_area[0:DC + 1, :]
        stacks = w1b_area[:].bitcast(BF16).rearrange("p (s h n) -> p s h n", s=2, h=HEADS)
        q_stack, k_stack = stacks[:, 0, :, :], stacks[:, 1, :, :]
        idle = sb("idle", [P, 2 * P], BF16)
        wvrow = sb("wvrow", [P, D])
        bvcol = sb("bvcol", [P, 1])
        wof = sb("wof", [DC, D])
        scale3 = sb("scale3", [DC, 1])

        wide = sb("wide", [P, 2 * S])
        conv = wide[0:DC, :].rearrange("p (c n) -> p c n", c=2)
        pooled = sb("pooled", [DC, 2, N])
        gh = sb("gh", [P, NT, D])
        y = sb("y", [P, NT, D])
        taps = y[:].rearrange("p t d -> p (t d)")[0:DC, 0:TAPS * DC].rearrange("p (k c) -> p k c", k=TAPS)
        xn = sb("xn", [P, NT, D])
        xnT = sb("xnT", [DC + 1, 2, N])
        x2T = sb("x2T", [DC + 1, 2, N])
        q_area = sb("q_area", [DC + 1, 2 * HID])
        k_area = sb("k_area", [DC + 1, 2 * HID])
        assert PARTS * N <= 2 * HID
        q_parts, k_parts = ([area[0:DC, i * N:i * N + N].bitcast(BF16).rearrange("p (c n) -> p c n", c=2)
                             for i in range(PARTS)] for area in (q_area, k_area))
        rest = x2T[0:DC, :, :]
        va = sb("va", [P, NT, HEADS, QUAD])
        probs = sb("probs", [P, 4 * 2 * N])
        prob = probs[:].rearrange("p (a h n) -> p a h n", a=4, h=2)
        rden_wide = probs[:, 0:HG * NT * P].rearrange("p (g h c) -> p g h c", h=4, c=QUAD)
        pbias = sb("pbias", [P, HG * NT])
        oT = sb("oT", [P, HG, N])
        rden = sb("rden", [P, HG * NT, 4])
        h_all = sb("h_all", [P, TT, D])
        x2_all = sb("x2_all", [P, TT, ROW])
        stats = sb("stats", [P, NT, 6])
        mv = sb("mv", [P, NT, 2])
        nx = sb("nx", [P, NT])
        ny = sb("ny", [P, NT])
        nz = sb("nz", [P, NT])

        lg = sb("lg", [P, TT, E + 1])
        score = sb("score", [P, TT])
        mx = sb("mx", [P, TT])
        ex = sb("ex", [P, TT, E])
        oh = sb("oh", [P, TT, E])
        key = sb("key", [P, TT, E])
        cnt = sb("cnt", [P, E, TT])
        incl = sb("incl", [P, E, TT])
        excl = sb("excl", [P, E, TT])
        et = sb("et", [P, 6, E])
        pos = sb("pos", [P, TT])
        pos_i = sb("pos_i", [P, TT], I32)
        te = sb("te", [1, SLOT_TILES + 1])
        te_i = sb("te_i", [1, SLOT_TILES + 1], I32)
        mask = sb("mask", [P, TT])
        mask_t = sb("mask_t", [TT, P])
        score_t = sb("score_t", [TT, P])
        empty = sb("empty", [P, ROW])
        token_row = sb("token_row", [P, TT])
        xs = [probs[:, ROW * i:ROW * i + ROW] for i in range(2)]
        at = 2 * ROW
        ys = [probs[:, at + D * i:at + D * (1 + i)] for i in range(2)]
        at += 2 * D
        hT = [probs[:, at + HID * i:at + HID * (i + 1)].rearrange("p (c n) -> p c n", n=P)
              for i in range(2)]
        w1_tile = [area[:].rearrange("p (k n) -> p k n", k=2) for area in (q_area, k_area)]
        meta = sb("meta", [P, SLOT_TILES, 2])
        target = [sb(f"target{i}", [P, 1], I32) for i in range(2)]
        v_col = [sb(f"v_col{i}", [P, 1]) for i in range(2)]
        b2 = oT[:].rearrange("p g n -> p (g n)")
        junk2 = gh[:].rearrange("p a b -> p (a b)")[:, 0:N]
        junk = y[:].rearrange("p a b -> p (a b)")[:, 0:N]
        xsT = [sb(f"xsT{i}", [DC + 1, 2, P]) for i in range(2)]
        v2 = sb("v2", [P, LCH])
        v_raw = sb("v_raw", [P, LCH])
        vv = sb("vv", [P, GR, SL, 2])
        neg_pos = sb("neg_pos", [P, 2])
        qq = sb("qq", [P, SL + 2, GR, 2, 2])
        qv = sb("qv", [P, GR, 2, 2])
        gm = sb("gm", [P, GR, 4, 4])
        gp = sb("gp", [P, GR, 4, 4])
        lm = [sb(f"lm{i}", [P, 4, 4]) for i in range(2)]
        size = sb("size", [P, 4])
        start = sb("start", [P, GR, 2, 2])
        sw = sb("sw", [P, 2, GR, 2, 2])
        xp = sb("xp", [P, 2, SL + 1, GR, 4])
        xx = sb("xx", [P, 2, SL + 1, GR])
        fa = sb("fa", [P, 2, SL, GR])
        fb = sb("fb", [P, 6, SL, GR])
        gg = sb("gg", [B * CH, 2, LCH])
        mask_l = sb("mask_l", [B * CH, LCH])
        f3 = wide[0:DC, 0:B * N]
        scan_tab = xn[:].rearrange("p t d -> p (t d)")[:, 0:LEVELS * P + LEVELS * 16 + B * CH]
        shift = [scan_tab[:, P * i:P * i + P] for i in range(LEVELS)]
        unit = [scan_tab[:, LEVELS * P + 16 * i:LEVELS * P + 16 * i + 16] for i in range(LEVELS)]
        flip = scan_tab[:, LEVELS * (P + 16):LEVELS * (P + 16) + B * CH]
        def dram(name, shape, dt=F32):
            return nc.dram_tensor(name, shape, dt, kind="Internal").ap()

        part_dram = [dram(f"{n}_parts", (PARTS, HD, HEADS, N), BF16) for n in "qk"]

        xs_dram = dram("tokens_by_expert", (SLOT_TILES * P, ROW))
        ffn_dram = dram("ffn_by_token", (B * N + P, D))
        v_dram = dram("v_by_token", (B * N + P, 1))
        v_lanes = v_dram[0:B * N, :].rearrange("(b c l) one -> b c (l one)", b=B, l=LCH)
        sc_dram = dram("scores_linear", (B * N,))

        s_x = sem("x_loaded")
        s_wc = sem("conv_weights_loaded")
        s_wf = sem("front_weights_loaded")
        s_wa = sem("attention_weights_loaded")
        s_wo = sem("output_projection_loaded")
        s_wm = sem("moe_weights_loaded")
        s_out = sem("output_stored")
        zeroed, idle_zeroed = sem("buffers_zeroed"), sem("idle_operand_zeroed")
        conv_done = sem("conv_done")
        taps_ready, tap_sums_done, tap_sums_copied = sem("taps_ready"), sem("tap_sums_done"), sem("tap_sums_copied")
        pw_done = sem("pointwise_done")
        pool_done = sem("pooled_done")
        col_done = sem("channel_dft_done")
        gh_copied = sem("gh_copied")
        row_done = sem("token_dft_done")
        a_copied = sem("cosine_part_copied")
        y_done = sem("y_done")
        xn_ready = sem("xn_ready")
        q1_ready, q2_ready, q3_ready = sem("q_part1"), sem("q_part2"), sem("q_part3")
        k1_ready, k2_ready, k3_ready = sem("k_part1"), sem("k_part2"), sem("k_part3")
        q_rest, k_rest = sem("q_rest"), sem("k_rest")
        s_part_out = [sem("q_parts_stored"), sem("k_parts_stored")]
        s_stack = sem("stacks_loaded")
        xt_done = sem("xn_transposed")
        xt_copied = sem("xnT_copied")
        q_done, k_done, v_done = sem("q_done"), sem("k_done"), sem("v_done")
        v_copied = sem("v_copied")
        pre_done = sem("prefix_done")
        pre_copied = sem("prefix_copied")
        s_done = sem("scores_done")
        sq_done = sem("squared")
        p_ready, p_ready_dve = sem("weights_ready"), sem("weights_ready_by_dve")
        av_done = sem("weights_used")
        ot_done = sem("attention_sums_done")
        ot_copied = sem("attention_sums_copied")
        den_done = sem("denominators_by_token")
        rden_ready = sem("reciprocals_ready")
        den_spread = sem("reciprocals_spread")
        o_ready = sem("attention_normalised")
        wo_done = sem("attention_projected")
        attn_added = sem("attention_added")
        x2_ready = sem("x2_ready")
        dve_step, pool_step = sem("dve_step"), sem("pool_step")
        ones_rows = sem("bias_rows_ready")
        t2_done, t2_copied = sem("x2_transposed"), sem("x2T_copied")
        t2_first_copied = sem("x2T_of_batch_0_copied")
        lg_done = sem("logits_done")
        nd_ready, ex_ready, sc_ready = sem("logits_shifted"), sem("exp_ready"), sem("score_ready")
        oh_ready, cnt_done = sem("one_hot_ready"), sem("counts_done")
        pos_ready, te_ready = sem("positions_ready"), sem("tile_experts_ready")
        s_empty, s_fill, s_scatter = sem("empty_row_loaded"), sem("slots_filled"), [sem("first_tokens_scattered"), sem("last_tokens_scattered")]
        mask_ready, mt_done, mt_copied = sem("mask_ready"), sem("mask_transposed"), sem("mask_t_copied")
        s_mask = sem("mask_in_lanes")
        st_done, st_copied = sem("scores_transposed"), sem("score_t_copied")
        s_sc_out, s_sc_in = sem("scores_stored"), sem("scores_spread")
        s_w1a, s_w1b, s_w2 = sem("w1a_loaded"), sem("w1b_loaded"), sem("w2_loaded")
        s_xs = [sem(f"slots_loaded{i}") for i in range(2)]
        xst_done, xst_copied = sem("slots_transposed"), sem("slots_t_copied")
        up_done, gelu_done = sem("up_done"), sem("gelu_done")
        s_meta, target_ready = sem("meta_loaded"), sem("targets_ready")
        dn_done, ys_copied = sem("down_done"), sem("expert_out_copied")
        w1_fetched = sem("w1_fetched")
        ys_ready, vc_ready = sem("expert_out_weighted"), sem("v_col_ready")
        s_ys = [sem(f"expert_out_stored{i}") for i in range(2)]
        s_vs = [sem(f"expert_v_stored{i}") for i in range(2)]
        s_ffn = [sem(f"ffn_loaded{b}") for b in range(B)]
        h_added, stores_begun = sem("ffn_added"), sem("stores_begun")
        s_scan, s_lane = sem("scan_tables_loaded"), sem("lanes_loaded")
        lm_ready, lm_shifted = sem("lane_products_ready"), sem("lane_products_shifted")
        start_done = sem("lane_starts_done")
        frac_ready, flip_done = sem("fraction_ready"), sem("backward_fraction_flipped")
        feat_ready, s_f3, f3_ones = sem("features_ready"), sem("features_spread"), sem("f3_ones")
        ft_done, out_ready = sem("feature_rows_done"), sem("output_ready")

        block = ctx.enter_context(nc.Block())
        CONV = [(wdw, "w_dw"), (vec2, "vec2"), (ident, "ident")]
        FRONT = [(wpw, "w_pw"), (dft_c, "dft_c"), (cos_n, "cos_n"), (sin_n, "sin_n")]
        ATTN = [(gamma, "gamma"), (beta, "beta"), (wq, "wq"), (wk, "wk"), (wv, "wv"),
                (tri, "tri"), (pick, "pick"), (steps, "steps"), (ones, "ones"), (epscol, "epscol")]
        MOE = [(tri_strict, "tri_strict"), (rev, "rev"), (thr, "thr"), (tidx, "tidx"), (wgm, "wgm"),
               (wvrow, "wvrow"), (bvcol, "bvcol"), (wof, "wof"), (scale3, "scale3"), (token_row, "token_row")]
        TILE_PAIRS = (SLOT_TILES - 1) // 2
        LAST_PAIR = TILE_PAIRS - 1
        assert SLOT_TILES % 2 == 1
        FIRST_SCATTERS = TT // 2 + TT // 4
        WARM_PROJECT, WARM_EXPERTS, WARM_FEATURES = 100, 32, 18
        POOL_BATCHES = B - 1

        def order(front, project, attend):
            front(0)
            project(0)
            front(1)
            attend(0)
            project(1)
            for b in range(1, B):
                if b + 1 < B:
                    front(b + 1)
                attend(b)
                if b + 1 < B:
                    project(b + 1)

        @block.sync
        def _(sp):
            def load(dst, name, s):
                sp.dma_start(dst if isinstance(dst, bass.AP) else dst[:], t[name]).then_inc(s, 16)

            def load_x(b):
                if b > 0:
                    sp.wait_ge(tap_sums_done, 1)
                    sp.wait_ge(conv_done, 2 * b)
                sp.dma_start(xin[:, :, HALO:HALO + S], t["x"][b]).then_inc(s_x, 16)

            for dst, name in CONV:
                load(dst, name, s_wc)
            load_x(0)
            for dst, name in FRONT:
                load(dst, name, s_wf)
            load_x(1)
            for dst, name in ATTN:
                load(dst, name, s_wa)
            sp.wait_ge(zeroed, 2)
            for q in range(4):
                sp.dma_start(wo[QUAD * q:QUAD * q + HD, :, :], t["wo"][q]).then_inc(s_wo, 16)

            def front(b):
                if 0 < b < B - 1:
                    load_x(b + 1)

            def project(b):
                for dram_, parts, ready, out, stack, which in (
                        (part_dram[0], q_parts, (q1_ready, q2_ready, q3_ready), s_part_out[0], q_stack, Q_PART),
                        (part_dram[1], k_parts, (k1_ready, k2_ready, k3_ready), s_part_out[1], k_stack, K_PART)):
                    for i in range(PARTS):
                        sp.wait_ge(ready[i], b + 1)
                        if b > 0 and i == 0:
                            sp.wait_ge(s_stack, 16 * 6 * b)
                        for o in range(2):
                            sp.dma_start(dram_[i, :, 6 * o:6 * o + 6, :].rearrange("d h n -> h d n"),
                                         parts[i][:, o, :]).then_inc(out, 16)
                    sp.wait_ge(out, 16 * 2 * PARTS * (b + 1))
                    if b > 0:
                        sp.wait_ge(s_done, 24 * b)
                    if which is Q_PART:
                        for i in range(PARTS):
                            m = which.count(i)
                            r = HD * which.index(i)
                            sp.dma_start(stack[r:r + HD * m, :, :],
                                         dram_[i][None, :, :, :].to_broadcast([m, HD, HEADS, N])
                                         ).then_inc(s_stack, 16)
                    else:
                        for first in range(0, len(which), PARTS):
                            m = min(PARTS, len(which) - first)
                            sp.dma_start(stack[HD * first:HD * (first + m), :, :],
                                         dram_[0:m].rearrange("i d h n -> (i d) h n")).then_inc(s_stack, 16)

            def attend(b):
                pass

            load(empty, "empty_row", s_empty)
            sp.wait_ge(s_empty, 16)
            for i in range(SLOT_TILES):
                sp.dma_start(xs_dram[P * i:P * i + P, :], empty[:]).then_inc(s_fill, 16)
            for dst, name in MOE:
                load(dst, name, s_wm)
            sp.dma_start(w1a[:], t["w1a"]).then_inc(s_w1a, 16)
            order(front, project, attend)
            sp.wait_ge(row_done, B)
            sp.wait_ge(conv_done, 2 * B)
            sp.dma_start(w2[:], t["w2"]).then_inc(s_w2, 16)
            sp.wait_ge(s_done, 24 * B)
            sp.dma_start(w1b[:], t["w1b"]).then_inc(s_w1b, 16)
            sp.wait_ge(wo_done, B)
            sp.dma_start(b2, t["b2"].to_broadcast([P, E * D])).then_inc(s_w2, 16)
            sp.wait_ge(xt_done, B)
            load(scan_tab, "scan_tab", s_scan)
            sp.wait_ge(st_copied, 1)
            sp.dma_start(sc_dram.rearrange("(t n) -> t n", n=P), score_t[:]).then_inc(s_sc_out, 16)
            sp.wait_ge(s_sc_out, 16)
            sp.wait_ge(conv_done, 2 * B)
            sp.wait_ge(pw_done, 2 * B)
            sp.dma_start(wide[:], sc_dram[None, :].to_broadcast([P, B * N])).then_inc(s_sc_in, 16)
            sp.wait_ge(s_scatter[0], 16 * FIRST_SCATTERS)
            sp.wait_ge(s_scatter[1], 16 * (TT - FIRST_SCATTERS))

            def load_slots(i, slot):
                sp.dma_start(xs[slot], xs_dram[bass.ds(i * P, P), :]).then_inc(s_xs[slot], 16)

            def load_pair(i):
                for value, slot in ((2 * i, 1), (2 * i + 1, 0)):
                    ahead(sp, xst_done, value)
                    load_slots(value + 1, slot)

            load_slots(0, 0)
            sp.dma_start(meta[:], xs_dram[:, D:ROW].rearrange("(t p) k -> p t k", p=P)).then_inc(s_meta, 16)
            load_pair(0)
            with sp.Fori(1, TILE_PAIRS) as i:
                load_pair(i)

            sp.wait_ge(mt_copied, 1)
            sp.dma_start(mask_l[:], mask_t[:]).then_inc(s_mask, 16)
            sp.wait_ge(s_vs[0], 16 * (TILE_PAIRS + 1))
            sp.wait_ge(s_vs[1], 16 * TILE_PAIRS)
            sp.dma_start(v2[0:B * CH, :], v_lanes.rearrange("b c l -> (b c) l")).then_inc(s_lane, 16)
            sp.dma_start(v_raw[B * CH:P, :], v_lanes[:, ::-1, :]).then_inc(s_lane, 16)
            sp.wait_ge(s_ys[0], 16 * (TILE_PAIRS + 1))
            sp.wait_ge(s_ys[1], 16 * TILE_PAIRS)
            sp.wait_ge(t2_done, B)
            for b in range(B):
                sp.dma_start(x2_all[:, NT * b:NT * b + NT, 0:D],
                             ffn_dram[N * b:N * b + N, :].rearrange("(n p) d -> p n d", p=P)
                             ).then_inc(s_ffn[b], 16)
            sp.wait_ge(feat_ready, 1)
            sp.wait_ge(f3_ones, 1)
            for k in range(2):
                sp.dma_start(f3[k:k + 1, :], gg[:, k, :]).then_inc(s_f3, 16)
            for b in range(B):
                sp.wait_ge(out_ready, b + 1)
                sp.dma_start(t["out"][N * b:N * b + N, :].rearrange("(n p) d -> p n d", p=P),
                             h_all[:, NT * b:NT * b + NT, :]).then_inc(s_out, 16)
            sp.wait_ge(s_out, 16 * B)

        @block.gpsimd
        def _(pool):
            nc.gpsimd.memset(idle[:], 0.0).then_inc(idle_zeroed, 1)
            nc.gpsimd.memset(xin[:, :, 0:HALO], 0.0).then_inc(pool_step, 1)
            nc.gpsimd.memset(xin[:, :, HALO + S:], 0.0).then_inc(zeroed, 1)
            nc.gpsimd.memset(wo[:], 0.0).then_inc(zeroed, 1)
            nc.gpsimd.memset(va[:], 0.0).then_inc(pool_step, 1)
            pool.wait_ge(pool_step, 2)
            nc.gpsimd.memset(va[:, :, :, HD:HD + 1], 1.0).then_inc(zeroed, 1)

            def front(b):
                pass

            def project(b):
                pass

            def attend(b):
                if b == 0:
                    pool.wait_ge(s_wa, 16 * len(ATTN))
                for n in range(24 if b < POOL_BATCHES else 0):
                    pool.wait_ge(sq_done, 24 * b + n + 1)
                    diag = prob[:, n % 4, :, 0:P]
                    nc.gpsimd.tensor_tensor(diag, diag, tri[:, None, :].to_broadcast([P, 2, P]),
                                            ALU.mult).then_inc(p_ready, 1)

            order(front, project, attend)
            pool.wait_ge(s_fill, 16 * SLOT_TILES)
            pool.wait_ge(x2_ready, B)
            pool.wait_ge(pos_ready, 1)
            for i in range(TT):
                nc.gpsimd.indirect_dma_start(xs_dram, bass.IndirectOffsetOnAxis(pos_i[:, i:i + 1], 0),
                                             x2_all[:, i, :], None).then_inc(s_scatter[i // FIRST_SCATTERS], 16)

            pool.wait_ge(mask_ready, 1)
            nc.gpsimd.memset(f3, 0.0).then_inc(pool_step, 1)
            pool.wait_ge(pool_step, 3)
            nc.gpsimd.memset(f3[0:3, :], 1.0).then_inc(f3_ones, 1)

            def store_slots(i, slot, others):
                pool.wait_ge(target_ready, i + 1)
                pool.wait_ge(vc_ready, i + 1)
                ahead(pool, s_vs[1 - slot], 16 * others)
                ahead(pool, s_ys[1 - slot], 16 * others)
                pool.sem_inc(stores_begun, 1)
                for out, src, stored in ((v_dram, v_col[slot][:], s_vs), (ffn_dram, ys[slot], s_ys)):
                    nc.gpsimd.indirect_dma_start(out, bass.IndirectOffsetOnAxis(target[slot][:], 0),
                                                 src, None).then_inc(stored[slot], 16)

            def store_pair(i):
                store_slots(2 * i, 0, i)
                store_slots(2 * i + 1, 1, i + 1)

            store_pair(0)
            with pool.Fori(1, TILE_PAIRS) as i:
                store_pair(i)
            store_slots(SLOT_TILES - 1, 0, TILE_PAIRS)
            for b in range(B):
                pool.wait_ge(s_ffn[b], 16)
                hb = h_all[:, NT * b:NT * b + NT, :]
                nc.gpsimd.tensor_tensor(hb, hb, x2_all[:, NT * b:NT * b + NT, 0:D], ALU.add
                                        ).then_inc(h_added, 1)

        @block.scalar
        def _(act):
            def front(b):
                for half in range(2):
                    act.wait_ge(col_done, 2 * b + half + 1)
                    if b > 0:
                        act.wait_ge(row_done, b)
                    nc.scalar.activation(gh[:, 2 * half:2 * half + 2, :], ring[0][:, half, :].rearrange(
                        "p (i n) -> p i n", i=2)[:, :, 0:D], ACT.Copy).then_inc(gh_copied, 1)
                act.wait_ge(row_done, b + 1)
                if b > 0:
                    act.wait_ge(xn_ready, b)
                nc.scalar.activation(y[:, :, 0:NC], ring4[1][:, :, 0:NC], ACT.Copy).then_inc(a_copied, 1)

            def attend(b):
                for n in range(24):
                    j = n // PAIRS
                    act.wait_ge(s_done, 24 * b + n + 1)
                    if n == 0 and b > 0:
                        act.wait_ge(den_spread, 3 * b)
                    if n >= 4 or b > 0:
                        act.wait_ge(av_done, 24 * b + n - 3)
                    w = N - P * j
                    nc.scalar.activation(prob[:, n % 4, :, 0:w], ring[n % 2][:, :, 0:w], ACT.Square,
                                         bias=ones[:, 0:1], scale=0.25).then_inc(sq_done, 1)

            def sums(b):
                for g in range(HG):
                    if b < POOL_BATCHES:
                        act.wait_ge(ot_done, 3 * b + g + 1)
                    else:
                        act.wait_ge(av_done, 24 * b + 24 - PAIRS + 2 * g + 2)
                    if g == 0:
                        act.wait_ge(pre_copied, b + 1)
                        if b > 0:
                            act.wait_ge(wo_done, b)
                    for i in range(NT):
                        nc.scalar.activation(oT[:, g, P * i:P * i + P], att[g][:, P * i:P * i + P],
                                             ACT.Identity,
                                             bias=pbias[:, g * NT + i:g * NT + i + 1]).then_inc(ot_copied, 1)

            def project(b):
                act.wait_ge(xt_done, b + 1)
                if b > 0:
                    act.wait_ge(v_done, b)
                nc.scalar.activation(xnT[0:DC, :, :], ring[0][0:DC, :, :], ACT.Copy).then_inc(xt_copied, 1)
                if b > 0:
                    sums(b - 1)
                for s, part, ready1, ready2, rest_ready, r, out in (
                        (q_done, q_parts, q1_ready, q2_ready, q_rest, 1, s_part_out[0]),
                        (k_done, k_parts, k1_ready, k2_ready, k_rest, 0, s_part_out[1])):
                    act.wait_ge(s, b + 1)
                    if b > 0:
                        act.wait_ge(out, 16 * 2 * PARTS * b)
                    nc.scalar.activation(part[0][:], ring[r][0:DC, :, :], ACT.Copy).then_inc(ready1, 1)
                    if r == 0:
                        act.wait_ge(v_done, b + 1)
                        if b == 0:
                            act.wait_ge(zeroed, 3)
                        else:
                            act.wait_ge(av_done, 24 * b)
                        nc.scalar.activation(va[:, :, :, 0:HD],
                                             ring4[1][:, :, 0:D].rearrange("p t (h d) -> p t h d", d=HD),
                                             ACT.Copy).then_inc(v_copied, 1)
                    act.wait_ge(rest_ready, b + 1)
                    nc.scalar.activation(part[1][:], rest, ACT.Copy).then_inc(ready2, 1)
                act.wait_ge(pre_done, b + 1)
                if b > 0:
                    act.wait_ge(ot_copied, 12 * b)
                nc.scalar.activation(pbias[:], misc[:, 0:HG * NT], ACT.Identity,
                                     bias=epscol[:, 0:1]).then_inc(pre_copied, 1)

            act.wait_ge(s_wc, 16 * len(CONV))
            act.wait_ge(tap_sums_done, 1)
            nc.scalar.activation(conv[:, 1, S // 2:], att[0][0:DC, :], ACT.Identity,
                                 bias=vec2[:, 0, 1:2]).then_inc(tap_sums_copied, 1)
            act.wait_ge(s_wa, 16 * len(ATTN))
            order(front, project, attend)
            sums(B - 1)
            act.wait_ge(t2_done, 1)
            for c in range(2):
                nc.scalar.activation(xnT[0:DC, c, :], att[c][0:DC, :], ACT.Copy).then_inc(t2_first_copied, 1)
            for b in range(1, B):
                act.wait_ge(t2_done, b + 1)
                if b >= 2:
                    act.wait_ge(lg_done, b - 1)
                nc.scalar.activation((xnT, x2T)[b % 2][0:DC, :, :], ring[b % 2][0:DC, :, :],
                                     ACT.Copy).then_inc(t2_copied, 1)
            act.wait_ge(nd_ready, 1)
            nc.scalar.activation(ex[:], ex[:], ACT.Exp).then_inc(ex_ready, 1)
            nc.scalar.activation(score[:], lg[:, :, E], ACT.Sigmoid).then_inc(sc_ready, 1)

            def copy_slots(i, slot):
                act.wait_ge(xst_done, i + 1)
                ahead(act, up_done, i - 1)
                nc.scalar.activation(xsT[slot][0:DC, :, :],
                                     att[slot][0:DC, 0:2 * P].rearrange("p (c n) -> p c n", c=2),
                                     ACT.Copy).then_inc(xst_copied, 1)

            def gelu(i, slot):
                act.wait_ge(up_done, i + 1)
                ahead(act, dn_done, i - 1)
                nc.scalar.activation(hT[slot].rearrange("p (a c) n -> p a (c n)", a=2),
                                     ring[slot][:, :, 0:HID // 2], ACT.Gelu_apprx_tanh).then_inc(gelu_done, 1)

            def pair(i, last=False):
                gelu(2 * i + 1, 1)
                copy_slots(2 * i + 2, 0)
                gelu(2 * i + 2, 0)
                if not last:
                    copy_slots(2 * i + 3, 1)

            copy_slots(0, 0)
            gelu(0, 0)
            copy_slots(1, 1)
            pair(0)
            with act.Fori(1, TILE_PAIRS - 1) as i:
                pair(i)
            pair(LAST_PAIR, last=True)

        @block.vector
        def _(dve):
            st = Steps(dve, dve_step)

            def convolve(b, halves=(0, 1)):
                dve.wait_ge(s_x, 16 * (b + 1))
                if b == 0:
                    dve.wait_ge(s_wc, 16 * len(CONV))
                if b > 0:
                    dve.wait_ge(pw_done, 2 * b)
                for half in halves:
                    at = S // 2 * half
                    chunks = 1 if b == 0 and half == 1 else 2
                    for tap in range(TAPS):
                        for c in range(chunks):
                            src = xin[:, c, at + tap:at + tap + S // 2]
                            dst = conv[:, c, at:at + S // 2]
                            w = wdw[:, c, tap:tap + 1]
                            if tap == 0:
                                ins = nc.vector.tensor_scalar(dst, src, w, vec2[:, 0, c:c + 1],
                                                              ALU.mult, ALU.add)
                            else:
                                st.settle(but=chunks - 1)
                                ins = nc.vector.scalar_tensor_tensor(dst, src, w, dst, ALU.mult, ALU.add)
                            st.mark(ins)
                    st.settle()
                    nc.vector.tensor_scalar(nz[:, 0:1], nz[:, 0:1], 1.0, None, ALU.mult).then_inc(conv_done, 1)

            def layernorm(src, dst):
                for i in range(NT):
                    st.mark(nc.vector.bn_stats(stats[:, i, :], src(i)))
                st.settle()
                for i in range(NT):
                    st.mark(nc.vector.bn_aggr(mv[:, i, :], stats[:, i, :]))
                st.settle()
                st.then(nc.vector.tensor_scalar(nx[:], mv[:, :, 1], EPS_LN, None, ALU.add))
                st.then(nc.vector.tensor_scalar(ny[:].bitcast(I32), nx[:].bitcast(I32), -0.5, MAGIC,
                                                ALU.mult, ALU.add))
                for _ in range(RSQRT_ROUNDS):
                    st.then(nc.vector.tensor_tensor(nz[:], ny[:], ny[:], ALU.mult))
                    st.then(nc.vector.scalar_tensor_tensor(nz[:], nz[:], -0.5, nx[:], ALU.mult, ALU.mult))
                    st.then(nc.vector.scalar_tensor_tensor(ny[:], nz[:], 1.5, ny[:], ALU.add, ALU.mult))
                for i in range(NT):
                    st.mark(nc.vector.tensor_scalar(dst(i), src(i), mv[:, i, 0:1], ny[:, i:i + 1],
                                                    ALU.subtract, ALU.mult))
                st.settle()

            def pool(b):
                for half in range(2):
                    dve.wait_ge(pw_done, 2 * b + half + 1)
                    if b > 0:
                        dve.wait_ge(col_done, 2 * b)
                    part = slice(N // 2 * half, N // 2 * half + N // 2)
                    for o in range(2):
                        pairs = ring[o][0:DC, half, :].rearrange("p (n two) -> p n two", two=2)
                        st.mark(nc.vector.tensor_reduce(pooled[:, o, part], pairs, AX, ALU.max))
                    for o in range(2):
                        st.settle(but=1 - o)
                        nc.vector.tensor_scalar(pooled[:, o, part], pooled[:, o, part], vec2[:, 1, o:o + 1], 0.0,
                                                ALU.add, ALU.max).then_inc(pool_done, 1)

            def untangle(b):
                dve.wait_ge(a_copied, b + 1)
                sine = ring4[1][:, :, P:P + NS]
                st.then(nc.vector.tensor_tensor(y[:, :, D - 1:NC - 1:-1], y[:, :, 1:NC - 1], sine, ALU.add))
                st.then(nc.vector.tensor_tensor(y[:, :, 1:NC - 1], y[:, :, 1:NC - 1], sine, ALU.subtract))
                nc.vector.tensor_copy(nz[:, 0:1], y[:, 0, 0:1]).then_inc(y_done, 1)

            def normalise(b):
                layernorm(lambda i: y[:, i, :], lambda i: y[:, i, :])
                if b == 0:
                    dve.wait_ge(s_wa, 16 * len(ATTN))
                else:
                    dve.wait_ge(xt_done, b)
                hb = h_all[:, NT * b:NT * b + NT, :]
                g3 = gamma[:, None, :].to_broadcast([P, NT, D])
                b3 = beta[:, None, :].to_broadcast([P, NT, D])
                st.then(nc.vector.tensor_tensor(hb, y[:], g3, ALU.mult))
                st.then(nc.vector.tensor_tensor(hb, hb, b3, ALU.add))
                layernorm(lambda i: h_all[:, NT * b + i, :], lambda i: xn[:, i, :])
                nc.vector.tensor_copy(nz[:, 0:1], xn[:, 0, 0:1]).then_inc(xn_ready, 1)

            def front(b):
                pool(b)
                if b == 0:
                    convolve(1, (0,))
                untangle(b)
                normalise(b)
                if b == 0:
                    convolve(1, (1,))
                elif b < B - 1:
                    convolve(b + 1)

            def project(b):
                for src, part, ready1, rest_ready, ready2, ready3 in (
                        (ring[1], q_parts, q1_ready, q_rest, q2_ready, q3_ready),
                        (ring[0], k_parts, k1_ready, k_rest, k2_ready, k3_ready)):
                    dve.wait_ge(ready1, b + 1)
                    nc.vector.tensor_tensor(rest, src[0:DC, :, :], part[0][:], ALU.subtract
                                            ).then_inc(rest_ready, 1)
                    dve.wait_ge(ready2, b + 1)
                    dve.wait_ge(rest_ready, b + 1)
                    nc.vector.tensor_tensor(part[2][:], rest, part[1][:], ALU.subtract).then_inc(ready3, 1)
                    dve.wait_ge(ready3, b + 1)
                if b > 0:
                    finish(b - 1)

            def attend(b):
                if b < POOL_BATCHES:
                    return
                for n in range(24):
                    dve.wait_ge(sq_done, 24 * b + n + 1)
                    diag = prob[:, n % 4, :, 0:P]
                    nc.vector.scalar_tensor_tensor(diag, diag, 1.0, tri[:, None, :].to_broadcast([P, 2, P]),
                                                   ALU.add, ALU.mult).then_inc(p_ready_dve, 1)
            def normalise_again(b):
                layernorm(lambda i: h_all[:, NT * b + i, :], lambda i: x2_all[:, NT * b + i, 0:D])
                nc.vector.tensor_copy(nz[:, 0:1], x2_all[:, NT * b, 0:1]).then_inc(x2_ready, 1)

            def finish(b):
                dve.wait_ge(den_done, b + 1)
                st.then(nc.vector.reciprocal(rden[:], misc[:, 64:64 + HG * NT * 4].rearrange("p (g h) -> p g h", h=4)))
                nc.vector.tensor_copy(rden_wide, rden[:, :, :, None].to_broadcast([P, HG * NT, 4, QUAD])
                                      ).then_inc(rden_ready, 1)
                for g in range(HG):
                    dve.wait_ge(den_spread, 3 * b + g + 1)
                    nc.vector.tensor_tensor(oT[:, g, :], oT[:, g, :], ring[g // 2][:, g % 2, :], ALU.mult
                                            ).then_inc(o_ready, 1)
                if b == B - 1:
                    normalise_again(B - 2)
                dve.wait_ge(wo_done, b + 1)
                hb = h_all[:, NT * b:NT * b + NT, :]
                st.then(nc.vector.tensor_tensor(hb, hb, ring4[0][:, :, 0:D], ALU.add))
                nc.vector.tensor_copy(nz[:, 0:1], hb[:, 0, 0:1]).then_inc(attn_added, 1)
                if b != B - 2:
                    normalise_again(b)

            st.then(nc.vector.memset(nz[:], 0.0))
            for m in (xnT, x2T, xsT[0], xsT[1]):
                nc.vector.memset(m[DC:DC + 1, :, :], 1.0).then_inc(ones_rows, 1)
            dve.wait_ge(s_wc, 16 * len(CONV))
            nc.vector.tensor_tensor(taps, ident[0:DC, None, 0:DC].to_broadcast([DC, TAPS, DC]),
                                    wdw[:, 1, :, None].to_broadcast([DC, TAPS, DC]), ALU.mult
                                    ).then_inc(taps_ready, 1)
            dve.wait_ge(zeroed, 1)
            dve.wait_ge(pool_step, 1)
            convolve(0)
            order(front, project, attend)
            finish(B - 1)

            V = nc.vector
            dve.wait_ge(s_wm, 16 * len(MOE))
            dve.wait_ge(lg_done, B)
            st.then(V.tensor_copy(lg[:], misc[:, 0:16 * TT].rearrange("p (t e) -> p t e", e=16)[:, :, 0:E + 1]))
            le = lg[:, :, 0:E]

            def over(ap):
                return ap[:, :, None].to_broadcast([P, TT, E])

            st.then(V.tensor_reduce(mx[:], le, AX, ALU.max))
            V.tensor_tensor(ex[:], le, over(mx), ALU.subtract).then_inc(nd_ready, 1)
            revb = rev[:, None, :].to_broadcast([P, TT, E])
            st.then(V.tensor_tensor(key[:], le, over(mx), ALU.is_ge))
            st.then(V.tensor_tensor(key[:], key[:], revb, ALU.mult))
            st.then(V.tensor_reduce(pos[:], key[:], AX, ALU.max))
            V.tensor_tensor(oh[:], revb, over(pos), ALU.is_equal).then_inc(oh_ready, 1)
            dve.wait_ge(ex_ready, 1)
            st.mark(V.tensor_copy(x2_all[:, :, D + 1], token_row[:]))
            st.then(V.tensor_reduce(mx[:], ex[:], AX, ALU.add))
            st.then(V.reciprocal(x2_all[:, :, D], mx[:]))
            dve.wait_ge(cnt_done, 1)
            dve.wait_ge(oh_ready, 1)
            st.then(V.tensor_copy(cnt[:], att[1][:, 0:P].rearrange("p (t e) -> p e t", e=E)))
            flat = lambda ap: ap[:].rearrange("p e t -> p (e t)")
            st.then(V.tensor_tensor_scan(flat(incl), ones[:], flat(cnt), 0.0, ALU.mult, ALU.add))
            st.then(V.tensor_tensor(excl[:], incl[:], cnt[:], ALU.subtract))
            tot, ntl, ti, tb, base = (et[:, k, :] for k in range(5))
            st.then(V.tensor_tensor(tot, incl[:, :, TT - 1], excl[:, :, 0], ALU.subtract))
            st.then(V.tensor_tensor(cnt[:], tot[:, :, None].to_broadcast([P, E, TT]),
                                    thr[:, None, :].to_broadcast([P, E, TT]), ALU.is_gt))
            st.then(V.tensor_reduce(ntl, cnt[:], AX, ALU.add))
            st.then(V.tensor_tensor_scan(ti, ones[:, 0:E], ntl, 0.0, ALU.mult, ALU.add))
            st.then(V.tensor_tensor(tb, ti, ntl, ALU.subtract))
            st.then(V.scalar_tensor_tensor(base, tb, float(P), excl[:, :, 0], ALU.mult, ALU.subtract))
            st.then(V.tensor_tensor(excl[:], excl[:], base[:, :, None].to_broadcast([P, E, TT]), ALU.add))
            pre = att[0][:, 0:P].rearrange("p (t e) -> p t e", e=E)
            st.then(V.tensor_tensor(key[:], excl[:].rearrange("p e t -> p t e"), pre, ALU.add))
            st.then(V.tensor_tensor(key[:], key[:], oh[:], ALU.mult))
            st.then(V.tensor_reduce(pos[:], key[:], AX, ALU.add))
            V.tensor_copy(pos_i[:], pos[:]).then_inc(pos_ready, 1)
            tiles = wide[0:1, 0:(SLOT_TILES + 1) * E].rearrange("p (t e) -> p t e", e=E)
            st.then(V.tensor_tensor(tiles, tidx[:, :, None].to_broadcast([1, SLOT_TILES + 1, E]),
                                    ti[0:1, None, :].to_broadcast([1, SLOT_TILES + 1, E]), ALU.is_ge))
            st.then(V.tensor_reduce(te[:], tiles, AX, ALU.add))
            V.tensor_scalar(te_i[:], te[:], float(E - 1), None, ALU.min).then_inc(te_ready, 1)
            def fetch_w1(i, slot):
                e = dve.value_load(te_i[0:1, bass.ds(i, 1)], min_val=0, max_val=E - 1)
                ahead(dve, up_done, i - 1)
                for k, w in ((0, w1a), (1, w1b)):
                    V.tensor_copy(w1_tile[slot][0:DC + k, k, :], w[0:DC + k, bass.ds(e * HID, HID)]
                                  ).then_inc(w1_fetched, 1)

            dve.wait_ge(te_ready, 1)
            dve.wait_ge(s_w1a, 16)
            dve.wait_ge(s_w1b, 16)
            dve.wait_ge(s_w2, 32)
            dve.wait_ge(s_part_out[0], 16 * 2 * PARTS * B)
            dve.wait_ge(s_part_out[1], 16 * 2 * PARTS * B)
            dve.wait_ge(st_done, 1)
            V.tensor_copy(score_t[:], misc[0:TT, 256:256 + P]).then_inc(st_copied, 1)
            fetch_w1(0, 0)
            fetch_w1(1, 1)
            st.then(V.memset(qq[:, 0:2, :, :, :], 0.0))
            st.mark(V.memset(qq[:, 1, :, 0, 0:1], 1.0))
            st.mark(V.memset(qq[:, 0, :, 0, 1:2], 1.0))
            st.mark(V.memset(neg_pos[:, 0:1], -GROUP_SCALE))
            st.mark(V.memset(neg_pos[:, 1:2], GROUP_SCALE))
            st.then(V.tensor_scalar(wof[:], wof[:], scale3[:, 0:1], None, ALU.mult))
            dve.wait_ge(s_sc_in, 16)
            for i in range(TT):
                b = i // NT
                if i > 1:
                    st.settle(but=1)
                st.mark(V.tensor_scalar((junk, junk2)[i % 2], wide[:, N * b:N * b + N], score[:, i:i + 1], None,
                                        ALU.is_gt, ALU.add, accum_out=pos[:, i:i + 1]))
            st.settle()
            V.tensor_scalar(mask[:], pos[:], float(KEEP), None, ALU.is_lt).then_inc(mask_ready, 1)
            dve.wait_ge(mt_done, 1)
            V.tensor_copy(mask_t[:], misc[0:TT, 384:384 + P]).then_inc(mt_copied, 1)

            def copy_out(i, slot, pair):
                e = dve.value_load(te_i[0:1, bass.ds(i, 1)], min_val=0, max_val=E - 1)
                ahead(dve, s_vs[slot], 16 * pair)
                ahead(dve, s_ys[slot], 16 * pair)
                dve.wait_ge(dn_done, i + 1)
                V.tensor_tensor(ys[slot], att[2][:, 0:D], b2[:, bass.ds(e * D, D)], ALU.add
                                ).then_inc(ys_copied, 1)
                dve.wait_ge(ys_copied, i + 1)
                V.tensor_scalar(ys[slot], ys[slot], meta[:, bass.ds(i, 1), 0], None, ALU.mult
                                ).then_inc(ys_ready, 1)
                V.tensor_copy(target[slot][:], meta[:, bass.ds(i, 1), 1]).then_inc(target_ready, 1)
                dve.wait_ge(ys_ready, i + 1)
                V.tensor_tensor_reduce(junk[:, 0:D], ys[slot], wvrow[:], 1.0, 0.0, ALU.mult, ALU.add,
                                       v_col[slot][:]).then_inc(vc_ready, 1)

            def copy_pair(i):
                fetch_w1(2 * i + 2, 0)
                copy_out(2 * i, 0, i)
                fetch_w1(2 * i + 3, 1)
                copy_out(2 * i + 1, 1, i)

            dve.wait_ge(s_meta, 16)
            copy_pair(0)
            with dve.Fori(1, TILE_PAIRS) as i:
                copy_pair(i)
            copy_out(SLOT_TILES - 1, 0, TILE_PAIRS)

            dve.wait_ge(s_lane, 16 * 2)
            half = B * CH
            st.mark(V.tensor_scalar(v2[0:half, :], v2[0:half, :], bvcol[0:half, 0:1], -V_MAX, ALU.add, ALU.max))
            st.then(V.tensor_scalar(v2[half:P, :], v_raw[half:P, ::-1], bvcol[half:P, 0:1], -V_MAX,
                                    ALU.add, ALU.max))
            by_group = v2[:].rearrange("p (g l) -> p g l", g=GR)
            st.mark(V.tensor_scalar(vv[:, :, :, 0], by_group, V_MAX, -1.0, ALU.min, ALU.mult))
            st.then(V.tensor_scalar(vv[:, :, :, 1], by_group, V_MAX, None, ALU.min))
            for l in range(SL):
                new, one, two = qq[:, l + 2, :, :, :], qq[:, l + 1, :, :, :], qq[:, l, :, :, :]
                st.mark(V.tensor_tensor(new, one, two, ALU.add))
                st.then(V.tensor_tensor(qv[:], one[:, :, ::-1, :],
                                        vv[:, :, l, :, None].to_broadcast([P, GR, 2, 2]), ALU.mult))
                st.then(V.tensor_tensor(new, new, qv[:], ALU.add))
            gm6 = gm[:].rearrange("p g (k c) (s d) -> p g k c s d", c=2, d=2)
            signs = neg_pos[:, None, :, None].to_broadcast([P, GR, 2, 2])
            for k in range(2):
                src = qq[:, SL + 1 - k, :, :, :]
                st.mark(V.tensor_scalar(gm6[:, :, k, :, :, 0], src, GROUP_SCALE, None, ALU.mult))
                st.mark(V.tensor_tensor(gm6[:, :, k, :, :, 1], src[:, :, ::-1, :], signs, ALU.mult))
            st.settle()

            def times(dst, later, earlier):
                st.then(V.tensor_tensor(gp[:], later[:, :, None, :].to_broadcast([P, 4, 4, 4]),
                                        earlier.rearrange("p k j -> p j k")[:, None, :, :]
                                        .to_broadcast([P, 4, 4, 4]), ALU.mult))
                return V.tensor_reduce(dst, gp[:], AX, ALU.add)

            for g in range(1, GR):
                st.then(times(gm[:, g, :, :], gm[:, g, :, :], gm[:, g - 1, :, :]))
            whole = gm[:, GR - 1, :, :]
            st.then(V.tensor_tensor_reduce(size[:, 0:2], whole[:, 0, 0:2], whole[:, 0, 0:2], 1.0, 0.0,
                                           ALU.mult, ALU.add, size[:, 2:3]))
            st.then(V.tensor_scalar(size[:, 3:4].bitcast(I32), size[:, 2:3].bitcast(I32), -0.5, MAGIC,
                                    ALU.mult, ALU.add))
            V.tensor_scalar(lm[0][:], whole, size[:, 3:4], None, ALU.mult).then_inc(lm_ready, 1)
            for i in range(LEVELS):
                dve.wait_ge(lm_ready, i + 1)
                dve.wait_ge(lm_shifted, i + 1)
                shifted = misc[:, 16 * i:16 * i + 16].rearrange("p (k j) -> p k j", j=4)
                times(lm[(i + 1) % 2][:], lm[i % 2][:], shifted).then_inc(lm_ready, 1)
            dve.wait_ge(start_done, 1)
            lane_start = misc[:, 64:68]
            st.mark(V.tensor_copy(start[:, 0, :, :].rearrange("p s c -> p (s c)"), lane_start))
            st.then(V.tensor_tensor(gp[:, 0:GR - 1, :, :], gm[:, 0:GR - 1, :, :],
                                    lane_start[:, None, None, :].to_broadcast([P, GR - 1, 4, 4]), ALU.mult))
            st.then(V.tensor_reduce(start[:, 1:GR, :, :].rearrange("p g s c -> p g (s c)"),
                                    gp[:, 0:GR - 1, :, :], AX, ALU.add))
            st.mark(V.tensor_copy(sw[:, 0, :, 0, :], start[:, :, :, 0]))
            st.mark(V.tensor_scalar(sw[:, 0, :, 1, :], start[:, :, :, 1], -1.0, None, ALU.mult))
            st.mark(V.tensor_copy(sw[:, 1, :, 0, :], start[:, :, :, 1]))
            st.then(V.tensor_copy(sw[:, 1, :, 1, :], start[:, :, :, 0]))
            basis = qq[:, 1:SL + 2, :, :, :].rearrange("p l g c s -> p l (g c s)")
            for k in range(2):
                st.mark(V.tensor_tensor(xp[:, k, :, :, :].rearrange("p l g c -> p l (g c)"), basis,
                                        sw[:, k, :, :, :].rearrange("p g c s -> p (g c s)")[:, None, :]
                                        .to_broadcast([P, SL + 1, GR * 4]), ALU.mult))
            st.settle()
            st.then(V.tensor_reduce(xx[:].rearrange("p k l g -> p (k l g)"),
                                    xp[:].rearrange("p k l g c -> p (k l g) c"), AX, ALU.add))
            new, old = xx[:, :, 1:SL + 1, :], xx[:, :, 0:SL, :]
            st.mark(V.tensor_tensor(fb[:, 0:2, :, :], new[:, ::-1, :, :], old, ALU.mult))
            st.mark(V.tensor_tensor(fb[:, 2:4, :, :], new, old, ALU.mult))
            st.then(V.tensor_tensor(fb[:, 4:6, :, :], old, old, ALU.mult))
            st.mark(V.tensor_tensor(fb[:, 4, :, :], fb[:, 4, :, :], fb[:, 5, :, :], ALU.add))
            st.mark(V.tensor_tensor(fb[:, 0, :, :], fb[:, 0, :, :], fb[:, 1, :, :], ALU.subtract))
            st.then(V.tensor_tensor(fb[:, 2, :, :], fb[:, 2, :, :], fb[:, 3, :, :], ALU.add))
            st.then(V.reciprocal(fb[:, 5, :, :], fb[:, 4, :, :]))
            st.mark(V.tensor_tensor(fa[:, 0, :, :], fb[:, 0, :, :], fb[:, 5, :, :], ALU.mult))
            V.scalar_tensor_tensor(fa[:, 1, :, :], fb[:, 2, :, :], -1.0, fb[:, 5, :, :], ALU.mult, ALU.mult
                                   ).then_inc(frac_ready, 1)
            dve.wait_ge(flip_done, 1)
            dve.wait_ge(s_mask, 16)
            flipped = misc[0:half, P:P + 2 * LCH].rearrange("p (k l g) -> p k l g", k=2, g=GR)
            cc = fb[0:half, 0:2, :, :]
            st.then(V.tensor_tensor(cc, fa[0:half, :, :, :], flipped[:, :, ::-1, ::-1], ALU.add))
            by_step = lambda ap: ap.rearrange("p g l -> p l g")
            st.mark(V.tensor_tensor(cc[:, 0, :, :], cc[:, 0, :, :], by_step(vv[0:half, :, :, 1]), ALU.subtract))
            st.then(V.tensor_scalar(cc[:, 1, :, :], cc[:, 1, :, :], 1.0, None, ALU.add))
            sq = fb[0:half, 2:4, :, :]
            den, rec = fb[0:half, 4, :, :], fb[0:half, 5, :, :]
            st.then(V.tensor_tensor(sq, cc, cc, ALU.mult))
            st.then(V.tensor_tensor(den, sq[:, 0, :, :], sq[:, 1, :, :], ALU.add))
            st.then(V.reciprocal(rec, den))
            gg4 = gg[:].rearrange("p k (g l) -> p k g l", g=GR)
            st.mark(V.tensor_tensor(gg4[:, 0, :, :], cc[:, 0, :, :].rearrange("p l g -> p g l"),
                                    rec.rearrange("p l g -> p g l"), ALU.mult))
            st.then(V.scalar_tensor_tensor(gg4[:, 1, :, :], cc[:, 1, :, :].rearrange("p l g -> p g l"), -1.0,
                                           rec.rearrange("p l g -> p g l"), ALU.mult, ALU.mult))
            st.then(V.tensor_tensor(gg[:], gg[:], mask_l[:, None, :].to_broadcast([half, 2, LCH]), ALU.mult))
            V.tensor_scalar(gg[:], gg[:], CLAMP, -CLAMP, ALU.min, ALU.max).then_inc(feat_ready, 1)
            for b in range(B):
                dve.wait_ge(ft_done, b + 1)
                dve.wait_ge(h_added, b + 1)
                hb = h_all[:, NT * b:NT * b + NT, :]
                V.tensor_tensor(hb, hb, ring4[b % 2][:, :, 0:D], ALU.add).then_inc(out_ready, 1)

        @block.tensor
        def _(pe):
            def keep_clock(n, bank=att[2]):
                for _ in range(n):
                    nc.tensor.matmul(bank[:, 0:2 * P], idle[:, 0:P], idle[:], start=True, stop=True)

            def pointwise(b):
                if b > 0:
                    pe.wait_ge(gh_copied, 2 * b)
                    pe.wait_ge(y_done, b)
                if b == 1:
                    pe.wait_ge(k_rest, 1)
                    pe.wait_ge(v_copied, 1)
                if b > 1:
                    keep_clock(12)
                    pe.wait_ge(attn_added, b - 1)
                for half in range(2):
                    if b == 0 and half == 1:
                        pe.wait_ge(tap_sums_copied, 1)
                    pe.wait_ge(conv_done, 2 * b + half + 1)
                    for o in range(2):
                        for c in range(2):
                            last = nc.tensor.matmul(ring[o][0:DC, half, :], wpw[:, c, DC * o:DC * o + DC],
                                                    conv[:, c, 512 * half:512 * half + 512],
                                                    start=(c == 0), stop=(c == 1))
                    last.then_inc(pw_done, 1)

            def transform(b):
                for half in range(2):
                    pe.wait_ge(pool_done, 4 * b + 2 * half + 2)
                    for i in (2 * half, 2 * half + 1):
                        for c in range(2):
                            last = nc.tensor.matmul(ring4[0][:, i, 0:D], pooled[:, c, P * i:P * i + P],
                                                    dft_c[:, c, :], start=(c == 0), stop=(c == 1))
                    last.then_inc(col_done, 1)
                pe.wait_ge(gh_copied, 2 * b + 2)
                for k in range(NT):
                    for table, dst, src in ((cos_n, slice(0, NC), slice(0, NC)),
                                            (sin_n, slice(P, P + NS), slice(NC, D))):
                        for i in range(NT):
                            last = nc.tensor.matmul(ring4[1][:, k, dst], table[:, i, P * k:P * k + P],
                                                    gh[:, i, src], start=(i == 0), stop=(i == NT - 1))
                last.then_inc(row_done, 1)

            def project(b):
                pe.wait_ge(xn_ready, b + 1)
                if b > 0:
                    pe.wait_ge(sq_done, 24 * b)
                for c in range(2):
                    for i in range(NT):
                        last = nc.tensor.transpose(ring[0][0:DC, c, P * i:P * i + P],
                                                   xn[:, i, DC * c:DC * c + DC], ident[:])
                last.then_inc(xt_done, 1)
                keep_clock(10, misc)
                pe.wait_ge(xt_copied, b + 1)
                for r, w, s in ((1, wq, q_done), (0, wk, k_done)):
                    for o in range(2):
                        for c in range(2):
                            last = nc.tensor.matmul(ring[r][0:DC, o, :], w[:, c, DC * o:DC * o + DC],
                                                    xnT[0:DC, c, :], start=(c == 0), stop=(c == 1))
                    last.then_inc(s, 1)
                pe.wait_ge(q_rest, b + 1)
                for i in range(NT):
                    for c in range(2):
                        last = nc.tensor.matmul(ring4[1][:, i, 0:D], xnT[0:DC, c, P * i:P * i + P],
                                                wv[:, c, :], start=(c == 0), stop=(c == 1))
                last.then_inc(v_done, 1)
                keep_clock(8, misc)
                pe.wait_ge(v_copied, b + 1)
                for g in range(HG):
                    for j in range(NT - 1):
                        last = nc.tensor.matmul(misc[:, NT * g:NT * g + NT],
                                                va[:, j, 4 * g:4 * g + 4, :].rearrange("p h d -> p (h d)"),
                                                steps[:, j, :], start=(j == 0), stop=(j == NT - 2))
                last.then_inc(pre_done, 1)

            def attend(b):
                keep_clock(16)
                pe.wait_ge(s_stack, 16 * 6 * (b + 1))
                pe.wait_ge(pre_copied, b + 1)
                if b < B - 1:
                    pe.wait_ge(y_done, b + 2)
                else:
                    pe.wait_ge(attn_added, B - 1)
                if b > 0:
                    pe.wait_ge(ot_copied, 12 * b)

                def scores(n):
                    j, pr = divmod(n, PAIRS)
                    if n >= 2:
                        pe.wait_ge(sq_done, 24 * b + n - 1)
                    for h in (2 * pr, 2 * pr + 1):
                        last = nc.tensor.matmul(ring[n % 2][:, h % 2, 0:N - P * j],
                                                k_stack[:, h, P * j:P * j + P], q_stack[:, h, P * j:N],
                                                start=True, stop=True)
                    last.then_inc(s_done, 1)

                def values(n):
                    j, pr = divmod(n, PAIRS)
                    g = pr // 2
                    by_pool = b < POOL_BATCHES
                    for m in (n, n + 1):
                        if by_pool:
                            pe.wait_ge(p_ready, 24 * b + m + 1)
                        else:
                            pe.wait_ge(p_ready_dve, 24 * (b - POOL_BATCHES) + m + 1)
                        for h in range(2):
                            q = 2 * (m - n) + h
                            last = nc.tensor.matmul(att[g][QUAD * q:QUAD * q + QUAD, P * j:N],
                                                    va[:, j, 4 * g + q, :], prob[:, m % 4, h, 0:N - P * j],
                                                    start=(j == 0), stop=(j == NT - 1 and not by_pool))
                        last.then_inc(av_done, 1)
                    if by_pool:
                        last = nc.tensor.matmul(att[g][:, P * j:P * j + P],
                                                va[:, j, 4 * g:4 * g + 4, :].rearrange("p h d -> p (h d)"),
                                                tri[:], start=False, stop=(j == NT - 1))
                    if by_pool and j == NT - 1:
                        last.then_inc(ot_done, 1)

                for n in range(24):
                    scores(n)
                    if n % 2 and n >= 3:
                        values(n - 3)
                values(22)

            def turn(b):
                pe.wait_ge(x2_ready, b + 1)
                if b == 1:
                    pe.wait_ge(attn_added, B)
                if b >= 3:
                    pe.wait_ge(t2_copied, b - 2)
                for c in range(2):
                    dst = att[c][0:DC, :] if b == 0 else ring[b % 2][0:DC, c, :]
                    for i in range(NT):
                        last = nc.tensor.transpose(dst[:, P * i:P * i + P],
                                                   x2_all[:, NT * b + i, DC * c:DC * c + DC], ident[:])
                last.then_inc(t2_done, 1)

            def logits(b):
                for i in range(NT):
                    at = 16 * (NT * b + i)
                    for c in range(2):
                        last = nc.tensor.matmul(misc[:, at:at + E + 1],
                                                (xnT, x2T)[b % 2][0:DC + c, c, P * i:P * i + P],
                                                wgm[0:DC + c, c, :], start=(c == 0), stop=(c == 1))
                last.then_inc(lg_done, 1)

            def finish(b):
                for g in range(HG):
                    if g == 0:
                        pe.wait_ge(pre_copied, min(b + 2, B))
                    else:
                        keep_clock(5, att[g - 1])
                    pe.wait_ge(ot_copied, 12 * b + NT * (g + 1))
                    for i in range(NT):
                        at = 64 + 4 * (NT * g + i)
                        last = nc.tensor.matmul(misc[:, at:at + 4], oT[:, g, P * i:P * i + P], pick[:],
                                                start=True, stop=True)
                last.then_inc(den_done, 1)
                if b < B - 1:
                    keep_clock(8)
                else:
                    turn(0)
                pe.wait_ge(rden_ready, b + 1)
                if b + 1 < B:
                    pe.wait_ge(k_rest, b + 2)
                    pe.wait_ge(v_copied, b + 2)
                else:
                    pe.wait_ge(sq_done, 24 * B)
                for g in range(HG):
                    for i in range(NT):
                        last = nc.tensor.transpose(ring[g // 2][:, g % 2, P * i:P * i + P],
                                                   rden_wide[:, NT * g + i, :, :].rearrange("p h c -> p (h c)"),
                                                   ident[:])
                    last.then_inc(den_spread, 1)
                if b < B - 1:
                    keep_clock(8)
                else:
                    pe.wait_ge(s_wm, 16 * len(MOE))
                    pe.wait_ge(ones_rows, 4)
                    pe.wait_ge(t2_first_copied, 2)
                    logits(0)
                pe.wait_ge(o_ready, 3 * b + 3)
                for i in range(NT):
                    for g in range(HG):
                        last = nc.tensor.matmul(ring4[0][:, i, 0:D], oT[:, g, P * i:P * i + P], wo[:, g, :],
                                                start=(g == 0), stop=(g == HG - 1))
                last.then_inc(wo_done, 1)

            pe.wait_ge(idle_zeroed, 1)
            pe.wait_ge(s_x, 16)
            pe.wait_ge(zeroed, 1)
            pe.wait_ge(taps_ready, 1)
            for tap in range(TAPS):
                last = nc.tensor.matmul(att[0][0:DC, :], taps[:, tap, :],
                                        xin[:, 1, S // 2 + tap:S + tap], start=(tap == 0), stop=(tap == TAPS - 1))
            last.then_inc(tap_sums_done, 1)
            pe.wait_ge(s_wf, 16 * len(FRONT))
            pointwise(0)
            transform(0)
            pe.wait_ge(y_done, 1)
            keep_clock(WARM_PROJECT)
            pe.wait_ge(s_wa, 16 * len(ATTN))
            pe.wait_ge(s_wo, 16 * 4)
            project(0)
            pointwise(1)
            transform(1)
            attend(0)
            project(1)
            finish(0)
            for b in range(1, B):
                if b + 1 < B:
                    pointwise(b + 1)
                    transform(b + 1)
                attend(b)
                if b + 1 < B:
                    project(b + 1)
                finish(b)

            keep_clock(12)
            turn(1)
            turn(2)
            for b in range(1, B):
                if b == B - 1:
                    turn(b)
                    keep_clock(8)
                pe.wait_ge(t2_copied, b)
                logits(b)
            pe.wait_ge(oh_ready, 1)
            ohf = oh[:].rearrange("p t e -> p (t e)")
            nc.tensor.matmul(att[0][:, 0:P], tri_strict[:], ohf, start=True, stop=True)
            nc.tensor.matmul(att[1][:, 0:P], ones[:], ohf, start=True, stop=True).then_inc(cnt_done, 1)
            pe.wait_ge(sc_ready, 1)
            nc.tensor.transpose(misc[0:TT, 256:256 + P], score[:], ident[:]).then_inc(st_done, 1)
            def turn_slots(i, slot, loads):
                pe.wait_ge(s_xs[slot], 16 * loads)
                ahead(pe, xst_copied, i - 1)
                for c in range(2):
                    last = nc.tensor.transpose(att[slot][0:DC, P * c:P * c + P], xs[slot][:, DC * c:DC * c + DC],
                                               ident[:])
                last.then_inc(xst_done, 1)

            def up(i, slot):
                pe.wait_ge(w1_fetched, 2 * i + 2)
                pe.wait_ge(xst_copied, i + 1)
                ahead(pe, gelu_done, i - 1)
                for c in range(HC):
                    for k in range(2):
                        last = nc.tensor.matmul(ring[slot][:, c // 3, P * (c % 3):P * (c % 3) + P],
                                                w1_tile[slot][0:DC + k, k, P * c:P * c + P],
                                                xsT[slot][0:DC + k, k, :], start=(k == 0), stop=(k == 1))
                last.then_inc(up_done, 1)

            def down(i, slot):
                e = pe.value_load(te_i[0:1, bass.ds(i, 1)], min_val=0, max_val=E - 1)
                pe.wait_ge(gelu_done, i + 1)
                ahead(pe, ys_copied, i)
                for c in range(HC):
                    last = nc.tensor.matmul(att[2][:, 0:D], hT[slot][:, c, :],
                                            w2[:, bass.ds((e * HC + c) * D, D)],
                                            start=(c == 0), stop=(c == HC - 1))
                last.then_inc(dn_done, 1)

            pe.wait_ge(te_ready, 1)
            pe.wait_ge(st_copied, 1)
            pe.wait_ge(s_w2, 32)

            def expert_pair(i, last=False):
                up(2 * i + 1, 1)
                turn_slots(2 * i + 2, 0, i + 2)
                down(2 * i, 0)
                up(2 * i + 2, 0)
                if not last:
                    turn_slots(2 * i + 3, 1, i + 2)
                down(2 * i + 1, 1)

            pe.wait_ge(s_scatter[0], 16 * FIRST_SCATTERS)
            keep_clock(WARM_EXPERTS)
            turn_slots(0, 0, 1)
            up(0, 0)
            turn_slots(1, 1, 1)
            pe.wait_ge(mask_ready, 1)
            nc.tensor.transpose(misc[0:TT, 384:384 + P], mask[:], ident[:]).then_inc(mt_done, 1)
            expert_pair(0)
            with pe.Fori(1, TILE_PAIRS - 1) as i:
                expert_pair(i)
            expert_pair(LAST_PAIR, last=True)
            down(SLOT_TILES - 1, 0)

            pe.wait_ge(ys_copied, SLOT_TILES)
            pe.wait_ge(s_scan, 16)
            for i in range(LEVELS):
                pe.wait_ge(lm_ready, i + 1)
                at = misc[:, 16 * i:16 * i + 16]
                nc.tensor.matmul(at, shift[i], lm[i % 2][:].rearrange("p i j -> p (i j)"), start=True, stop=False)
                nc.tensor.matmul(at, ident[:], unit[i], start=False, stop=True).then_inc(lm_shifted, 1)
            pe.wait_ge(lm_ready, LEVELS + 1)
            nc.tensor.matmul(misc[:, 64:68], shift[0], lm[LEVELS % 2][:, :, 0], start=True, stop=False)
            nc.tensor.matmul(misc[:, 64:68], ident[:], unit[0][:, 0:16:4], start=False, stop=True
                             ).then_inc(start_done, 1)
            keep_clock(WARM_FEATURES)
            pe.wait_ge(frac_ready, 1)
            nc.tensor.matmul(misc[0:B * CH, P:P + 2 * LCH], flip, fa[:].rearrange("p k l g -> p (k l g)"),
                             start=True, stop=True).then_inc(flip_done, 1)
            keep_clock(WARM_FEATURES)
            pe.wait_ge(feat_ready, 1)
            keep_clock(WARM_FEATURES)
            pe.wait_ge(s_f3, 32)
            for b in range(B):
                if b >= 2:
                    pe.wait_ge(out_ready, b - 1)
                for i in range(NT):
                    last = nc.tensor.matmul(ring4[b % 2][:, i, 0:D],
                                            f3[:, N * b + P * i:N * b + P * i + P], wof[:],
                                            start=True, stop=True)
                last.then_inc(ft_done, 1)


def layouts(inp, np):
    a = {k: np.asarray(v) for k, v in inp.items()}

    def chunked(w):
        return np.ascontiguousarray(w.reshape(2, DC, -1).transpose(1, 0, 2))

    o = {}
    o["x"] = np.ascontiguousarray(a["x"].reshape(B, S, 2, DC).transpose(0, 3, 2, 1))
    o["w_dw"] = chunked(a["L0_tok_w_dw"][:, 0, :])
    o["vec2"] = np.ascontiguousarray(np.stack([a["L0_tok_b_dw"].reshape(2, DC).T, a["L0_tok_b_pw"].reshape(2, DC).T], 1))
    o["w_pw"] = chunked(a["L0_tok_w_pw"][:, :, 0].T)
    o["gamma"] = np.ascontiguousarray(np.broadcast_to(a["L0_tok_gamma"], (P, D)))
    o["beta"] = np.ascontiguousarray(np.broadcast_to(a["L0_tok_beta"], (P, D)))
    o["wq"] = chunked(a["L0_attn_Wq"].T)
    o["wk"] = chunked(a["L0_attn_Wk"].T)
    o["wv"] = chunked(a["L0_attn_Wv"].T)
    o["wo"] = np.ascontiguousarray(a["L0_attn_Wo"].T.reshape(HG, 4, HD, D).transpose(1, 2, 0, 3))
    f = np.float32
    n = np.arange(N)
    ang = 2 * np.pi * ((n[:, None] * n[None, :]) % N) / N
    o["cos_n"] = np.ascontiguousarray(np.cos(ang).astype(f).reshape(NT, P, N).transpose(1, 0, 2))
    o["sin_n"] = np.ascontiguousarray(np.sin(ang).astype(f).reshape(NT, P, N).transpose(1, 0, 2))
    d = np.arange(D)
    ang = 2 * np.pi * ((d[:, None] * d[None, :]) % D) / D
    o["dft_c"] = chunked(np.concatenate([np.cos(ang[:, :NC]), np.sin(ang[:, 1:NC - 1])], 1).astype(f))
    p = np.arange(P)
    o["ident"] = np.eye(P, dtype=f)
    o["tri"] = (p[:, None] <= p[None, :]).astype(f)
    o["tri_strict"] = (p[:, None] < p[None, :]).astype(f)
    o["pick"] = (p[:, None] == np.arange(4)[None, :] * QUAD + HD).astype(f)
    o["steps"] = np.broadcast_to((np.arange(NT)[None, :] > np.arange(NT - 1)[:, None]).astype(f), (P, NT - 1, NT)).copy()
    o["ones"] = np.ones((P, P), f)
    o["epscol"] = np.where(p % QUAD == HD, f(EPS_ATTN), f(0)).astype(f)[:, None]
    o["rev"] = np.broadcast_to(np.arange(E, 0, -1).astype(f), (P, E)).copy()
    o["thr"] = np.broadcast_to((P * np.arange(TT)).astype(f), (P, TT)).copy()
    o["tidx"] = np.arange(SLOT_TILES + 1).astype(f)[None, :]
    o["empty_row"] = np.zeros((P, ROW), f)
    o["empty_row"][:, D + 1] = B * N + p
    o["token_row"] = (P * np.arange(TT)[None, :] + p[:, None]).astype(f)
    shifts = [((p[:, None] + 2 ** i == p[None, :]) & (p[None, :] % CH >= 2 ** i)).astype(f) for i in range(LEVELS)]
    units = [np.where(p[:, None] % CH < 2 ** i, np.eye(4).reshape(1, 16), 0).astype(f) for i in range(LEVELS)]
    m = np.arange(B * CH)
    turned = B * CH + m // CH * CH + CH - 1 - m % CH
    o["scan_tab"] = np.concatenate(shifts + units + [(p[:, None] == turned[None, :]).astype(f)], 1)
    wgm = np.zeros((DC + 1, 2, E + 1), f)
    wgm[:DC, :, :E] = chunked(a["L0_ffn_Wg"])
    wgm[:DC, :, E] = a["L0_ffn_Wm"].reshape(2, DC).T
    wgm[DC, 1, :E] = a["L0_ffn_bg"]
    wgm[DC, 1, E] = a["L0_ffn_bm"]
    o["wgm"] = wgm
    w1 = a["L0_ffn_W1"].reshape(E, 2, DC, HID).transpose(1, 2, 0, 3).reshape(2, DC, E * HID)
    o["w1a"] = np.ascontiguousarray(w1[0])
    o["w1b"] = np.concatenate([w1[1], a["L0_ffn_b1"].reshape(1, E * HID)], 0)
    o["w2"] = np.ascontiguousarray(a["L0_ffn_W2"].reshape(E, HC, P, D).transpose(2, 0, 1, 3).reshape(P, -1))
    o["b2"] = np.ascontiguousarray(a["L0_ffn_b2"].reshape(1, -1))
    o["wvrow"] = np.ascontiguousarray(np.broadcast_to(a["L0_ffn_Wv"], (P, D)))
    o["bvcol"] = np.ascontiguousarray(np.broadcast_to(a["L0_ffn_bv"], (P, 1)))
    o["wof"] = np.concatenate([a["L0_ffn_Wo"], a["L0_ffn_bo"][None, :], np.zeros((DC - 3, D), f)], 0)
    o["scale3"] = np.ascontiguousarray(np.broadcast_to(a["L0_ffn_bk_scale"], (DC, 1)))
    return o


def kernel(**inputs):
    import numpy as np
    import concourse.bacc as bacc
    from concourse.bass_utils import run_bass_kernel_spmd as run

    nc = bacc.Bacc("TRN2", target_bir_lowering=False, num_devices=1)
    arrays, t = {}, {}
    for name, a in layouts(inputs, np).items():
        arrays[f"in_{name}"] = a
        t[name] = nc.dram_tensor(f"in_{name}", a.shape, mybir.dt.from_np(a.dtype), kind="ExternalInput").ap()
    t["out"] = nc.dram_tensor("out_0", (B * N, D), F32, kind="ExternalOutput").ap()
    build(nc, t)
    r = run(nc, [arrays], core_ids=[0])
    return r.results[0]["out_0"].reshape(B, N, D)
```
